# Optimizing a Trainium2 kernel written in Bass

```python
import numpy as np
import jax
import jax.numpy as jnp

def _softmax(x, axis=-1):
    return jax.nn.softmax(x, axis=axis)

def _gelu(x):
    return jax.nn.gelu(x, approximate=True)

def _silu(x):
    return jax.nn.silu(x)

def _sigmoid(x):
    return jax.nn.sigmoid(x)

def _layernorm(x, axis=-1, eps=1e-05):
    m = jnp.mean(x, axis=axis, keepdims=True)
    v = jnp.var(x, axis=axis, keepdims=True)
    return (x - m) / jnp.sqrt(v + eps)

def _scatter_add(tgt, idx, src, axis=0):
    return tgt.at[idx].add(src)

def _segment_sum(src, seg, n):
    return jax.ops.segment_sum(src, seg, n)
kernel_name = 'mk_lm_tower_d2_tok_ids1024_r4_108c51'

def setup_inputs(seed: int=0):
    np.random.seed(seed)
    _w = jnp.asarray

    def _rec_inputs():
        import jax
        import jax.numpy as jnp
        _rk = jax.random.key(seed)
        x = jax.random.randint(jax.random.fold_in(_rk, 1), (16, 512), 0, 12564, jnp.int32)
        return x
    x = _rec_inputs()

    def _L0_tok_setup():
        import jax, jax.numpy as jnp
        import numpy as np
        BASE = 10000.0

        def _rope_tables(seq_len, embed_dim, dtype):
            inv = 1.0 / BASE ** (jnp.arange(0, embed_dim, 2, dtype=jnp.float32) / embed_dim)
            freqs = jnp.arange(seq_len, dtype=jnp.float32)[:, None] * inv[None, :]
            return (jnp.cos(freqs).astype(dtype), jnp.sin(freqs).astype(dtype))
        key = jax.random.key(seed)
        k1, k2 = jax.random.split(key)
        token_ids = jax.random.randint(k1, (8, 512), 0, 50257, dtype=jnp.int32)
        emb_weight = jax.random.normal(k2, (50257, 256), dtype=jnp.float32)
        return {'token_ids': token_ids, 'emb_weight': emb_weight}
    _L0_tok_all = _L0_tok_setup()
    _L0_tok_in = {k: v for k, v in _L0_tok_all.items() if k in ('emb_weight',)}
    del _L0_tok_all

    def _L0_attn_setup():
        import jax, jax.numpy as jnp
        import numpy as np
        LN_EPS = 1e-05

        def _layernorm(x, g, b):
            mu = jnp.mean(x, axis=-1, keepdims=True)
            var = jnp.var(x, axis=-1, keepdims=True)
            return (x - mu) * jax.lax.rsqrt(var + LN_EPS) * g + b
        key = jax.random.key(seed)
        B, S, D, H = (2, 512, 256, 16)
        dh = D // H
        r = 48
        r_out = 192
        I = 4 * D
        r_mlp = 128
        ks = jax.random.split(key, 24)
        sc = lambda *sh: 0.02
        inp = {'hidden_states': jax.random.normal(ks[0], (B, S, D), jnp.float32), 'ln1_g': jnp.ones((D,), jnp.float32), 'ln1_b': jnp.zeros((D,), jnp.float32), 'ln2_g': jnp.ones((D,), jnp.float32), 'ln2_b': jnp.zeros((D,), jnp.float32), 'q_U': jax.random.normal(ks[1], (D, H, r), jnp.float32) * 0.02, 'q_V': jax.random.normal(ks[2], (H, r, dh), jnp.float32) * 0.02, 'q_b': jax.random.normal(ks[3], (H, dh), jnp.float32) * 0.02, 'k_U': jax.random.normal(ks[4], (D, H, r), jnp.float32) * 0.02, 'k_V': jax.random.normal(ks[5], (H, r, dh), jnp.float32) * 0.02, 'k_b': jax.random.normal(ks[6], (H, dh), jnp.float32) * 0.02, 'v_U': jax.random.normal(ks[7], (D, H, r), jnp.float32) * 0.02, 'v_V': jax.random.normal(ks[8], (H, r, dh), jnp.float32) * 0.02, 'v_b': jax.random.normal(ks[9], (H, dh), jnp.float32) * 0.02, 'out_U': jax.random.normal(ks[10], (D, r_out), jnp.float32) * 0.02, 'out_V': jax.random.normal(ks[11], (r_out, D), jnp.float32) * 0.02, 'out_b': jnp.zeros((D,), jnp.float32), 'fc1_U': jax.random.normal(ks[12], (D, r_mlp), jnp.float32) * 0.02, 'fc1_V': jax.random.normal(ks[13], (r_mlp, I), jnp.float32) * 0.02, 'fc1_b': jnp.zeros((I,), jnp.float32), 'fc2_U': jax.random.normal(ks[14], (I, r_mlp), jnp.float32) * 0.02, 'fc2_V': jax.random.normal(ks[15], (r_mlp, D), jnp.float32) * 0.02, 'fc2_b': jnp.zeros((D,), jnp.float32)}
        return inp
    _L0_attn_all = _L0_attn_setup()
    _L0_attn_in = {k: v for k, v in _L0_attn_all.items() if k in ('ln1_g', 'ln1_b', 'ln2_g', 'ln2_b', 'q_U', 'q_V', 'q_b', 'k_U', 'k_V', 'k_b', 'v_U', 'v_V', 'v_b', 'out_U', 'out_V', 'out_b', 'fc1_U', 'fc1_V', 'fc1_b', 'fc2_U', 'fc2_V', 'fc2_b')}
    del _L0_attn_all

    def _L0_ffn_setup():
        import jax, jax.numpy as jnp
        import numpy as np
        EPS = 1e-08

        def _ternary_linear(x, w):
            alpha = jnp.mean(jnp.abs(w))
            w_t = jnp.sign(w) * (jnp.abs(w) > 0.5 * alpha).astype(w.dtype)
            w_q = w + jax.lax.stop_gradient(w_t - w)
            d = x.shape[-1]
            rms = jnp.sqrt(jnp.sum(x * x, axis=-1, keepdims=True)) / jnp.sqrt(jnp.asarray(d, x.dtype))
            x_norm = x / (rms + EPS)
            return jnp.einsum('bsd,fd->bsf', x_norm, w_q)
        key = jax.random.key(seed)
        k1, k2, k3 = jax.random.split(key, 3)
        d_model, d_ff = (256, 1024)
        B, S = (4, 1024)
        x = jax.random.normal(k1, (B, S, d_model), dtype=jnp.float32)
        w_up = jax.random.normal(k2, (d_ff, d_model), dtype=jnp.float32) * 0.02
        w_down = jax.random.normal(k3, (d_model, d_ff), dtype=jnp.float32) * 0.02
        return {'x': x, 'w_up': w_up, 'w_down': w_down}
    _L0_ffn_all = _L0_ffn_setup()
    _L0_ffn_in = {k: v for k, v in _L0_ffn_all.items() if k in ('w_up', 'w_down')}
    del _L0_ffn_all

    def _L1_attn_setup():
        import jax, jax.numpy as jnp
        import numpy as np
        D_MODEL = 256
        EXPAND = 2
        D_INNER = EXPAND * D_MODEL
        HEADDIM = 64
        NHEADS = D_INNER // HEADDIM
        D_STATE = 64
        D_CONV = 4
        BATCH = 2
        SEQ_LEN = 256
        LN_EPS = 1e-05

        def _layernorm(x, w, b):
            mu = jnp.mean(x, axis=-1, keepdims=True)
            var = jnp.var(x, axis=-1, keepdims=True)
            return (x - mu) * jax.lax.rsqrt(var + LN_EPS) * w + b

        def _forward(hidden_states, in_proj_w, conv_w, conv_b, A_log, dt_w, dt_b, B_w, C_w, D, ln_w, ln_b, out_proj_w):
            B_, L, _ = hidden_states.shape
            xz = hidden_states @ in_proj_w.T
            x, z = jnp.split(xz, 2, axis=-1)
            x_ncl = jnp.transpose(x, (0, 2, 1))
            x_conv = jax.lax.conv_general_dilated(x_ncl, conv_w, window_strides=(1,), padding=[(D_CONV - 1, 0)], dimension_numbers=('NCH', 'OIH', 'NCH'), feature_group_count=D_INNER)
            x_conv = x_conv + conv_b[None, :, None]
            x = jnp.transpose(x_conv, (0, 2, 1))
            x = jax.nn.silu(x)
            dt = jax.nn.softplus(x @ dt_w.T + dt_b)
            Bm = (x @ B_w.T).reshape(B_, L, NHEADS, D_STATE)
            Cm = (x @ C_w.T).reshape(B_, L, NHEADS, D_STATE)
            xh = x.reshape(B_, L, NHEADS, HEADDIM)
            A = -jnp.exp(A_log)
            h0 = jnp.zeros((B_, NHEADS, HEADDIM, D_STATE), x.dtype)

            def step(h, inp):
                x_t, dt_t, B_t, C_t = inp
                A_bar = jnp.exp(A[None, :] * dt_t)[..., None, None]
                h = A_bar * h + dt_t[..., None, None] * B_t[:, :, None, :] * x_t[..., None]
                y_t = jnp.einsum('bhpn,bhn->bhp', h, C_t) + D[None, :, None] * x_t
                return (h, y_t)
            xs = (jnp.transpose(xh, (1, 0, 2, 3)), jnp.transpose(dt, (1, 0, 2)), jnp.transpose(Bm, (1, 0, 2, 3)), jnp.transpose(Cm, (1, 0, 2, 3)))
            h_final, y = jax.lax.scan(step, h0, xs)
            y = jnp.transpose(y, (1, 0, 2, 3)).reshape(B_, L, D_INNER)
            y = _layernorm(y, ln_w, ln_b)
            y = y * jax.nn.silu(z)
            output = y @ out_proj_w.T
            return (output, h_final)

        def _reference_tuple_inner(hidden_states, in_proj_w, conv_w, conv_b, A_log, dt_w, dt_b, B_w, C_w, D, ln_w, ln_b, out_proj_w):
            return _forward(hidden_states, in_proj_w, conv_w, conv_b, A_log, dt_w, dt_b, B_w, C_w, D, ln_w, ln_b, out_proj_w)
        key = jax.random.key(seed)
        ks = jax.random.split(key, 12)
        s = 0.02
        return {'hidden_states': jax.random.normal(ks[0], (BATCH, SEQ_LEN, D_MODEL), jnp.float32), 'in_proj_w': jax.random.normal(ks[1], (2 * D_INNER, D_MODEL), jnp.float32) * s, 'conv_w': jax.random.normal(ks[2], (D_INNER, 1, D_CONV), jnp.float32) * 0.1, 'conv_b': jax.random.normal(ks[3], (D_INNER,), jnp.float32) * 0.01, 'A_log': jnp.zeros((NHEADS,), jnp.float32), 'dt_w': jax.random.normal(ks[4], (NHEADS, D_INNER), jnp.float32) * s, 'dt_b': jax.random.normal(ks[5], (NHEADS,), jnp.float32) * 0.1, 'B_w': jax.random.normal(ks[6], (NHEADS * D_STATE, D_INNER), jnp.float32) * s, 'C_w': jax.random.normal(ks[7], (NHEADS * D_STATE, D_INNER), jnp.float32) * s, 'D': jnp.ones((NHEADS,), jnp.float32), 'ln_w': jnp.ones((D_INNER,), jnp.float32), 'ln_b': jnp.zeros((D_INNER,), jnp.float32), 'out_proj_w': jax.random.normal(ks[8], (D_MODEL, D_INNER), jnp.float32) * s}
    _L1_attn_all = _L1_attn_setup()
    _L1_attn_in = {k: v for k, v in _L1_attn_all.items() if k in ('in_proj_w', 'conv_w', 'conv_b', 'A_log', 'dt_w', 'dt_b', 'B_w', 'C_w', 'D', 'ln_w', 'ln_b', 'out_proj_w')}
    del _L1_attn_all

    def _L1_ffn_setup():
        import jax, jax.numpy as jnp
        import numpy as np
        D_MODEL = 256
        HIDDEN = 1024
        N_ROUTING = 2
        key = jax.random.key(seed)
        ks = jax.random.split(key, 10)
        s = 0.02
        x = jax.random.normal(ks[0], (4, 1024, D_MODEL), dtype=jnp.float32)
        gate_w = jax.random.normal(ks[1], (N_ROUTING, D_MODEL), dtype=jnp.float32) * s
        w1 = jax.random.normal(ks[2], (N_ROUTING, D_MODEL, HIDDEN), dtype=jnp.float32) * s
        b1 = jax.random.normal(ks[3], (N_ROUTING, HIDDEN), dtype=jnp.float32) * s
        w2 = jax.random.normal(ks[4], (N_ROUTING, HIDDEN, D_MODEL), dtype=jnp.float32) * s
        b2 = jax.random.normal(ks[5], (N_ROUTING, D_MODEL), dtype=jnp.float32) * s
        sw1 = jax.random.normal(ks[6], (D_MODEL, HIDDEN), dtype=jnp.float32) * s
        sb1 = jax.random.normal(ks[7], (HIDDEN,), dtype=jnp.float32) * s
        sw2 = jax.random.normal(ks[8], (HIDDEN, D_MODEL), dtype=jnp.float32) * s
        sb2 = jax.random.normal(ks[9], (D_MODEL,), dtype=jnp.float32) * s
        return {'x': x, 'gate_w': gate_w, 'w1': w1, 'b1': b1, 'w2': w2, 'b2': b2, 'sw1': sw1, 'sb1': sb1, 'sw2': sw2, 'sb2': sb2}
    _L1_ffn_all = _L1_ffn_setup()
    _L1_ffn_in = {k: v for k, v in _L1_ffn_all.items() if k in ('gate_w', 'w1', 'b1', 'w2', 'b2', 'sw1', 'sb1', 'sw2', 'sb2')}
    del _L1_ffn_all
    return {'x': x, 'L0_tok_emb_weight': _L0_tok_in['emb_weight'], 'L0_attn_ln1_g': _L0_attn_in['ln1_g'], 'L0_attn_ln1_b': _L0_attn_in['ln1_b'], 'L0_attn_ln2_g': _L0_attn_in['ln2_g'], 'L0_attn_ln2_b': _L0_attn_in['ln2_b'], 'L0_attn_q_U': _L0_attn_in['q_U'], 'L0_attn_q_V': _L0_attn_in['q_V'], 'L0_attn_q_b': _L0_attn_in['q_b'], 'L0_attn_k_U': _L0_attn_in['k_U'], 'L0_attn_k_V': _L0_attn_in['k_V'], 'L0_attn_k_b': _L0_attn_in['k_b'], 'L0_attn_v_U': _L0_attn_in['v_U'], 'L0_attn_v_V': _L0_attn_in['v_V'], 'L0_attn_v_b': _L0_attn_in['v_b'], 'L0_attn_out_U': _L0_attn_in['out_U'], 'L0_attn_out_V': _L0_attn_in['out_V'], 'L0_attn_out_b': _L0_attn_in['out_b'], 'L0_attn_fc1_U': _L0_attn_in['fc1_U'], 'L0_attn_fc1_V': _L0_attn_in['fc1_V'], 'L0_attn_fc1_b': _L0_attn_in['fc1_b'], 'L0_attn_fc2_U': _L0_attn_in['fc2_U'], 'L0_attn_fc2_V': _L0_attn_in['fc2_V'], 'L0_attn_fc2_b': _L0_attn_in['fc2_b'], 'L0_ffn_w_up': _L0_ffn_in['w_up'], 'L0_ffn_w_down': _L0_ffn_in['w_down'], 'L1_attn_in_proj_w': _L1_attn_in['in_proj_w'], 'L1_attn_conv_w': _L1_attn_in['conv_w'], 'L1_attn_conv_b': _L1_attn_in['conv_b'], 'L1_attn_A_log': _L1_attn_in['A_log'], 'L1_attn_dt_w': _L1_attn_in['dt_w'], 'L1_attn_dt_b': _L1_attn_in['dt_b'], 'L1_attn_B_w': _L1_attn_in['B_w'], 'L1_attn_C_w': _L1_attn_in['C_w'], 'L1_attn_D': _L1_attn_in['D'], 'L1_attn_ln_w': _L1_attn_in['ln_w'], 'L1_attn_ln_b': _L1_attn_in['ln_b'], 'L1_attn_out_proj_w': _L1_attn_in['out_proj_w'], 'L1_ffn_gate_w': _L1_ffn_in['gate_w'], 'L1_ffn_w1': _L1_ffn_in['w1'], 'L1_ffn_b1': _L1_ffn_in['b1'], 'L1_ffn_w2': _L1_ffn_in['w2'], 'L1_ffn_b2': _L1_ffn_in['b2'], 'L1_ffn_sw1': _L1_ffn_in['sw1'], 'L1_ffn_sb1': _L1_ffn_in['sb1'], 'L1_ffn_sw2': _L1_ffn_in['sw2'], 'L1_ffn_sb2': _L1_ffn_in['sb2']}

def reference(x, L0_tok_emb_weight, L0_attn_ln1_g, L0_attn_ln1_b, L0_attn_ln2_g, L0_attn_ln2_b, L0_attn_q_U, L0_attn_q_V, L0_attn_q_b, L0_attn_k_U, L0_attn_k_V, L0_attn_k_b, L0_attn_v_U, L0_attn_v_V, L0_attn_v_b, L0_attn_out_U, L0_attn_out_V, L0_attn_out_b, L0_attn_fc1_U, L0_attn_fc1_V, L0_attn_fc1_b, L0_attn_fc2_U, L0_attn_fc2_V, L0_attn_fc2_b, L0_ffn_w_up, L0_ffn_w_down, L1_attn_in_proj_w, L1_attn_conv_w, L1_attn_conv_b, L1_attn_A_log, L1_attn_dt_w, L1_attn_dt_b, L1_attn_B_w, L1_attn_C_w, L1_attn_D, L1_attn_ln_w, L1_attn_ln_b, L1_attn_out_proj_w, L1_ffn_gate_w, L1_ffn_w1, L1_ffn_b1, L1_ffn_w2, L1_ffn_b2, L1_ffn_sw1, L1_ffn_sb1, L1_ffn_sw2, L1_ffn_sb2):
    import jax
    import jax.numpy as jnp

    def _L0_tok_ref(token_ids, emb_weight):
        import jax, jax.numpy as jnp
        import numpy as np
        BASE = 10000.0

        def _rope_tables(seq_len, embed_dim, dtype):
            inv = 1.0 / BASE ** (jnp.arange(0, embed_dim, 2, dtype=jnp.float32) / embed_dim)
            freqs = jnp.arange(seq_len, dtype=jnp.float32)[:, None] * inv[None, :]
            return (jnp.cos(freqs).astype(dtype), jnp.sin(freqs).astype(dtype))
        x = emb_weight[token_ids]
        seq_len, embed_dim = (x.shape[1], x.shape[2])
        cos, sin = _rope_tables(seq_len, embed_dim, x.dtype)
        x_rot = x[..., ::2]
        x_pass = x[..., 1::2]
        a = x_rot * cos - x_pass * sin
        b = x_rot * sin + x_pass * cos
        out = jnp.stack([a, b], axis=-1).reshape(x.shape)
        return out

    def _L0_attn_ref(hidden_states, ln1_g, ln1_b, ln2_g, ln2_b, q_U, q_V, q_b, k_U, k_V, k_b, v_U, v_V, v_b, out_U, out_V, out_b, fc1_U, fc1_V, fc1_b, fc2_U, fc2_V, fc2_b):
        import jax, jax.numpy as jnp
        import numpy as np
        LN_EPS = 1e-05

        def _layernorm(x, g, b):
            mu = jnp.mean(x, axis=-1, keepdims=True)
            var = jnp.var(x, axis=-1, keepdims=True)
            return (x - mu) * jax.lax.rsqrt(var + LN_EPS) * g + b
        B, S, D = hidden_states.shape
        H, dh = (q_V.shape[0], q_V.shape[2])
        x = _layernorm(hidden_states, ln1_g, ln1_b)
        Q = jnp.einsum('bsd,dhr,hre->bhse', x, q_U, q_V) + q_b[None, :, None, :]
        Pk = jnp.einsum('bsd,dhr->bhsr', x, k_U)
        Pv = jnp.einsum('bsd,dhr->bhsr', x, v_U)
        K = jnp.einsum('bhsr,hrd->bhsd', Pk, k_V) + k_b[None, :, None, :]
        V = jnp.einsum('bhsr,hrd->bhsd', Pv, v_V) + v_b[None, :, None, :]
        scale = 1.0 / jnp.sqrt(jnp.asarray(dh, x.dtype))
        scores = jnp.einsum('bhse,bhte->bhst', Q, K) * scale
        causal = jnp.tril(jnp.ones((S, S), bool))
        scores = jnp.where(causal[None, None], scores, jnp.asarray(-1000000000.0, scores.dtype))
        attn = jax.nn.softmax(scores, axis=-1)
        ctx = jnp.einsum('bhst,bhtd->bhsd', attn, V)
        ctx = ctx.transpose(0, 2, 1, 3).reshape(B, S, D)
        attn_out = ctx @ out_U @ out_V + out_b
        h = hidden_states + attn_out
        x2 = _layernorm(h, ln2_g, ln2_b)
        hmid = jax.nn.gelu(x2 @ fc1_U @ fc1_V + fc1_b, approximate=True)
        mlp_out = hmid @ fc2_U @ fc2_V + fc2_b
        return h + mlp_out

    def _L0_ffn_ref(x, w_up, w_down):
        import jax, jax.numpy as jnp
        import numpy as np
        EPS = 1e-08

        def _ternary_linear(x, w):
            alpha = jnp.mean(jnp.abs(w))
            w_t = jnp.sign(w) * (jnp.abs(w) > 0.5 * alpha).astype(w.dtype)
            w_q = w + jax.lax.stop_gradient(w_t - w)
            d = x.shape[-1]
            rms = jnp.sqrt(jnp.sum(x * x, axis=-1, keepdims=True)) / jnp.sqrt(jnp.asarray(d, x.dtype))
            x_norm = x / (rms + EPS)
            return jnp.einsum('bsd,fd->bsf', x_norm, w_q)
        h = jax.nn.gelu(_ternary_linear(x, w_up), approximate=False)
        return _ternary_linear(h, w_down)

    def _L1_attn_ref(hidden_states, in_proj_w, conv_w, conv_b, A_log, dt_w, dt_b, B_w, C_w, D, ln_w, ln_b, out_proj_w):
        import jax, jax.numpy as jnp
        import numpy as np
        D_MODEL = 256
        EXPAND = 2
        D_INNER = EXPAND * D_MODEL
        HEADDIM = 64
        NHEADS = D_INNER // HEADDIM
        D_STATE = 64
        D_CONV = 4
        BATCH = 2
        SEQ_LEN = 256
        LN_EPS = 1e-05

        def _layernorm(x, w, b):
            mu = jnp.mean(x, axis=-1, keepdims=True)
            var = jnp.var(x, axis=-1, keepdims=True)
            return (x - mu) * jax.lax.rsqrt(var + LN_EPS) * w + b

        def _forward(hidden_states, in_proj_w, conv_w, conv_b, A_log, dt_w, dt_b, B_w, C_w, D, ln_w, ln_b, out_proj_w):
            B_, L, _ = hidden_states.shape
            xz = hidden_states @ in_proj_w.T
            x, z = jnp.split(xz, 2, axis=-1)
            x_ncl = jnp.transpose(x, (0, 2, 1))
            x_conv = jax.lax.conv_general_dilated(x_ncl, conv_w, window_strides=(1,), padding=[(D_CONV - 1, 0)], dimension_numbers=('NCH', 'OIH', 'NCH'), feature_group_count=D_INNER)
            x_conv = x_conv + conv_b[None, :, None]
            x = jnp.transpose(x_conv, (0, 2, 1))
            x = jax.nn.silu(x)
            dt = jax.nn.softplus(x @ dt_w.T + dt_b)
            Bm = (x @ B_w.T).reshape(B_, L, NHEADS, D_STATE)
            Cm = (x @ C_w.T).reshape(B_, L, NHEADS, D_STATE)
            xh = x.reshape(B_, L, NHEADS, HEADDIM)
            A = -jnp.exp(A_log)
            h0 = jnp.zeros((B_, NHEADS, HEADDIM, D_STATE), x.dtype)

            def step(h, inp):
                x_t, dt_t, B_t, C_t = inp
                A_bar = jnp.exp(A[None, :] * dt_t)[..., None, None]
                h = A_bar * h + dt_t[..., None, None] * B_t[:, :, None, :] * x_t[..., None]
                y_t = jnp.einsum('bhpn,bhn->bhp', h, C_t) + D[None, :, None] * x_t
                return (h, y_t)
            xs = (jnp.transpose(xh, (1, 0, 2, 3)), jnp.transpose(dt, (1, 0, 2)), jnp.transpose(Bm, (1, 0, 2, 3)), jnp.transpose(Cm, (1, 0, 2, 3)))
            h_final, y = jax.lax.scan(step, h0, xs)
            y = jnp.transpose(y, (1, 0, 2, 3)).reshape(B_, L, D_INNER)
            y = _layernorm(y, ln_w, ln_b)
            y = y * jax.nn.silu(z)
            output = y @ out_proj_w.T
            return (output, h_final)

        def _reference_tuple_inner(hidden_states, in_proj_w, conv_w, conv_b, A_log, dt_w, dt_b, B_w, C_w, D, ln_w, ln_b, out_proj_w):
            return _forward(hidden_states, in_proj_w, conv_w, conv_b, A_log, dt_w, dt_b, B_w, C_w, D, ln_w, ln_b, out_proj_w)
        return _reference_tuple_inner(hidden_states, in_proj_w, conv_w, conv_b, A_log, dt_w, dt_b, B_w, C_w, D, ln_w, ln_b, out_proj_w)[0]

    def _L1_ffn_ref(x, gate_w, w1, b1, w2, b2, sw1, sb1, sw2, sb2):
        import jax, jax.numpy as jnp
        import numpy as np
        D_MODEL = 256
        HIDDEN = 1024
        N_ROUTING = 2
        B, S, D = x.shape
        xf = x.reshape(-1, D)
        gate_scores = xf @ gate_w.T
        gate_probs = jax.nn.softmax(gate_scores, axis=-1)
        top1 = jnp.argmax(gate_probs, axis=-1)
        one_hot = jax.nn.one_hot(top1, N_ROUTING, dtype=xf.dtype)
        masked = xf[None, :, :] * one_hot.T[:, :, None]
        h = jax.nn.relu(jnp.einsum('end,edh->enh', masked, w1) + b1[:, None, :])
        expert_out = jnp.einsum('enh,ehd->end', h, w2) + b2[:, None, :]
        routing_output = expert_out.sum(axis=0)
        shared = jax.nn.relu(xf @ sw1 + sb1) @ sw2 + sb2
        return (routing_output + shared).reshape(B, S, D)
    h = _L0_tok_ref(x, L0_tok_emb_weight)
    h = h + _L0_attn_ref(_layernorm(h, axis=-1), L0_attn_ln1_g, L0_attn_ln1_b, L0_attn_ln2_g, L0_attn_ln2_b, L0_attn_q_U, L0_attn_q_V, L0_attn_q_b, L0_attn_k_U, L0_attn_k_V, L0_attn_k_b, L0_attn_v_U, L0_attn_v_V, L0_attn_v_b, L0_attn_out_U, L0_attn_out_V, L0_attn_out_b, L0_attn_fc1_U, L0_attn_fc1_V, L0_attn_fc1_b, L0_attn_fc2_U, L0_attn_fc2_V, L0_attn_fc2_b)
    h = h + _L0_ffn_ref(_layernorm(h, axis=-1), L0_ffn_w_up, L0_ffn_w_down)
    h = h + _L1_attn_ref(_layernorm(h, axis=-1), L1_attn_in_proj_w, L1_attn_conv_w, L1_attn_conv_b, L1_attn_A_log, L1_attn_dt_w, L1_attn_dt_b, L1_attn_B_w, L1_attn_C_w, L1_attn_D, L1_attn_ln_w, L1_attn_ln_b, L1_attn_out_proj_w)
    h = h + _L1_ffn_ref(_layernorm(h, axis=-1), L1_ffn_gate_w, L1_ffn_w1, L1_ffn_b1, L1_ffn_w2, L1_ffn_b2, L1_ffn_sw1, L1_ffn_sb1, L1_ffn_sw2, L1_ffn_sb2)
    return h

_drawn_inputs = setup_inputs


def setup_inputs(seed=0):
    import zlib

    import numpy as np

    out = dict(_drawn_inputs(seed))
    spreads = {'L0_attn_ln1_g': (1.0, 0.6),
     'L0_attn_ln1_b': (0.0, 0.8),
     'L0_attn_ln2_g': (1.0, 0.6),
     'L0_attn_ln2_b': (0.0, 0.8),
     'L0_attn_out_b': (0.0, 0.8),
     'L0_attn_fc1_b': (0.0, 0.8),
     'L0_attn_fc2_b': (0.0, 2.0),
     'L1_attn_A_log': (0.0, 0.8),
     'L1_attn_D': (1.0, 0.6),
     'L1_attn_ln_w': (1.0, 0.6),
     'L1_attn_ln_b': (0.0, 0.8)}
    factors = {'L0_attn_q_U': 8.0,
     'L0_attn_q_V': 8.0,
     'L0_attn_q_b': 8.0,
     'L0_attn_k_U': 8.0,
     'L0_attn_k_V': 8.0,
     'L0_attn_k_b': 200.0,
     'L0_attn_v_U': 8.0,
     'L0_attn_v_V': 8.0,
     'L0_attn_v_b': 8.0,
     'L0_attn_out_U': 8.0,
     'L0_attn_out_V': 8.0,
     'L0_attn_fc1_U': 8.0,
     'L0_attn_fc1_V': 8.0,
     'L0_attn_fc2_U': 8.0,
     'L0_attn_fc2_V': 8.0,
     'L1_attn_in_proj_w': 8.0,
     'L1_attn_conv_w': 8.0,
     'L1_attn_conv_b': 55.427,
     'L1_attn_dt_w': 8.0,
     'L1_attn_dt_b': 30.184,
     'L1_attn_B_w': 8.0,
     'L1_attn_C_w': 8.0,
     'L1_attn_out_proj_w': 8.0,
     'L1_ffn_gate_w': 8.0,
     'L1_ffn_w1': 8.0,
     'L1_ffn_b1': 40.388,
     'L1_ffn_w2': 8.0,
     'L1_ffn_b2': 64.0,
     'L1_ffn_sw1': 8.0,
     'L1_ffn_sb1': 52.955,
     'L1_ffn_sw2': 8.0,
     'L1_ffn_sb2': 180.79}
    for name, (base, spread) in spreads.items():
        noise = np.random.default_rng([zlib.crc32(name.encode()), seed]).standard_normal(out[name].shape)
        drawn = base * np.exp(spread * noise) if base else spread * noise
        out[name] = jnp.asarray(drawn.astype(out[name].dtype))
    for name, factor in factors.items():
        out[name] = (out[name] * factor).astype(out[name].dtype)
    return out
```

```python
from contextlib import ExitStack

import concourse.bass as bass
from concourse import mybir

F32 = mybir.dt.float32
F32R = mybir.dt.float32r
I32 = mybir.dt.int32
ACT = mybir.ActivationFunctionType
ALU = mybir.AluOpType
AX_X = mybir.AxisListType.X

P = 128
SEQS = 16
SEQ = 512
TT = SEQ // P
D = 256
FB = D // P
LN_EPS = 1e-5
RMS_EPS = 1e-8
LOOKAHEAD = 2
RING = 3


class Signal:

    def __init__(self, ctx, nc, name, per_seq, credit=0, unit=1):
        self.sem = nc.alloc_semaphore(name=name)
        self.per_seq, self.credit, self.unit = per_seq, credit, unit

    def at(self, s, k):
        return s * (self.per_seq * self.unit) + (k + self.credit) * self.unit


class Loads:

    def __init__(self, ctx, nc, name):
        self.sems = [nc.alloc_semaphore(name=f"{name}{slot}") for slot in range(2)]

    def wait(self, eng, s, slot):
        eng.wait_ge(self.sems[slot], (s - slot) * 8 + 16)


def wait(eng, signal, s, k):
    eng.wait_ge(signal.sem, signal.at(s, k))


def wait_alone(eng, tally, sem, value):
    eng.wait_ge(sem, value)
    eng.sem_inc(tally, 1)


def give_credits(eng, signals):
    for signal in signals:
        if signal.credit:
            eng.sem_inc(signal.sem, signal.credit * signal.unit)


def over_sequences(eng, step):
    with eng.Fori(0, SEQS // 2 - 1) as pair:
        step(pair * 2, 0, False)
        step(pair * 2 + 1, 1, False)
    step(SEQS - 2, 0, False)
    step(SEQS - 1, 1, True)


def split_product(pe, out, w_hi, w_lo, x_hi, x_lo, first, last, shared_bank=False):
    pe.matmul(out, w_hi, x_hi, start=first, stop=False, skip_group_check=shared_bank)
    pe.matmul(out, w_hi, x_lo, start=False, stop=False, skip_group_check=shared_bank)
    return pe.matmul(out, w_lo, x_hi, start=False, stop=last, skip_group_check=shared_bank)


def tiles_of(x, s):
    return x.rearrange("(s t p) d -> s p t d", t=TT, p=P)[s]


class Ring:

    def __init__(self, ctx, nc, name, banks, before, each, end, skipped=()):
        self.banks, self.before, self.each, self.end, self.skipped = banks, before, each, end, skipped
        self.full = nc.alloc_semaphore(name=f"{name}_filled")
        self.free = {r: nc.alloc_semaphore(name=f"{name}_freed_by_{r}") for r in sorted(set(dict(each).values()))}
        assert len(before) % banks == 0 and len(each) % banks == 0

    def _uses(self, s, last):
        return self.before if s is None else self.end if last else self.each

    def _place(self, s, use, last):
        return [u for u, _ in self._uses(s, last)].index(use)

    def bank(self, s, use, last):
        return self._place(s, use, last) % self.banks

    def filled(self, s, use, last):
        n = self._place(s, use, last) + 1
        return n if s is None else s * len(self.each) + (len(self.before) - len(self.skipped) + n)

    def read(self, s, use, last):
        uses = self._uses(s, last)
        at = self._place(s, use, last)
        reader = uses[at][1]
        n = sum(r == reader for _, r in uses[:at + 1])
        if s is not None:
            n += self._earlier(s, reader)
        return self.free[reader], n

    def _earlier(self, s, reader):
        n = sum(r == reader for _, r in self.before) - sum(r == reader for _, r in self.skipped)
        return s * sum(r == reader for _, r in self.each) + n

    def freed(self, s, use, last):
        at = self._place(s, use, last)
        uses = self._uses(s, last)
        if at >= self.banks:
            reader = uses[at - self.banks][1]
            needs = [(reader, sum(r == reader for _, r in uses[:at - self.banks + 1]))]
        elif s is None:
            return []
        else:
            needs = [(reader, 0) for reader in self.free]
        found = []
        for reader, n in needs:
            if s is not None:
                n += self._earlier(s, reader)
            found.append((self.free[reader], n))
        return found


def wait_free(pe, ring, s, use, last):
    for sem, value in ring.freed(s, use, last):
        pe.wait_ge(sem, value)


def wait_filled(eng, ring, s, use, last):
    eng.wait_ge(ring.full, ring.filled(s, use, last))


def wait_read(eng, ring, s, use, last):
    eng.wait_ge(*ring.read(s, use, last))


def attention_phase(nc, ident_dram, sel_dram, mask_dram, rope_cos, rope_sin, tokens, emb, ln_cols,
                    q_ut, q_v, q_b_col, k_ut, k_v, k_b_col, v_ut, v_v, v_b, out_ut, out_v, out_b, h0_out, x_out):
    H, R, HD = q_v.shape
    GROUPS = 2
    GH = H // GROUPS
    PAIRS = H // 2
    ROB = out_ut.shape[0] // 2
    SCALE = float(HD) ** -0.5
    BF16 = mybir.dt.bfloat16
    assert GH * HD == P and D == H * HD and TT == 4

    PIECES = ((3,), (2, 0), (1,))
    NP = len(PIECES)
    TURNED_BY = ("act", "dve", "act")
    AT = {3: 0, 2: 4, 0: 7, 1: 8}
    TILES = 10

    def columns(qt, keys=None):
        start = AT[qt] * P
        return slice(start, start + (qt + 1) * P)

    WORK = {(0, 1): "oturn1", (1, 1): "out0", (2, 0): "out1", (8, 1): "oturn0"}
    FRONT = ["turn0", "turn1", "q0", "k0", "v0", "v1", "q1", "k1"]
    for j in range(PAIRS):
        FRONT += [f"ksel{j}", f"qsel{j}"]
    at = (3, 1)
    for name in FRONT:
        while at in WORK:
            at = (at[0] + at[1], 1 - at[1])
        WORK[at] = name
    TAIL = ["oturn1", "out0", "out1"]
    READER = {"turn": "dve", "q": "act", "k": "act", "v": "dve", "ksel": "act", "qsel": "dve", "oturn": "dve", "out": "dve"}
    WORK_ORDER = [WORK[h, i] for h in range(H) for i in range(2) if (h, i) in WORK]

    def kind(name):
        return name.rstrip("0123456789")

    def with_reader(names):
        return [(name, READER[kind(name)]) for name in names]

    NORM_AT = {0: "moments", 1: "x", 2: "moments2", 3: "xn"}

    def over_steps(eng, step, peeled):
        step(0, 0, True, False)
        with eng.Fori(0, (SEQS - 1 - peeled) // 2) as pair:
            step(pair * 2 + 1, 1, False, False)
            step(pair * 2 + 2, 0, False, False)
        for s in range(SEQS - peeled, SEQS):
            step(s, s % 2, False, s == SEQS - 1)

    with ExitStack() as ctx:
        def sb(name, shape, dt=F32):
            return ctx.enter_context(nc.sbuf_tensor("att_" + name, shape, dt))

        def psum(name, shape):
            return ctx.enter_context(nc.psum_tensor("att_" + name, shape, F32))

        def sem(name):
            return nc.alloc_semaphore(name="att_" + name)

        def signal(name, per_seq, credit=0, unit=1):
            return Signal(ctx, nc, "att_" + name, per_seq, credit, unit)

        w_scaled = sb("w_scaled", [P, 3, FB, D])
        w_hi, w_lo = sb("w_hi", [P, 3, FB, D], F32R), sb("w_lo", [P, 3, FB, D], F32R)
        wo_raw = sb("wo_raw", [P, FB, D])
        wo_hi, wo_lo = sb("wo_hi", [P, FB, D], F32R), sb("wo_lo", [P, FB, D], F32R)
        ln = sb("ln", [P, 2, FB])
        ln_b_wide = sb("ln_b_wide", [P, FB, P])
        b_in, b_col = sb("b_in", [P, 2, GROUPS]), sb("b_col", [P, 2, GROUPS])
        vb_in, vb_all = sb("vb_in", [P, D]), sb("vb_all", [P, D])
        ob_all = sb("ob_all", [P, D])
        ident, ident16 = sb("ident", [P, P]), sb("ident16", [P, P], BF16)
        mask_in, mask16 = sb("mask_in", [P, P]), sb("mask16", [P, P], BF16)
        sel = sb("sel", [P, 4, GH // 2, P], F32R)
        cos, sin = sb("cos", [P, TT, D // 2]), sb("sin", [P, TT, D // 2])
        minus_half = sb("minus_half", [P, TT])
        factor_u1 = sb("factor_u1", [P, H, D])
        factor_v = sb("factor_v", [P, 3, H, HD])
        factor_ou, factor_ov = sb("factor_ou", [P, 2, D]), sb("factor_ov", [P, 2, D])

        ids = sb("ids", [P, SEQS * TT], I32)
        ids_now = sb("ids_now", [P, TT], I32)
        e = sb("e", [P, TT, D])
        rope_work = sb("rope_work", [P, 2, TT, D // 2])
        h0 = sb("h0", [P, TT, D])
        stats, stats2 = sb("stats", [P, TT, 6]), sb("stats2", [P, TT, 6])
        moments, moments2 = sb("moments", [P, TT, 2]), sb("moments2", [P, TT, 2])
        var_eps, var_eps2 = sb("var_eps", [P, TT]), sb("var_eps2", [P, TT])
        rstd, rstd2 = sb("rstd", [P, TT]), sb("rstd2", [P, TT])
        x, xn = sb("x", [P, TT, D]), sb("xn", [P, TT, D])
        xb = sb("xb", [P, 2, TT, D])
        xT_hi, xT_lo = sb("xT_hi", [P, FB, SEQ], F32R), sb("xT_lo", [P, FB, SEQ], F32R)
        qk = sb("qk", [P, 2, SEQ])
        qk_hi, qk_lo = sb("qk_hi", [P, 2, GROUPS, SEQ], F32R), sb("qk_lo", [P, 2, GROUPS, SEQ], F32R)
        q_rows = sb("q_rows", [P, H, SEQ], F32R)
        k_rows = sb("k_rows", [P, PAIRS, SEQ], F32R)
        v = sb("v", [P, 2, TT, D])
        neg_max = sb("neg_max", [P, 2, TT])
        exps = sb("exps", [P, 4, TILES * P])
        denom = sb("denom", [P, H, TT])
        recip = sb("recip", [P, GH, TT])
        o = sb("o", [P, TT, P])
        oT_hi, oT_lo = sb("oT_hi", [P, GROUPS, SEQ], F32R), sb("oT_lo", [P, GROUPS, SEQ], F32R)
        factor_u0 = exps[:, :, :].rearrange("p a b -> p (a b)")[:, 0:H * D].rearrange("p (h d) -> p h d", h=H)
        w_raw = v[:, :, :, :].rearrange("p a b c -> p (a b c)")[:, 0:3 * FB * D].rearrange("p (i f d) -> p i f d", i=3, f=FB)

        ps_s = psum("ps_s", [P, NP, SEQ])
        ps_t = psum("ps_t", [P, 2, SEQ])
        ps_o = psum("ps_o", [P, GROUPS, TT, P])
        ps_w = psum("ps_w", [P, SEQ])

        ring = Ring(ctx, nc, "att_work", 1, with_reader(FRONT), with_reader(WORK_ORDER),
                    with_reader(TAIL + ["oturn0"]) + [("last_" + n, "dve") for n in TAIL], skipped=with_reader(TAIL))
        consts_in, sel_in, filled = sem("consts_in"), sem("sel_in"), sem("filled")
        factors_in = [sem(f"factors_in{i}") for i in range(4)]
        fused, w_copied, w_split_hi, w_ready = sem("fused"), sem("w_copied"), sem("w_split_hi"), sem("w_ready")
        wide_made, bias_fused, consts16 = sem("wide_made"), sem("bias_fused"), sem("consts16")
        ids_in = sem("ids_in")
        ids_copied = signal("ids_copied", 1)
        gathered = signal("gathered", 1, unit=16 * TT)
        rope_part = signal("rope_part", 2)
        rope_done = signal("rope_done", 2)
        h0_stored = signal("h0_stored", 1, credit=1, unit=16)
        h0_read = signal("h0_read", 1, credit=1)
        x_stored = signal("x_stored", 1, credit=2, unit=16)
        alone, alone_pool, alone_sp = sem("waits_of_dve"), sem("waits_of_pool"), sem("waits_of_sp")
        stats_done, stats2_done = signal("stats_done", TT), signal("stats2_done", TT)
        moments_done, moments2_done = signal("moments_done", TT), signal("moments2_done", TT)
        eps_added, eps2_added = signal("eps_added", 1), signal("eps2_added", 1)
        rstd_done, rstd2_done = signal("rstd_done", 1), signal("rstd2_done", 1)
        x_done, xn_done = signal("x_done", TT), signal("xn_done", TT)
        biased = signal("biased", 1, credit=1)
        turn_hi = signal("turn_hi", FB)
        qk_copied = signal("qk_copied", 2 * GROUPS)
        qk_split = signal("qk_split", 2 * GROUPS, credit=2)
        summed = signal("summed", NP * H)
        max_done = signal("max_done", NP * H)
        exp_done = signal("exp_done", NP * H, credit=NP)
        turned = signal("turned", NP * H)
        taken = {"act": signal("taken_by_act", 2 * H, credit=2), "dve": signal("taken_by_dve", H, credit=1)}
        o_summed = signal("o_summed", GROUPS)
        recip_done = signal("recip_done", GROUPS, credit=2)
        o_done = signal("o_done", GROUPS, credit=2)
        oturn_hi = signal("oturn_hi", GROUPS)

        def taken_at(h, p):
            by = TURNED_BY[p]
            per = TURNED_BY.count(by)
            return taken[by], h * per + TURNED_BY[:p + 1].count(by)

        def do_work(work, s, slot, first, last, h, i):
            name = WORK.get((h, i))
            if name is None or (first and name in TAIL) or (last and name in FRONT):
                return
            work(name, s, slot, last)

        block = ctx.enter_context(nc.Block())
        CONSTS = 10

        @block.sync
        def _(sp):
            give_credits(sp, [h0_stored, x_stored])
            sp.dma_start(ids[:, :], tokens).then_inc(ids_in, 16)

            def factors(i, ut, vv, buffer):
                sp.dma_start(buffer[0:R, :, :], ut.rearrange("h r d -> r h d")).then_inc(factors_in[i], 16)
                sp.dma_start(factor_v[0:R, i, :, :], vv.rearrange("h r d -> r h d")).then_inc(factors_in[i], 16)

            factors(0, q_ut, q_v, factor_u0)
            sp.dma_start(cos[:, :, :], rope_cos.rearrange("(t p) d -> p t d", p=P)).then_inc(consts_in, 16)
            sp.dma_start(sin[:, :, :], rope_sin.rearrange("(t p) d -> p t d", p=P)).then_inc(consts_in, 16)
            factors(1, k_ut, k_v, factor_u1)
            sp.dma_start(ln[:, :, :], ln_cols.rearrange("p (k f) -> p k f", f=FB)).then_inc(consts_in, 16)
            sp.dma_start(ident[:, :], ident_dram).then_inc(consts_in, 16)
            sp.dma_start(mask_in[:, :], mask_dram).then_inc(consts_in, 16)
            sp.dma_start(b_in[:, 0, :], q_b_col).then_inc(consts_in, 16)
            sp.dma_start(b_in[:, 1, :], k_b_col).then_inc(consts_in, 16)
            sp.dma_start(vb_in[:, :], v_b.partition_broadcast(P)).then_inc(consts_in, 16)
            sp.dma_start(ob_all[:, :], out_b.partition_broadcast(P)).then_inc(consts_in, 16)
            sp.wait_ge(fused, 1)
            factors(2, v_ut, v_v, factor_u0)
            sp.dma_start(factor_ou[0:ROB, :, :], out_ut.rearrange("(b r) d -> r b d", b=2)).then_inc(factors_in[3], 16)
            sp.dma_start(factor_ov[0:ROB, :, :], out_v.rearrange("(b r) d -> r b d", b=2)).then_inc(factors_in[3], 16)
            sp.dma_start(xb[:, :, :, :].rearrange("p a b c -> p (a b c)").rearrange("p (k j m) -> p k j m", k=4, j=GH // 2),
                         sel_dram.rearrange("k j p m -> p k j m")).then_inc(sel_in, 16)
            sp.wait_ge(sel_in, 16)
            sp.sem_inc(consts_in, 16)

            def store_h0(s):
                wait_alone(sp, alone_sp, rope_done.sem, rope_done.at(s, 2))
                sp.dma_start(tiles_of(h0_out, s), h0[:, :, :]).then_inc(h0_stored.sem, 16)

            store_h0(0)
            store_h0(1)

            def step(s, slot, first, last):
                if not first:
                    wait_alone(sp, alone_sp, *ring.read(s, "out1", last))
                    wait_alone(sp, alone_sp, biased.sem, biased.at(s, 1))
                    sp.dma_start(tiles_of(x_out, s - 1), xb[:, 1 - slot]).then_inc(x_stored.sem, 16)
                if not (isinstance(s, int) and s + 2 >= SEQS):
                    store_h0(s + 2)

            over_steps(sp, step, 3)
            wait_read(sp, ring, SEQS - 1, "last_out1", True)
            sp.dma_start(tiles_of(x_out, SEQS - 1), xb[:, (SEQS - 1) % 2]).then_inc(x_stored.sem, 16)
            wait(sp, x_stored, SEQS, 0)
            wait(sp, h0_stored, SEQS, 0)

        @block.gpsimd
        def _(pool):
            give_credits(pool, [biased])
            pool.memset(minus_half[:, :], -0.5).then_inc(filled, 1)
            pool.memset(q_rows[:, :, :].bitcast(F32), 0.0).then_inc(filled, 1)
            pool.wait_ge(filled, 2)
            pool.wait_ge(ids_in, 16)

            def gather(s):
                pool.tensor_copy(ids_now[:, :], ids[:, bass.ds(s * TT, TT)]).then_inc(ids_copied.sem, 1)
                wait_alone(pool, alone_pool, ids_copied.sem, ids_copied.at(s, 1))
                for t in range(TT):
                    pool.indirect_dma_start(e[:, t, :], None, emb, bass.IndirectOffsetOnAxis(ap=ids_now[:, t:t + 1], axis=0)
                                            ).then_inc(gathered.sem, 16)

            def rope(s):
                wait(pool, gathered, s, 1)
                even, odd = e[:, :, 0:D:2], e[:, :, 1:D:2]
                a, b = rope_work[:, 0], rope_work[:, 1]
                pool.tensor_tensor(a, even, cos[:, :, :], ALU.mult)
                pool.tensor_tensor(b, odd, sin[:, :, :], ALU.mult).then_inc(rope_part.sem, 1)
                wait(pool, rope_part, s, 1)
                wait(pool, h0_stored, s, 0)
                wait(pool, h0_read, s, 0)
                pool.tensor_tensor(h0[:, :, 0:D:2], a, b, ALU.subtract).then_inc(rope_done.sem, 1)
                wait(pool, rope_done, s, 1)
                pool.tensor_tensor(a, even, sin[:, :, :], ALU.mult)
                pool.tensor_tensor(b, odd, cos[:, :, :], ALU.mult).then_inc(rope_part.sem, 1)
                wait(pool, rope_part, s, 2)
                pool.tensor_tensor(h0[:, :, 1:D:2], a, b, ALU.add).then_inc(rope_done.sem, 1)

            def norm(s, done, mom, added, ve, ready, r):
                wait_alone(pool, alone_pool, done.sem, done.at(s, TT))
                pool.tensor_scalar(ve[:, :], mom[:, :, 1], LN_EPS, None, ALU.add).then_inc(added.sem, 1)
                wait(pool, added, s, 1)
                pool.tensor_tensor(r[:, :], ve[:, :], minus_half[:, :], ALU.pow).then_inc(ready.sem, 1)

            def norms(s, slot):
                norm(s, moments_done, moments, eps_added, var_eps, rstd_done, rstd)
                norm(s, moments2_done, moments2, eps2_added, var_eps2, rstd2_done, rstd2)
                wait(pool, x_done, s, TT)
                wait(pool, x_stored, s, -1)
                pool.tensor_tensor(xb[:, slot], x[:, :, :], ob_all[:, :].unsqueeze(1).broadcast_to([P, TT, D]),
                                   ALU.add).then_inc(biased.sem, 1)

            gather(0)
            pool.wait_ge(consts_in, 16 * CONSTS)
            rope(0)
            pool.wait_ge(consts16, 3)
            norms(0, 0)
            gather(1)
            rope(1)

            def step(s, slot, first, last):
                if not (isinstance(s, int) and s + 2 >= SEQS):
                    gather(s + 2)
                if not last:
                    norms(s + 1, 1 - slot)
                if not (isinstance(s, int) and s + 2 >= SEQS):
                    rope(s + 2)

            over_steps(pool, step, 3)

        def fused_bank(i):
            return (ps_s[:, i, :] if i < 3 else ps_t[:, 0, :]).rearrange("p (f d) -> p f d", f=FB)

        @block.scalar
        def _(act):
            give_credits(act, [exp_done, taken["act"]])
            act.wait_ge(consts_in, 16 * CONSTS)
            act.activation(sel[:, :, :, :].rearrange("p a b c -> p (a b c)"), xb[:, :, :, :].rearrange("p a b c -> p (a b c)"),
                           ACT.Copy).then_inc(consts16, 1)
            act.activation(ident16[:, :], ident[:, :], ACT.Copy).then_inc(consts16, 1)
            act.activation(mask16[:, :], mask_in[:, :], ACT.Copy).then_inc(consts16, 1)
            for i in range(3):
                act.wait_ge(w_copied, 2 * (i + 1))
                act.activation(w_hi[:, i], w_scaled[:, i], ACT.Copy).then_inc(w_split_hi, 1)
            act.wait_ge(w_copied, 7)
            act.activation(wo_hi[:, :, :], wo_raw[:, :, :], ACT.Copy).then_inc(w_split_hi, 1)

            def work(name, s, slot, last):
                k, n = kind(name), int(name[-1])
                if k == "v" or k == "out" or k == "qsel":
                    return
                wait_filled(act, ring, s, name, last)
                of = 0 if s is None else s if k == "oturn" else s + 1
                if k == "turn":
                    act.activation(xT_hi[:, n, :], ps_w[:, :], ACT.Copy).then_inc(turn_hi.sem, 1)
                if k == "oturn":
                    act.activation(oT_hi[:, n, :], ps_w[:, :], ACT.Copy).then_inc(oturn_hi.sem, 1)
                if k in ("q", "k"):
                    i = "qk".index(k)
                    wait(act, qk_split, of, 2 * n + i - 1)
                    bias = b_col[:, i, n:n + 1]
                    act.activation(qk[:, i, :], ps_w[:, :], ACT.Identity, bias=bias)
                    act.activation(qk_hi[:, i, n, :], ps_w[:, :], ACT.Identity, bias=bias
                                   ).then_inc(ring.free["act"], 1)
                if k == "ksel":
                    act.activation(k_rows[:, n, :], ps_w[:, :], ACT.Copy).then_inc(ring.free["act"], 1)

            def exp(s, h, p):
                wait(act, max_done, s, NP * h + p + 1)
                if p == 0 and h % GH == 0:
                    wait(act, recip_done, s, h // GH - 1)
                for qt in PIECES[p]:
                    first = AT[PIECES[p][0]]
                    src = ps_s[:, p, (AT[qt] - first) * P:(AT[qt] - first + qt + 1) * P]
                    done = act.activation(exps[:, h % 2, columns(qt)], src, ACT.Exp, bias=neg_max[:, h % 2, qt:qt + 1],
                                          accum_out=denom[:, h, qt:qt + 1])
                done.then_inc(exp_done.sem, 1)

            def take(s, h, p):
                wait(act, turned, s, NP * h + p + 1)
                piece = slice(AT[PIECES[p][0]] * P, AT[PIECES[p][0]] * P + sum(qt + 1 for qt in PIECES[p]) * P)
                n = piece.stop - piece.start
                act.activation(exps[:, 2 + h % 2, piece], ps_t[:, (NP * h + p) % 2, 0:n], ACT.Copy
                               ).then_inc(taken["act"].sem, 1)

            act.wait_ge(w_ready, 9)
            for name in FRONT:
                work(name, None, 0, False)
            for p in range(NP):
                exp(0, 0, p)

            def step(s, slot, first, last):
                for h in range(H):
                    more = h < H - 1 or not last
                    nxt = (s, h + 1) if h < H - 1 else (s + 1, 0)
                    take(s, h, 0)
                    if more:
                        exp(*nxt, 0)
                    do_work(work, s, slot, first, last, h, 0)
                    take(s, h, 2)
                    if more:
                        exp(*nxt, 1)
                        exp(*nxt, 2)
                    do_work(work, s, slot, first, last, h, 1)

            over_steps(act, step, 1)
            wait_filled(act, ring, SEQS - 1, "last_oturn1", True)
            act.activation(oT_hi[:, 1, :], ps_w[:, :], ACT.Copy).then_inc(oturn_hi.sem, 1)

        @block.vector
        def _(dve):
            give_credits(dve, [qk_split, taken["dve"], recip_done, o_done, h0_read])
            dve.wait_ge(consts_in, 16 * CONSTS)
            for f in range(FB):
                dve.tensor_copy(ln_b_wide[:, f, :], ln[:, 1, f:f + 1].broadcast_to([P, P])).then_inc(wide_made, 1)
            for i in range(3):
                scale = SCALE if i == 0 else 1.0
                dve.wait_ge(fused, i + 1)
                dve.tensor_scalar(w_raw[:, i], fused_bank(i), scale, None, ALU.mult).then_inc(w_copied, 1)
                dve.wait_ge(w_copied, 2 * i + 1)
                for f in range(FB):
                    done = dve.tensor_scalar(w_scaled[:, i, f, :], w_raw[:, i, f, :], ln[:, 0, f:f + 1], None, ALU.mult)
                done.then_inc(w_copied, 1)
            dve.wait_ge(fused, 4)
            dve.tensor_copy(wo_raw[:, :, :], fused_bank(3)).then_inc(w_copied, 1)
            dve.wait_ge(w_copied, 7)
            for i in range(3):
                dve.wait_ge(w_split_hi, i + 1)
                dve.tensor_tensor(w_lo[:, i], w_scaled[:, i], w_hi[:, i], ALU.subtract).then_inc(w_ready, 1)
            dve.wait_ge(w_split_hi, 4)
            dve.tensor_tensor(wo_lo[:, :, :], wo_raw[:, :, :], wo_hi[:, :, :], ALU.subtract).then_inc(w_ready, 1)
            dve.wait_ge(bias_fused, 1)
            dve.scalar_tensor_tensor(b_col[:, 0, :], b_in[:, 0, :], SCALE, ps_t[:, 1, 0:GROUPS], ALU.mult,
                                     ALU.add).then_inc(w_ready, 1)
            dve.tensor_tensor(b_col[:, 1, :], b_in[:, 1, :], ps_t[:, 1, GROUPS:2 * GROUPS], ALU.add).then_inc(w_ready, 1)
            dve.tensor_tensor(vb_all[:, :], vb_in[:, :], ps_t[:, 1, D:2 * D], ALU.add).then_inc(w_ready, 1)
            dve.wait_ge(w_ready, 7)
            dve.wait_ge(filled, 2)
            dve.sem_inc(w_ready, 2)

            def norm_part(part, s, slot):
                if part == "moments":
                    wait(dve, rope_done, s, 2)
                    for t in range(TT):
                        dve.bn_stats(stats[:, t, :], h0[:, t, :]).then_inc(stats_done.sem, 1)
                    wait_alone(dve, alone, stats_done.sem, stats_done.at(s, TT))
                    for t in range(TT):
                        dve.bn_aggr(moments[:, t, :], stats[:, t, :]).then_inc(moments_done.sem, 1)
                if part == "x":
                    wait(dve, rstd_done, s, 1)
                    wait(dve, biased, s, 0)
                    for t in range(TT):
                        done = dve.tensor_scalar(x[:, t, :], h0[:, t, :], moments[:, t, 0:1], rstd[:, t:t + 1],
                                                 ALU.subtract, ALU.mult).then_inc(x_done.sem, 1)
                    dve.wait_ge(x_done.sem, x_done.at(s, TT))
                    dve.sem_inc(h0_read.sem, 1)
                if part == "moments2":
                    for t in range(TT):
                        dve.bn_stats(stats2[:, t, :], x[:, t, :]).then_inc(stats2_done.sem, 1)
                    wait_alone(dve, alone, stats2_done.sem, stats2_done.at(s, TT))
                    for t in range(TT):
                        dve.bn_aggr(moments2[:, t, :], stats2[:, t, :]).then_inc(moments2_done.sem, 1)
                if part == "xn":
                    wait(dve, rstd2_done, s, 1)
                    for t in range(TT):
                        dve.tensor_scalar(xn[:, t, :], x[:, t, :], moments2[:, t, 0:1], rstd2[:, t:t + 1],
                                          ALU.subtract, ALU.mult).then_inc(xn_done.sem, 1)

            def work(name, s, slot, last):
                k, n = kind(name), int(name[-1])
                of, vslot = (0, 0) if s is None else (s + 1, 1 - slot)
                if k == "turn":
                    wait(dve, turn_hi, of, n + 1)
                    dve.tensor_tensor(xT_lo[:, n, :], ps_w[:, :], xT_hi[:, n, :], ALU.subtract).then_inc(ring.free["dve"], 1)
                if k == "oturn":
                    wait(dve, oturn_hi, s - 1 if n else s, n + 1)
                    dve.tensor_tensor(oT_lo[:, n, :], ps_w[:, :], oT_hi[:, n, :], ALU.subtract).then_inc(ring.free["dve"], 1)
                if k in ("q", "k"):
                    i = "qk".index(k)
                    dve.wait_ge(*ring.read(s, name, last))
                    dve.tensor_tensor(qk_lo[:, i, n, :], qk[:, i, :], qk_hi[:, i, n, :], ALU.subtract).then_inc(qk_split.sem, 1)
                if k == "v":
                    wait_filled(dve, ring, s, name, last)
                    dve.tensor_tensor(v[:, vslot, 2 * n:2 * n + 2, :], ps_w[:, :].rearrange("p (t d) -> p t d", t=2),
                                      vb_all[:, :].unsqueeze(1).broadcast_to([P, 2, D]), ALU.add
                                      ).then_inc(ring.free["dve"], 1)
                if k == "qsel":
                    wait_filled(dve, ring, s, name, last)
                    dve.tensor_copy(q_rows[0:P // 2, 2 * n, :], ps_w[0:P // 2, :])
                    dve.tensor_copy(q_rows[P // 2:P, 2 * n + 1, :], ps_w[P // 2:P, :]).then_inc(ring.free["dve"], 1)
                if k == "out":
                    wait_filled(dve, ring, s, name, last)
                    wait(dve, biased, s, 0)
                    dst = xb[:, 1 - slot, 2 * n:2 * n + 2, :]
                    dve.tensor_tensor(dst, dst, ps_w[:, :].rearrange("p (t d) -> p t d", t=2), ALU.add
                                      ).then_inc(ring.free["dve"], 1)

            def maximum(s, h, p):
                wait(dve, summed, s, NP * h + p + 1)
                for qt in PIECES[p]:
                    first = AT[PIECES[p][0]]
                    src = ps_s[:, p, (AT[qt] - first) * P:(AT[qt] - first + qt + 1) * P]
                    done = dve.tensor_reduce(neg_max[:, h % 2, qt:qt + 1], src, AX_X, ALU.max, negate=True)
                done.then_inc(max_done.sem, 1)

            def take(s, h, p):
                wait(dve, turned, s, NP * h + p + 1)
                piece = slice(AT[PIECES[p][0]] * P, AT[PIECES[p][0]] * P + sum(qt + 1 for qt in PIECES[p]) * P)
                n = piece.stop - piece.start
                dve.tensor_copy(exps[:, 2 + h % 2, piece], ps_t[:, (NP * h + p) % 2, 0:n]).then_inc(taken["dve"].sem, 1)

            def normalise(s, g):
                wait(dve, exp_done, s, NP * GH * (g + 1))
                wait(dve, recip_done, s, g - 1)
                wait(dve, o_done, s, g)
                dve.reciprocal(recip[:, :, :], denom[:, g * GH:(g + 1) * GH, :]).then_inc(recip_done.sem, 1)
                wait(dve, o_summed, s, g + 1)
                wait(dve, recip_done, s, g + 1)
                dve.tensor_tensor(o[:, :, :].rearrange("p t (h d) -> p t h d", h=GH),
                                  ps_o[:, g].rearrange("p t (h d) -> p t h d", h=GH),
                                  recip[:, :, :].rearrange("p h t -> p t h").unsqueeze(3).broadcast_to([P, TT, GH, HD]),
                                  ALU.mult).then_inc(o_done.sem, 1)

            norm_part("moments", 0, 0)
            norm_part("x", 0, 0)
            norm_part("moments2", 0, 0)
            norm_part("xn", 0, 0)
            for name in FRONT:
                work(name, None, 0, False)
            for p in range(NP):
                maximum(0, 0, p)

            def step(s, slot, first, last):
                for h in range(H):
                    more = h < H - 1 or not last
                    nxt = (s, h + 1) if h < H - 1 else (s + 1, 0)
                    if more:
                        maximum(*nxt, 0)
                    take(s, h, 1)
                    if h == 0 and not first:
                        normalise(s - 1, 1)
                    if h == GH:
                        normalise(s, 0)
                    if h in NORM_AT and not last:
                        norm_part(NORM_AT[h], s + 1, 1 - slot)
                    do_work(work, s, slot, first, last, h, 0)
                    if more:
                        maximum(*nxt, 1)
                        maximum(*nxt, 2)
                    do_work(work, s, slot, first, last, h, 1)

            over_steps(dve, step, 1)
            normalise(SEQS - 1, 1)
            wait(dve, oturn_hi, SEQS - 1, 2)
            dve.tensor_tensor(oT_lo[:, 1, :], ps_w[:, :], oT_hi[:, 1, :], ALU.subtract).then_inc(ring.free["dve"], 1)
            wait(dve, biased, SEQS - 1, 1)
            for n in range(2):
                wait_filled(dve, ring, SEQS - 1, f"last_out{n}", True)
                dst = xb[:, (SEQS - 1) % 2, 2 * n:2 * n + 2, :]
                dve.tensor_tensor(dst, dst, ps_w[:, :].rearrange("p (t d) -> p t d", t=2), ALU.add
                                  ).then_inc(ring.free["dve"], 1)

        @block.tensor
        def _(pe):
            for i in range(3):
                pe.wait_ge(factors_in[i], 32)
                buffer = factor_u1 if i == 1 else factor_u0
                for h in range(H):
                    for f in range(FB):
                        mm = pe.matmul(fused_bank(i)[:, f, h * HD:(h + 1) * HD], buffer[0:R, h, f * P:(f + 1) * P],
                                       factor_v[0:R, i, h, :], start=True, stop=True, skip_group_check=True)
                mm.then_inc(fused, 1)
            pe.wait_ge(factors_in[3], 32)
            for f in range(FB):
                for b in range(2):
                    mm = pe.matmul(fused_bank(3)[:, f, :], factor_ou[0:ROB, b, f * P:(f + 1) * P], factor_ov[0:ROB, b, :],
                                   start=(b == 0), stop=(b == 1), skip_group_check=True)
            mm.then_inc(fused, 1)
            pe.wait_ge(wide_made, 2)
            pe.wait_ge(w_copied, 6)
            for i in range(2):
                for m in range(GROUPS):
                    for f in range(FB):
                        pe.matmul(ps_t[:, 1, 2 * i + m:2 * i + m + 1], w_raw[:, i, f, m * P:(m + 1) * P], ln[:, 1, f:f + 1],
                                  start=(f == 0), stop=(f == FB - 1), skip_group_check=True)
            for f in range(FB):
                mm = pe.matmul(ps_t[:, 1, D:2 * D], ln_b_wide[:, f, :], w_raw[:, 2, f, :], start=(f == 0), stop=(f == FB - 1),
                               skip_group_check=True)
            mm.then_inc(bias_fused, 1)
            pe.wait_ge(w_ready, 9)
            pe.wait_ge(consts16, 3)

            def work(name, s, slot, last):
                k, n = kind(name), int(name[-1])
                of = 0 if s is None else s + 1
                wait_free(pe, ring, s, name, last)
                if k == "turn":
                    wait(pe, xn_done, of, TT)
                    for t in range(TT):
                        mm = pe.transpose(ps_w[:, t * P:(t + 1) * P], xn[:, t, n * P:(n + 1) * P], ident[:, :])
                if k in ("q", "k"):
                    i = "qk".index(k)
                    wait_read(pe, ring, s, "turn1", last)
                    for f in range(FB):
                        mm = split_product(pe, ps_w[:, :], w_hi[:, i, f, n * P:(n + 1) * P], w_lo[:, i, f, n * P:(n + 1) * P],
                                           xT_hi[:, f, :], xT_lo[:, f, :], f == 0, f == FB - 1)
                if k == "v":
                    for t in range(2):
                        tok = slice((2 * n + t) * P, (2 * n + t + 1) * P)
                        for f in range(FB):
                            mm = split_product(pe, ps_w[:, t * D:(t + 1) * D], xT_hi[:, f, tok], xT_lo[:, f, tok],
                                               w_hi[:, 2, f, :], w_lo[:, 2, f, :], f == 0, f == FB - 1, True)
                if k in ("qsel", "ksel"):
                    i = "qk".index(k[0])
                    g, j = n // (GH // 2), n % (GH // 2)
                    wait(pe, qk_split, of, 2 * g + i + 1)
                    pe.matmul(ps_w[:, :], sel[:, 2 * i, j, :], qk_hi[:, i, g, :], start=True, stop=False)
                    mm = pe.matmul(ps_w[:, :], sel[:, 2 * i + 1, j, :], qk_lo[:, i, g, :], start=False, stop=True)
                if k == "oturn":
                    oturn(s - 1 if n else s, n)
                    return
                if k == "out":
                    wait_read(pe, ring, s, "oturn1", last)
                    mm = out(n)
                mm.then_inc(ring.full, 1)

            def oturn(s, g):
                wait(pe, o_done, s, g + 1)
                for t in range(TT):
                    mm = pe.transpose(ps_w[:, t * P:(t + 1) * P], o[:, t, :], ident[:, :])
                mm.then_inc(ring.full, 1)

            def out(n):
                for t in range(2):
                    tok = slice((2 * n + t) * P, (2 * n + t + 1) * P)
                    for g in range(GROUPS):
                        mm = split_product(pe, ps_w[:, t * D:(t + 1) * D], oT_hi[:, g, tok], oT_lo[:, g, tok],
                                           wo_hi[:, g, :], wo_lo[:, g, :], g == 0, g == GROUPS - 1, True)
                return mm

            def scores(s, h, p, made_in):
                if h % 2 == 0 and p == 0:
                    wait_read(pe, ring, made_in, f"ksel{h // 2}", False)
                    wait_read(pe, ring, made_in, f"qsel{h // 2}", False)
                wait(pe, exp_done, s, NP * (h - 1) + p + 1)
                for qt in PIECES[p]:
                    at = (AT[qt] - AT[PIECES[p][0]]) * P
                    pe.matmul(ps_s[:, p, at:at + (qt + 1) * P], q_rows[:, h, qt * P:(qt + 1) * P],
                              k_rows[:, h // 2, 0:(qt + 1) * P], start=True, stop=False, skip_group_check=True)
                    mm = pe.matmul(ps_s[:, p, at + qt * P:at + (qt + 1) * P], ident16[:, :], mask16[:, :],
                                   start=False, stop=True, skip_group_check=True)
                mm.then_inc(summed.sem, 1)

            def turn(s, h, p):
                wait(pe, exp_done, s, NP * h + p + 1)
                hb, pb = (h - 1, p + 1) if p < 2 else (h, 0)
                by, n = taken_at(hb, pb)
                wait(pe, by, s, n)
                first = AT[PIECES[p][0]]
                for i in range(sum(qt + 1 for qt in PIECES[p])):
                    mm = pe.transpose(ps_t[:, (NP * h + p) % 2, i * P:(i + 1) * P],
                                      exps[:, h % 2, (first + i) * P:(first + i + 1) * P], ident[:, :])
                mm.then_inc(turned.sem, 1)

            def weigh(s, slot, h):
                g = h // GH
                if h % GH == 0:
                    wait(pe, o_done, s, g - 1)
                for p in range(NP):
                    by, n = taken_at(h, p)
                    wait(pe, by, s, n)
                    for qt in PIECES[p]:
                        for kt in range(qt + 1):
                            c = (AT[qt] + kt) * P
                            mm = pe.matmul(ps_o[:, g, qt, (h % GH) * HD:(h % GH + 1) * HD], exps[:, 2 + h % 2, c:c + P],
                                           v[:, slot, kt, h * HD:(h + 1) * HD], start=(kt == 0), stop=(kt == qt),
                                           skip_group_check=True)
                if h % GH == GH - 1:
                    mm.then_inc(o_summed.sem, 1)

            for name in FRONT:
                work(name, None, 0, False)
            for p in range(NP):
                scores(0, 0, p, None)

            def step(s, slot, first, last):
                for h in range(H):
                    more = h < H - 1 or not last
                    nxt, made_in = ((s, h + 1), None if first else s - 1) if h < H - 1 else ((s + 1, 0), s)
                    turn(s, h, 0)
                    turn(s, h, 1)
                    if more:
                        scores(*nxt, 0, made_in)
                    do_work(work, s, slot, first, last, h, 0)
                    turn(s, h, 2)
                    if more:
                        scores(*nxt, 1, made_in)
                        scores(*nxt, 2, made_in)
                    do_work(work, s, slot, first, last, h, 1)
                    weigh(s, slot, h)

            over_steps(pe, step, 1)
            wait_free(pe, ring, SEQS - 1, "last_oturn1", True)
            oturn(SEQS - 1, 1)
            for n in range(2):
                wait_free(pe, ring, SEQS - 1, f"last_out{n}", True)
                out(n).then_inc(ring.full, 1)


def mlp_phase(nc, ident_dram, x_in, res_in, ln_cols, fc1_u, fc1_v, fc1_b_col, fc2_u, fc2_v, fc2_b, x_out):
    F = fc1_v.shape[1]
    R = fc1_u.shape[1]
    K = F // P
    RING, PS_RING = 4, 2
    NORM_WITH = [0, 1]
    TURN_AT = [3, 5]
    TAKE_AT = [min(k + LOOKAHEAD, K - 1) for k in TURN_AT]
    assert R == P

    with ExitStack() as ctx:
        def sb(name, shape, dt=F32):
            return ctx.enter_context(nc.sbuf_tensor("mlp_" + name, shape, dt))

        def psum(name, shape):
            return ctx.enter_context(nc.psum_tensor("mlp_" + name, shape, F32))

        def sem(name):
            return nc.alloc_semaphore(name="mlp_" + name)

        def signal(name, per_seq, credit=0, unit=1):
            return Signal(ctx, nc, "mlp_" + name, per_seq, credit, unit)

        u1_raw, u1_scaled = sb("u1_raw", [P, FB, R]), sb("u1_scaled", [P, FB, R])
        v1_raw, u2_raw, v2_raw = sb("v1_raw", [P, F]), sb("u2_raw", [P, K, R]), sb("v2_raw", [P, D])
        u1_hi, u1_lo = sb("u1_hi", [P, FB, R], F32R), sb("u1_lo", [P, FB, R], F32R)
        v1_hi, v1_lo = sb("v1_hi", [P, F], F32R), sb("v1_lo", [P, F], F32R)
        u2_hi, u2_lo = sb("u2_hi", [P, K, R], F32R), sb("u2_lo", [P, K, R], F32R)
        v2_hi, v2_lo = sb("v2_hi", [P, D], F32R), sb("v2_lo", [P, D], F32R)
        ln = sb("ln", [P, 2, FB])
        rank_bias = sb("rank_bias", [P, 1])
        fc1_b = sb("fc1_b", [P, K])
        fc2_b_all = sb("fc2_b_all", [P, D])
        ident = sb("ident", [P, P])
        x = sb("x", [P, 2, TT, D])
        res = sb("res", [P, 2, TT, D])
        y = sb("y", [P, 2, TT, D])
        stats = sb("stats", [P, TT, 6])
        moments = sb("moments", [P, TT, 2])
        var_eps = sb("var_eps", [P, TT])
        minus_half = sb("minus_half", [P, TT])
        rstd = sb("rstd", [P, TT])
        xn = sb("xn", [P, TT, D])
        xT_hi, xT_lo = sb("xT_hi", [P, FB, SEQ], F32R), sb("xT_lo", [P, FB, SEQ], F32R)
        m1, m1_hi, m1_lo = sb("m1", [P, SEQ]), sb("m1_hi", [P, SEQ], F32R), sb("m1_lo", [P, SEQ], F32R)
        m2_hi, m2_lo = sb("m2_hi", [P, SEQ], F32R), sb("m2_lo", [P, SEQ], F32R)
        hid = sb("hid", [P, RING, SEQ])
        hid_hi, hid_lo = sb("hid_hi", [P, RING, SEQ], F32R), sb("hid_lo", [P, RING, SEQ], F32R)

        ps_hid = psum("ps_hid", [P, PS_RING, SEQ])
        ps_m1, ps_m2, ps_turn = psum("ps_m1", [P, SEQ]), psum("ps_m2", [P, SEQ]), psum("ps_turn", [P, SEQ])
        ps_out = psum("ps_out", [P, TT, D])

        consts_in, filled = sem("consts_in"), sem("filled")
        scaled, bias_summed, halves_hi, w_ready = sem("scaled"), sem("bias_summed"), sem("halves_hi"), sem("w_ready")
        x_loads = Loads(ctx, nc, "mlp_x_loads")
        res_loads = Loads(ctx, nc, "mlp_res_loads")
        y_stored = signal("y_stored", 1, credit=2, unit=16)
        alone, alone_pool = sem("waits_of_dve"), sem("waits_of_pool")
        stats_done = signal("stats_done", TT)
        moments_done = signal("moments_done", TT)
        eps_added = signal("eps_added", 1)
        rstd_done = signal("rstd_done", 1)
        xn_done = signal("xn_done", TT)
        x_added = signal("x_added", 1)
        biased = signal("biased", 1)
        turned = signal("turned", FB)
        turn_hi = signal("turn_hi", FB)
        turn_lo = signal("turn_lo", FB, credit=1)
        m1_summed = signal("m1_summed", 1)
        m1_hi_done = signal("m1_hi_done", 1)
        m1_split = signal("m1_split", 1)
        hid_summed = signal("hid_summed", K)
        hid_act = signal("hid_act", K, credit=RING)
        hid_split = signal("hid_split", K, credit=RING)
        hid_used = signal("hid_used", K, credit=RING)
        m2_hi_done = signal("m2_hi_done", 1)
        m2_split = signal("m2_split", 1, credit=1)
        out_summed = signal("out_summed", TT // 2)
        out_done = signal("out_done", TT // 2, credit=TT // 2)

        def flat(w):
            return w[:, :] if len(w.shape) == 2 else w[:, :, :].rearrange("p a b -> p (a b)")

        block = ctx.enter_context(nc.Block())
        CONSTS = 8

        @block.sync
        def _(sp):
            def load_x(s, slot):
                sp.dma_start(x[:, slot], tiles_of(x_in, s)).then_inc(x_loads.sems[slot], 16)

            def load_res(s, slot):
                sp.dma_start(res[:, slot], tiles_of(res_in, s)).then_inc(res_loads.sems[slot], 16)

            give_credits(sp, [y_stored])
            load_x(0, 0)
            sp.dma_start(u1_raw[:, :, :], fc1_u.rearrange("(f p) r -> p f r", p=P)).then_inc(consts_in, 16)
            sp.dma_start(ln[:, :, :], ln_cols.rearrange("p (k f) -> p k f", f=FB)).then_inc(consts_in, 16)
            sp.dma_start(ident[:, :], ident_dram).then_inc(consts_in, 16)
            sp.dma_start(v1_raw[:, :], fc1_v).then_inc(consts_in, 16)
            sp.dma_start(u2_raw[:, :, :], fc2_u.rearrange("(k p) r -> p k r", p=P)).then_inc(consts_in, 16)
            sp.dma_start(v2_raw[:, :], fc2_v).then_inc(consts_in, 16)
            sp.dma_start(fc1_b[:, :], fc1_b_col).then_inc(consts_in, 16)
            sp.dma_start(fc2_b_all[:, :], fc2_b.partition_broadcast(P)).then_inc(consts_in, 16)
            load_res(0, 0)
            load_x(1, 1)
            load_res(1, 1)

            def step(s, slot, last):
                wait(sp, out_done, s, TT // 2)
                sp.dma_start(tiles_of(x_out, s), y[:, slot]).then_inc(y_stored.sem, 16)
                if not (isinstance(s, int) and s + 2 >= SEQS):
                    load_x(s + 2, slot)
                    load_res(s + 2, slot)

            over_sequences(sp, step)
            wait(sp, y_stored, SEQS, 0)

        @block.gpsimd
        def _(pool):
            pool.memset(minus_half[:, :], -0.5).then_inc(filled, 1)
            pool.wait_ge(filled, 1)
            pool.wait_ge(consts_in, 16 * CONSTS)

            def norm(s):
                wait_alone(pool, alone_pool, moments_done.sem, moments_done.at(s, TT))
                pool.tensor_scalar(var_eps[:, :], moments[:, :, 1], LN_EPS, None, ALU.add).then_inc(eps_added.sem, 1)
                wait(pool, eps_added, s, 1)
                pool.tensor_tensor(rstd[:, :], var_eps[:, :], minus_half[:, :], ALU.pow).then_inc(rstd_done.sem, 1)

            norm(0)

            def step(s, slot, last):
                if not last:
                    norm(s + 1)
                res_loads.wait(pool, s, slot)
                x_loads.wait(pool, s, slot)
                pool.tensor_tensor(res[:, slot], res[:, slot], x[:, slot], ALU.add).then_inc(x_added.sem, 1)
                wait(pool, x_added, s, 1)
                pool.tensor_tensor(res[:, slot], res[:, slot], fc2_b_all[:, :].unsqueeze(1).broadcast_to([P, TT, D]),
                                   ALU.add).then_inc(biased.sem, 1)

            over_sequences(pool, step)

        @block.scalar
        def _(act):
            give_credits(act, [hid_act])
            act.wait_ge(scaled, FB)
            for src, hi in ((u1_scaled, u1_hi), (v1_raw, v1_hi), (u2_raw, u2_hi), (v2_raw, v2_hi)):
                act.activation(flat(hi), flat(src), ACT.Copy).then_inc(halves_hi, 1)

            def turn(s, f):
                wait(act, turned, s, f + 1)
                act.activation(xT_hi[:, f, :], ps_turn[:, :], ACT.Copy).then_inc(turn_hi.sem, 1)

            def take_m1(s):
                wait(act, m1_summed, s, 1)
                act.activation(m1[:, :], ps_m1[:, :], ACT.Identity, bias=rank_bias[:, 0:1])
                act.activation(m1_hi[:, :], ps_m1[:, :], ACT.Identity, bias=rank_bias[:, 0:1]).then_inc(m1_hi_done.sem, 1)

            for f in range(FB):
                turn(0, f)
            act.wait_ge(w_ready, 5)
            take_m1(0)

            def step(s, slot, last):
                for k in range(K):
                    wait(act, hid_summed, s, k + 1)
                    wait(act, hid_split, s, k + 1 - RING)
                    act.activation(hid[:, k % RING, :], ps_hid[:, k % PS_RING, :], ACT.Gelu_apprx_tanh,
                                   bias=fc1_b[:, k:k + 1])
                    wait(act, hid_used, s, k + 1 - RING)
                    act.activation(hid_hi[:, k % RING, :], ps_hid[:, k % PS_RING, :], ACT.Gelu_apprx_tanh,
                                   bias=fc1_b[:, k:k + 1]).then_inc(hid_act.sem, 1)
                    for f in range(FB):
                        if k == TAKE_AT[f] and not last:
                            turn(s + 1, f)
                wait(act, hid_used, s, K)
                act.activation(m2_hi[:, :], ps_m2[:, :], ACT.Copy).then_inc(m2_hi_done.sem, 1)
                if not last:
                    take_m1(s + 1)

            over_sequences(act, step)

        @block.vector
        def _(dve):
            give_credits(dve, [turn_lo, hid_split, m2_split, out_done])
            dve.wait_ge(consts_in, 16 * CONSTS)
            for f in range(FB):
                dve.tensor_scalar(u1_scaled[:, f, :], u1_raw[:, f, :], ln[:, 0, f:f + 1], None,
                                  ALU.mult).then_inc(scaled, 1)
            dve.wait_ge(bias_summed, 1)
            dve.tensor_copy(rank_bias[:, :], ps_m1[:, 0:1]).then_inc(w_ready, 1)
            dve.wait_ge(scaled, FB)
            for i, (src, hi, lo) in enumerate(((u1_scaled, u1_hi, u1_lo), (v1_raw, v1_hi, v1_lo), (u2_raw, u2_hi, u2_lo),
                                               (v2_raw, v2_hi, v2_lo))):
                dve.wait_ge(halves_hi, i + 1)
                dve.tensor_tensor(flat(lo), flat(src), flat(hi), ALU.subtract).then_inc(w_ready, 1)

            def norm_part(s, slot, n):
                if n == 0:
                    x_loads.wait(dve, s, slot)
                    for t in range(TT):
                        dve.bn_stats(stats[:, t, :], x[:, slot, t, :]).then_inc(stats_done.sem, 1)
                    wait_alone(dve, alone, stats_done.sem, stats_done.at(s, TT))
                    for t in range(TT):
                        dve.bn_aggr(moments[:, t, :], stats[:, t, :]).then_inc(moments_done.sem, 1)
                if n == 1:
                    wait(dve, rstd_done, s, 1)
                    for t in range(TT):
                        dve.tensor_scalar(xn[:, t, :], x[:, slot, t, :], moments[:, t, 0:1], rstd[:, t:t + 1],
                                          ALU.subtract, ALU.mult).then_inc(xn_done.sem, 1)

            def turn(s, f):
                wait(dve, turn_hi, s, f + 1)
                dve.tensor_tensor(xT_lo[:, f, :], ps_turn[:, :], xT_hi[:, f, :], ALU.subtract).then_inc(turn_lo.sem, 1)

            def take_m1(s):
                wait(dve, m1_hi_done, s, 1)
                dve.tensor_tensor(m1_lo[:, :], m1[:, :], m1_hi[:, :], ALU.subtract).then_inc(m1_split.sem, 1)

            for n in range(2):
                norm_part(0, 0, n)
            for f in range(FB):
                turn(0, f)
            take_m1(0)

            def step(s, slot, last):
                for k in range(K):
                    wait(dve, hid_act, s, k + 1)
                    dve.tensor_tensor(hid_lo[:, k % RING, :], hid[:, k % RING, :], hid_hi[:, k % RING, :],
                                      ALU.subtract).then_inc(hid_split.sem, 1)
                    if k in NORM_WITH and not last:
                        norm_part(s + 1, 1 - slot, NORM_WITH.index(k))
                    for f in range(FB):
                        if k == TAKE_AT[f] and not last:
                            turn(s + 1, f)
                wait(dve, m2_hi_done, s, 1)
                dve.tensor_tensor(m2_lo[:, :], ps_m2[:, :], m2_hi[:, :], ALU.subtract).then_inc(m2_split.sem, 1)
                if not last:
                    take_m1(s + 1)
                wait(dve, biased, s, 1)
                wait(dve, y_stored, s, -1)
                for h in range(TT // 2):
                    wait(dve, out_summed, s, h + 1)
                    part = slice(2 * h, 2 * h + 2)
                    dve.tensor_tensor(y[:, slot, part, :], ps_out[:, part, :], res[:, slot, part, :],
                                      ALU.add).then_inc(out_done.sem, 1)

            over_sequences(dve, step)

        @block.tensor
        def _(pe):
            give_credits(pe, [hid_used])
            pe.wait_ge(consts_in, 16 * CONSTS)
            for f in range(FB):
                mm = pe.matmul(ps_m1[:, 0:1], u1_raw[:, f, :], ln[:, 1, f:f + 1], start=(f == 0), stop=(f == FB - 1))
            mm.then_inc(bias_summed, 1)

            def turn(s, f):
                wait(pe, xn_done, s, TT)
                wait(pe, turn_lo, s, f)
                for t in range(TT):
                    last = pe.transpose(ps_turn[:, t * P:(t + 1) * P], xn[:, t, f * P:(f + 1) * P], ident[:, :])
                last.then_inc(turned.sem, 1)

            def rank_in(s):
                wait(pe, turn_lo, s, FB)
                wait(pe, m1_split, s, 0)
                for f in range(FB):
                    mm = split_product(pe, ps_m1[:, :], u1_hi[:, f, :], u1_lo[:, f, :], xT_hi[:, f, :], xT_lo[:, f, :],
                                       f == 0, f == FB - 1)
                mm.then_inc(m1_summed.sem, 1)

            for f in range(FB):
                turn(0, f)
            pe.wait_ge(w_ready, 5)
            wait(pe, turn_lo, 0, FB)
            for f in range(FB):
                mm = split_product(pe, ps_m1[:, :], u1_hi[:, f, :], u1_lo[:, f, :], xT_hi[:, f, :], xT_lo[:, f, :],
                                   f == 0, f == FB - 1)
            mm.then_inc(m1_summed.sem, 1)

            def up(s, k):
                if k == 0:
                    wait(pe, m1_split, s, 1)
                wait(pe, hid_act, s, k + 1 - PS_RING)
                h = slice(k * P, (k + 1) * P)
                split_product(pe, ps_hid[:, k % PS_RING, :], v1_hi[:, h], v1_lo[:, h], m1_hi[:, :], m1_lo[:, :],
                              True, True).then_inc(hid_summed.sem, 1)

            def down(s, k):
                wait(pe, hid_split, s, k + 1)
                if k == 0:
                    wait(pe, m2_split, s, 0)
                split_product(pe, ps_m2[:, :], u2_hi[:, k, :], u2_lo[:, k, :], hid_hi[:, k % RING, :],
                              hid_lo[:, k % RING, :], k == 0, k == K - 1).then_inc(hid_used.sem, 1)

            def step(s, slot, last):
                for k in range(LOOKAHEAD):
                    up(s, k)
                for k in range(K):
                    if k + LOOKAHEAD < K:
                        up(s, k + LOOKAHEAD)
                    down(s, k)
                    if k in TURN_AT and not last:
                        turn(s + 1, TURN_AT.index(k))
                if not last:
                    rank_in(s + 1)
                wait(pe, m2_split, s, 1)
                wait(pe, out_done, s, 0)
                for t in range(TT):
                    tok = slice(t * P, (t + 1) * P)
                    mm = split_product(pe, ps_out[:, t, :], m2_hi[:, tok], m2_lo[:, tok], v2_hi[:, :], v2_lo[:, :],
                                       True, True)
                    if t % 2:
                        mm.then_inc(out_summed.sem, 1)

            over_sequences(pe, step)


def ffn_phase(nc, ident_dram, x_in, w_up_t, w_down_t, x_out):
    F = w_up_t.shape[1]
    K = F // P
    RING, PS_RING = 4, 2
    NORM_WITH = [0, 2, 5]
    TURN_AT = [5, 6]
    TAKE_AT = [min(k + LOOKAHEAD, K - 1) for k in TURN_AT]

    with ExitStack() as ctx:
        def sb(name, shape, dt=F32):
            return ctx.enter_context(nc.sbuf_tensor(name, shape, dt))

        def psum(name, shape):
            return ctx.enter_context(nc.psum_tensor(name, shape, F32))

        def sem(name):
            return nc.alloc_semaphore(name=name)

        def signal(name, per_seq, credit=0, unit=1):
            return Signal(ctx, nc, name, per_seq, credit, unit)

        w_raw = sb("ffn_w_raw", [P, 2, FB * F])
        w_abs = sb("ffn_w_abs", [P, FB * F])
        w_sum = sb("ffn_w_sum", [P, 2])
        limit = sb("ffn_limit", [P, 2])
        minus_limit = sb("ffn_minus_limit", [P, 2])
        below = sb("ffn_below", [P, 2, FB * F])
        w_up = sb("ffn_w_up", [P, FB, F], F32R)
        w_down = sb("ffn_w_down", [P, K, D], F32R)
        ones = sb("ffn_ones", [P, P])
        ident = sb("ffn_ident", [P, P])
        x = sb("ffn_x", [P, 2, TT, D])
        y = sb("ffn_y", [P, 2, TT, D])
        stats = sb("ffn_stats", [P, TT, 6])
        moments = sb("ffn_moments", [P, TT, 2])
        var_eps = sb("ffn_var_eps", [P, TT])
        minus_half = sb("ffn_minus_half", [P, TT])
        half = sb("ffn_half", [P, TT])
        rstd = sb("ffn_rstd", [P, TT])
        square_work = sb("ffn_square_work", [P, D])
        x_sq = sb("ffn_x_sq", [P, TT])
        x_ms = sb("ffn_x_ms", [P, TT])
        x_rms = sb("ffn_x_rms", [P, TT])
        x_rms_eps = sb("ffn_x_rms_eps", [P, TT])
        x_scale = sb("ffn_x_scale", [P, TT])
        h_ms = sb("ffn_h_ms", [P, TT])
        h_rms = sb("ffn_h_rms", [P, TT])
        h_rms_eps = sb("ffn_h_rms_eps", [P, TT])
        h_scale = sb("ffn_h_scale", [P, TT])
        xn = sb("ffn_xn", [P, TT, D])
        xr = sb("ffn_xr", [P, TT, D])
        xT_hi = sb("ffn_xT_hi", [P, 2, FB, SEQ], F32R)
        xT_lo = sb("ffn_xT_lo", [P, 2, FB, SEQ], F32R)
        hid = sb("ffn_hid", [P, RING, SEQ])
        hid_sq = sb("ffn_hid_sq", [P, RING, SEQ])
        hid_hi = sb("ffn_hid_hi", [P, RING, SEQ], F32R)
        hid_lo = sb("ffn_hid_lo", [P, RING, SEQ], F32R)

        ps_hid = psum("ffn_ps_hid", [P, PS_RING, SEQ])
        ps_out = psum("ffn_ps_out", [P, 2, TT, D])
        ps_turn = psum("ffn_ps_turn", [P, SEQ])
        ps_sq = psum("ffn_ps_sq", [P, SEQ])

        consts_in, w_in = sem("ffn_consts_in"), sem("ffn_w_in")
        filled, abs_done, total_done, limit_done = sem("ffn_filled"), sem("ffn_abs_done"), sem("ffn_total_done"), sem("ffn_limit_done")
        below_done, w_ready = sem("ffn_below_done"), sem("ffn_w_ready")
        x_loads = Loads(ctx, nc, "ffn_x_loads")
        y_stored = signal("ffn_y_stored", 1, credit=2, unit=16)
        alone, alone_pool = sem("waits_of_dve"), sem("waits_of_pool")
        stats_done = signal("ffn_stats_done", TT)
        moments_done = signal("ffn_moments_done", TT)
        eps_added = signal("ffn_eps_added", 1)
        rstd_done = signal("ffn_rstd_done", 1)
        xn_done = signal("ffn_xn_done", TT)
        x_sq_done = signal("ffn_x_sq_done", TT)
        x_ms_done = signal("ffn_x_ms_done", 1)
        x_rms_done = signal("ffn_x_rms_done", 1)
        x_scale_part = signal("ffn_x_scale_part", 2)
        xr_done = signal("ffn_xr_done", TT)
        turned = signal("ffn_turned", FB)
        turn_hi = signal("ffn_turn_hi", FB)
        turn_lo = signal("ffn_turn_lo", FB, credit=1)
        hid_summed = signal("ffn_hid_summed", K)
        hid_act = signal("ffn_hid_act", K, credit=RING)
        sq_done = signal("ffn_sq_done", K, credit=RING)
        hid_split = signal("ffn_hid_split", K, credit=RING)
        hid_used = signal("ffn_hid_used", K, credit=RING)
        sq_summed = signal("ffn_sq_summed", K, credit=RING)
        h_ms_done = signal("ffn_h_ms_done", 1, credit=1)
        h_rms_done = signal("ffn_h_rms_done", 1)
        h_scale_part = signal("ffn_h_scale_part", 2)
        out_done = signal("ffn_out_done", TT, credit=2 * TT)

        block = ctx.enter_context(nc.Block())

        @block.sync
        def _(sp):
            def load_x(s, slot):
                sp.dma_start(x[:, slot], tiles_of(x_in, s)).then_inc(x_loads.sems[slot], 16)

            give_credits(sp, [y_stored])
            sp.dma_start(w_raw[:, 0, :].rearrange("p (f h) -> p f h", f=FB),
                         w_up_t.rearrange("(f p) h -> p f h", p=P)).then_inc(w_in, 16)
            load_x(0, 0)
            sp.dma_start(w_raw[:, 1, :].rearrange("p (k d) -> p k d", k=K),
                         w_down_t.rearrange("(k p) d -> p k d", p=P)).then_inc(w_in, 16)
            sp.dma_start(ident[:, :], ident_dram).then_inc(consts_in, 16)
            load_x(1, 1)

            def step(s, slot, last):
                wait(sp, out_done, s, TT)
                sp.dma_start(tiles_of(x_out, s), y[:, slot]).then_inc(y_stored.sem, 16)
                if not (isinstance(s, int) and s + 2 >= SEQS):
                    load_x(s + 2, slot)

            over_sequences(sp, step)
            wait(sp, y_stored, SEQS, 0)

        @block.gpsimd
        def _(pool):
            pool.memset(minus_half[:, :], -0.5).then_inc(filled, 1)
            pool.memset(half[:, :], 0.5).then_inc(filled, 1)
            pool.memset(ones[:, :], 1.0).then_inc(filled, 1)
            pool.wait_ge(filled, 3)
            give_credits(pool, [sq_done])

            def norm(s):
                wait_alone(pool, alone_pool, moments_done.sem, moments_done.at(s, TT))
                pool.tensor_scalar(var_eps[:, :], moments[:, :, 1], LN_EPS, None, ALU.add).then_inc(eps_added.sem, 1)
                wait(pool, eps_added, s, 1)
                pool.tensor_tensor(rstd[:, :], var_eps[:, :], minus_half[:, :], ALU.pow).then_inc(rstd_done.sem, 1)

            def rms(s):
                wait_alone(pool, alone_pool, x_sq_done.sem, x_sq_done.at(s, TT))
                pool.tensor_scalar(x_ms[:, :], x_sq[:, :], 1.0 / D, None, ALU.mult).then_inc(x_ms_done.sem, 1)
                wait(pool, x_ms_done, s, 1)
                pool.tensor_tensor(x_rms[:, :], x_ms[:, :], half[:, :], ALU.pow).then_inc(x_rms_done.sem, 1)

            norm(0)
            rms(0)

            def step(s, slot, last):
                for k in range(K):
                    wait(pool, hid_act, s, k + 1)
                    wait(pool, sq_summed, s, k + 1 - RING)
                    pool.tensor_tensor(hid_sq[:, k % RING, :], hid[:, k % RING, :], hid[:, k % RING, :],
                                       ALU.mult).then_inc(sq_done.sem, 1)
                    if k == 0 and not last:
                        norm(s + 1)
                    if k == 4 and not last:
                        rms(s + 1)
                wait(pool, h_ms_done, s, 1)
                pool.tensor_tensor(h_rms[:, :], h_ms[:, :], half[:, :], ALU.pow).then_inc(h_rms_done.sem, 1)

            over_sequences(pool, step)

        @block.scalar
        def _(act):
            give_credits(act, [hid_act])
            act.wait_ge(w_in, 32)
            for i in range(2):
                if i:
                    act.wait_ge(abs_done, i)
                act.activation(w_abs[:, :], w_raw[:, i, :], ACT.Abs, accum_out=w_sum[:, i:i + 1]).then_inc(abs_done, 1)

            def squares(s):
                for t in range(TT):
                    wait(act, xn_done, s, t + 1)
                    if t:
                        wait(act, x_sq_done, s, t)
                    act.activation(square_work[:, :], xn[:, t, :], ACT.Square,
                                   accum_out=x_sq[:, t:t + 1]).then_inc(x_sq_done.sem, 1)

            squares(0)

            def turn(s, slot, f):
                wait(act, turned, s, f + 1)
                act.activation(xT_hi[:, slot, f, :], ps_turn[:, :], ACT.Copy).then_inc(turn_hi.sem, 1)

            for f in range(FB):
                turn(0, 0, f)

            def step(s, slot, last):
                for k in range(K):
                    wait(act, hid_summed, s, k + 1)
                    wait(act, hid_split, s, k + 1 - RING)
                    wait(act, sq_done, s, k + 1 - RING)
                    act.activation(hid[:, k % RING, :], ps_hid[:, k % PS_RING, :], ACT.Gelu)
                    wait(act, hid_used, s, k + 1 - RING)
                    act.activation(hid_hi[:, k % RING, :], ps_hid[:, k % PS_RING, :], ACT.Gelu).then_inc(hid_act.sem, 1)
                    if k == 3 and not last:
                        squares(s + 1)
                    for f in range(FB):
                        if k == TAKE_AT[f] and not last:
                            turn(s + 1, 1 - slot, f)

            over_sequences(act, step)

        @block.vector
        def _(dve):
            give_credits(dve, [turn_lo, hid_split, out_done, h_ms_done])
            dve.wait_ge(total_done, 1)
            dve.tensor_scalar(limit[:, :], ps_sq[:, 0:2], 0.5 / (F * D), None, ALU.mult).then_inc(limit_done, 1)
            dve.tensor_scalar(minus_limit[:, :], ps_sq[:, 0:2], -0.5 / (F * D), None, ALU.mult).then_inc(limit_done, 1)
            dve.wait_ge(limit_done, 2)
            for i, w in enumerate((w_up, w_down)):
                dve.tensor_scalar(below[:, i, :], w_raw[:, i, :], minus_limit[:, i:i + 1], None,
                                  ALU.is_lt).then_inc(below_done, 1)
                dve.wait_ge(below_done, i + 1)
                dve.scalar_tensor_tensor(out=w[:, :, :].rearrange("p a b -> p (a b)"), in0=w_raw[:, i, :],
                                         scalar=limit[:, i:i + 1], in1=below[:, i, :], op0=ALU.is_gt,
                                         op1=ALU.subtract).then_inc(w_ready, 1)

            def norm_part(s, slot, n):
                if n == 0:
                    x_loads.wait(dve, s, slot)
                    for t in range(TT):
                        dve.bn_stats(stats[:, t, :], x[:, slot, t, :]).then_inc(stats_done.sem, 1)
                    wait_alone(dve, alone, stats_done.sem, stats_done.at(s, TT))
                    for t in range(TT):
                        dve.bn_aggr(moments[:, t, :], stats[:, t, :]).then_inc(moments_done.sem, 1)
                if n == 1:
                    wait(dve, rstd_done, s, 1)
                    for t in range(TT):
                        dve.tensor_scalar(xn[:, t, :], x[:, slot, t, :], moments[:, t, 0:1], rstd[:, t:t + 1],
                                          ALU.subtract, ALU.mult).then_inc(xn_done.sem, 1)
                if n == 2:
                    wait(dve, x_rms_done, s, 1)
                    dve.tensor_scalar(x_rms_eps[:, :], x_rms[:, :], RMS_EPS, None, ALU.add).then_inc(x_scale_part.sem, 1)
                    wait(dve, x_scale_part, s, 1)
                    dve.reciprocal(x_scale[:, :], x_rms_eps[:, :]).then_inc(x_scale_part.sem, 1)
                    wait(dve, x_scale_part, s, 2)
                    for t in range(TT):
                        dve.tensor_scalar(xr[:, t, :], xn[:, t, :], x_scale[:, t:t + 1], None,
                                          ALU.mult).then_inc(xr_done.sem, 1)

            def turn(s, slot, f):
                wait(dve, turn_hi, s, f + 1)
                dve.tensor_tensor(xT_lo[:, slot, f, :], ps_turn[:, :], xT_hi[:, slot, f, :],
                                  ALU.subtract).then_inc(turn_lo.sem, 1)

            for n in range(len(NORM_WITH)):
                norm_part(0, 0, n)
            for f in range(FB):
                turn(0, 0, f)

            def step(s, slot, last):
                for k in range(K):
                    wait(dve, hid_act, s, k + 1)
                    dve.tensor_tensor(hid_lo[:, k % RING, :], hid[:, k % RING, :], hid_hi[:, k % RING, :],
                                      ALU.subtract).then_inc(hid_split.sem, 1)
                    if k in NORM_WITH and not last:
                        norm_part(s + 1, 1 - slot, NORM_WITH.index(k))
                    for f in range(FB):
                        if k == TAKE_AT[f] and not last:
                            turn(s + 1, 1 - slot, f)
                wait(dve, sq_summed, s, K)
                dve.tensor_scalar(h_ms[:, :], ps_sq[:, 0:TT], 1.0 / F, None, ALU.mult).then_inc(h_ms_done.sem, 1)
                wait(dve, h_rms_done, s, 1)
                dve.tensor_scalar(h_rms_eps[:, :], h_rms[:, :], RMS_EPS, None, ALU.add).then_inc(h_scale_part.sem, 1)
                wait(dve, h_scale_part, s, 1)
                dve.reciprocal(h_scale[:, :], h_rms_eps[:, :]).then_inc(h_scale_part.sem, 1)
                wait(dve, h_scale_part, s, 2)
                wait(dve, hid_used, s, K)
                wait(dve, y_stored, s, -1)
                for t in range(TT):
                    dve.scalar_tensor_tensor(out=y[:, slot, t, :], in0=ps_out[:, slot, t, :], scalar=h_scale[:, t:t + 1],
                                             in1=x[:, slot, t, :], op0=ALU.mult, op1=ALU.add).then_inc(out_done.sem, 1)

            over_sequences(dve, step)

        @block.tensor
        def _(pe):
            give_credits(pe, [hid_used, sq_summed])
            pe.wait_ge(consts_in, 16)
            pe.wait_ge(filled, 3)
            pe.wait_ge(abs_done, 2)
            pe.matmul(ps_sq[:, 0:2], ones[:, :], w_sum[:, :], start=True, stop=True).then_inc(total_done, 1)

            def turn(s, f):
                wait(pe, xr_done, s, TT)
                wait(pe, turn_lo, s, f)
                for t in range(TT):
                    last = pe.transpose(ps_turn[:, t * P:(t + 1) * P], xr[:, t, f * P:(f + 1) * P], ident[:, :])
                last.then_inc(turned.sem, 1)

            for f in range(FB):
                turn(0, f)
            pe.wait_ge(w_ready, 2)

            def up(s, slot, k):
                wait(pe, hid_act, s, k + 1 - PS_RING)
                for f in range(FB):
                    w = w_up[:, f, k * P:(k + 1) * P]
                    pe.matmul(ps_hid[:, k % PS_RING, :], w, xT_hi[:, slot, f, :], start=(f == 0), stop=False)
                    mm = pe.matmul(ps_hid[:, k % PS_RING, :], w, xT_lo[:, slot, f, :], start=False, stop=(f == FB - 1))
                mm.then_inc(hid_summed.sem, 1)

            def down(s, slot, k):
                wait(pe, hid_split, s, k + 1)
                if k == 0:
                    wait(pe, out_done, s, -TT)
                for t in range(TT):
                    tok = slice(t * P, (t + 1) * P)
                    pe.matmul(ps_out[:, slot, t, :], hid_hi[:, k % RING, tok], w_down[:, k, :],
                              start=(k == 0 and t % 2 == 0), stop=False, skip_group_check=True)
                    mm = pe.matmul(ps_out[:, slot, t, :], hid_lo[:, k % RING, tok], w_down[:, k, :],
                                   start=False, stop=(k == K - 1), skip_group_check=True)
                mm.then_inc(hid_used.sem, 1)

            def squares(s, k):
                wait(pe, sq_done, s, k + 1)
                if k == 0:
                    wait(pe, h_ms_done, s, 0)
                for t in range(TT):
                    mm = pe.matmul(ps_sq[:, t:t + 1], hid_sq[:, k % RING, t * P:(t + 1) * P], ones[:, 0:1],
                                   start=(k == 0 and t == 0), stop=(k == K - 1), skip_group_check=True)
                mm.then_inc(sq_summed.sem, 1)

            def step(s, slot, last):
                wait(pe, turn_lo, s, FB)
                for k in range(LOOKAHEAD):
                    up(s, slot, k)
                for k in range(K):
                    if k + LOOKAHEAD < K:
                        up(s, slot, k + LOOKAHEAD)
                    if k:
                        squares(s, k - 1)
                    down(s, slot, k)
                    if k in TURN_AT and not last:
                        turn(s + 1, TURN_AT.index(k))
                squares(s, K - 1)

            over_sequences(pe, step)


def mamba_phase(nc, ident_dram, triangles_dram, x_in, in_proj_t, conv_cols, conv_b_col, a_log, dt_w_t, dt_b,
                b_w_t, c_w_t, d_skip, ln_cols, out_proj_t, x_out):
    DI = b_w_t.shape[0]
    H = a_log.shape[0]
    HD = DI // H
    IB = DI // P
    CONV = conv_cols.shape[1] // IB
    PAD = CONV - 1
    HALF = H // 2
    HALVES = 2 * TT
    PIECE = 1024
    assert HD * 2 == P and HALF * P == SEQ

    with ExitStack() as ctx:
        def sb(name, shape, dt=F32):
            return ctx.enter_context(nc.sbuf_tensor("ssm_" + name, shape, dt))

        def psum(name, shape):
            return ctx.enter_context(nc.psum_tensor("ssm_" + name, shape, F32))

        def sem(name):
            return nc.alloc_semaphore(name="ssm_" + name)

        def signal(name, per_seq, credit=0, unit=1):
            return Signal(ctx, nc, "ssm_" + name, per_seq, credit, unit)

        in_hi, in_lo = sb("in_hi", [P, FB, 2 * DI], F32R), sb("in_lo", [P, FB, 2 * DI], F32R)
        bw_hi, bw_lo = sb("bw_hi", [P, IB, DI], F32R), sb("bw_lo", [P, IB, DI], F32R)
        cw_hi, cw_lo = sb("cw_hi", [P, IB, DI], F32R), sb("cw_lo", [P, IB, DI], F32R)
        ow_hi, ow_lo = sb("ow_hi", [P, IB, D], F32R), sb("ow_lo", [P, IB, D], F32R)
        ident = sb("ident", [P, P])
        triangles = sb("triangles", [P, 4, P])
        ident16 = sb("ident16", [P, P], mybir.dt.bfloat16)
        masked16 = sb("masked16", [P, HALF, P], mybir.dt.bfloat16)
        conv_w = sb("conv_w", [P, IB, CONV])
        conv_b = sb("conv_b", [P, IB])
        dt_w = sb("dt_w", [P, IB, H])
        dt_bias = sb("dt_bias", [P, H])
        a_logs = sb("a_logs", [P, H])
        a_exp = sb("a_exp", [P, H])
        a_neg = sb("a_neg", [P, H])
        d_all = sb("d_all", [P, H])
        ln_w = sb("ln_w", [P, 2, IB])

        x = sb("x", [P, 2, TT, D])
        stats = sb("stats", [P, TT, 6])
        moments = sb("moments", [P, TT, 2])
        var_eps = sb("var_eps", [P, TT])
        minus_half = sb("minus_half", [P, TT])
        rstd = sb("rstd", [P, TT])
        xn = sb("xn", [P, TT, D])
        xT_hi, xT_lo = sb("xT_hi", [P, FB, SEQ], F32R), sb("xT_lo", [P, FB, SEQ], F32R)
        u_pad = sb("u_pad", [P, IB, PAD + SEQ])
        u = sb("u", [P, IB, SEQ])
        u_hi, u_lo = sb("u_hi", [P, IB, SEQ], F32R), sb("u_lo", [P, IB, SEQ], F32R)
        z = sb("z", [P, IB, SEQ])
        bT = sb("bT", [P, IB, SEQ])
        cT = sb("cT", [P, 2, IB, SEQ])
        b_tok, u_tok, u_dt = sb("b_tok", [P, TT, DI]), sb("u_tok", [P, TT, DI]), sb("u_dt", [P, TT, DI])
        stage = b_tok[:, :, :].rearrange("p (i t) d -> p i (t d)", i=2)
        dt_raw = sb("dt_raw", [P, TT, H])
        dt_abs = sb("dt_abs", [P, TT, H])
        dt_exp = sb("dt_exp", [P, TT, H])
        dt_log = sb("dt_log", [P, TT, H])
        dt = sb("dt", [P, TT, H])
        a = sb("a", [P, TT, H])
        sums = sb("sums", [P, 2, TT, H])
        to_end = sb("to_end", [P, TT, H])
        decays = sb("decays", [P, 2, TT, H])
        decay_end = sb("decay_end", [P, TT, H])
        decay_state = sb("decay_state", [P, TT, H // 2])
        a_tri = sb("a_tri", [P, 2, HALF, P])
        decay = sb("decay", [P, 2, HALF, P])
        scores = sb("scores", [P, 2, HALF, P])
        u_end = sb("u_end", [P, DI])
        state = sb("state", [P, H // 2, HD])
        state_old = sb("state_old", [P, H // 2, HD])
        y_old = sb("y_old", [P, DI])
        y_sum = sb("y_sum", [P, DI])
        y_stats = sb("y_stats", [P, TT, 6])
        y_moments = sb("y_moments", [P, TT, 2])
        y_var_eps = sb("y_var_eps", [P, TT])
        y_rstd = sb("y_rstd", [P, TT])
        g_hi, g_lo = sb("g_hi", [P, IB, SEQ], F32R), sb("g_lo", [P, IB, SEQ], F32R)

        ps = psum("ps", [P, 2, SEQ])
        ps_decay = psum("ps_decay", [P, 2, HALF, P])
        ps_scores = psum("ps_scores", [P, HALF, P])
        ps_y = psum("ps_y", [P, DI])
        ps_y_old = psum("ps_y_old", [P, DI])
        ps_small = psum("ps_small", [P, 512])
        ps_state = ps_small[:, 0:H // 2 * HD].rearrange("p (q d) -> p q d", d=HD)
        ps_dt = ps_small[:, 256:256 + TT * H].rearrange("p (t h) -> p t h", h=H)
        ps_sums = ps_small[:, 320:320 + 2 * TT * H].rearrange("p (k t h) -> p k t h", k=2, h=H)

        def uses(name, n, reader):
            return [(f"{name}{i}", reader) for i in range(n)]

        ahead = uses("turn", FB, "dve")
        own = (uses("z", IB, "act") + uses("b", IB, "act") + uses("c", IB, "dve") + uses("u_tok", TT, "act")
               + uses("b_tok", TT, "act"))
        tail = uses("y", IB, "act") + uses("out", TT // 2, "dve")
        ring = Ring(ctx, nc, "ssm_ps", 2, ahead + uses("u", IB, "act"),
                    own + ahead + uses("u", IB, "act") + tail, own + tail)

        consts_in, filled = sem("consts_in"), sem("filled")
        stage_in = [sem(f"stage_in{i}") for i in range(2)]
        stage_hi, stage_lo = sem("stage_hi"), sem("stage_lo")
        a_exp_done, consts_made = sem("a_exp_done"), sem("consts_made")
        x_in_sem = signal("x_in", 1, unit=16)
        x_stored = signal("x_stored", 1, credit=2, unit=16)
        alone, alone_pool = sem("waits_of_dve"), sem("waits_of_pool")
        stats_done = signal("stats_done", TT)
        moments_done = signal("moments_done", TT)
        eps_added = signal("eps_added", 1)
        rstd_done = signal("rstd_done", 1)
        xn_done = signal("xn_done", TT)
        turn_hi = signal("turn_hi", FB)
        conv_part = signal("conv_part", IB * CONV)
        u_done = signal("u_done", IB)
        u_split = signal("u_split", IB)
        dt_summed = signal("dt_summed", 1)
        dt_raw_done = signal("dt_raw_done", 1)
        softplus_part = signal("softplus_part", 3)
        dt_done = signal("dt_done", 1)
        a_done = signal("a_done", 1)
        sums_summed = signal("sums_summed", 1)
        sums_done = signal("sums_done", 2)
        decays_done = signal("decays_done", 2)
        decay_state_done = signal("decay_state_done", 2)
        u_dt_done = signal("u_dt_done", TT)
        skip_done = signal("skip_done", TT)
        a_tri_done = signal("a_tri_done", HALVES)
        u_end_done = signal("u_end_done", TT - 1)
        log_decay_summed = signal("log_decay_summed", HALVES, credit=2)
        decay_done = signal("decay_done", HALVES, credit=2)
        scores_summed = signal("scores_summed", HALVES)
        scores_done = signal("scores_done", HALVES, credit=2)
        y_summed = signal("y_summed", HALVES, credit=2)
        y_old_summed = signal("y_old_summed", TT - 1)
        state_summed = signal("state_summed", TT - 1, credit=1)
        state_decayed = signal("state_decayed", TT - 2)
        state_done = signal("state_done", TT - 1, credit=1)
        y_read = signal("y_read", TT, credit=1)
        y_part = signal("y_part", TT - 1)
        y_done = signal("y_done", TT)
        y_stats_done = signal("y_stats_done", TT)
        y_moments_done = signal("y_moments_done", TT)
        y_eps_added = signal("y_eps_added", 1)
        y_rstd_done = signal("y_rstd_done", 1)
        yn_done = signal("yn_done", TT)
        g_gated = signal("g_gated", IB)
        g_hi_done = signal("g_hi_done", IB)
        g_split = signal("g_split", IB)

        pieces = []
        for f in range(FB):
            pieces.append((in_proj_t.rearrange("(f p) h -> f p h", p=P)[f], in_hi[:, f, :], in_lo[:, f, :]))
        for w, hi, lo, width in ((b_w_t, bw_hi, bw_lo, DI), (c_w_t, cw_hi, cw_lo, DI), (out_proj_t, ow_hi, ow_lo, D)):
            n = PIECE // width
            for c in range(0, IB, n):
                pieces.append((w.rearrange("(k p) d -> p k d", p=P)[:, c:c + n, :], hi[:, c:c + n, :], lo[:, c:c + n, :]))

        def staged(i, dst):
            v = stage[:, i % 2, :]
            return v if len(dst.shape) == 2 else v.rearrange("p (k d) -> p k d", k=dst.shape[1])

        def heads(v):
            return v.rearrange("p (h d) -> p h d", d=HD)

        def per_head(v, n=HD):
            return v.unsqueeze(2).broadcast_to([v.shape[0], v.shape[1], n])

        CONSTS = 9
        block = ctx.enter_context(nc.Block())

        @block.sync
        def _(sp):
            def load_x(s, slot):
                wait(sp, x_stored, s, -1)
                sp.dma_start(x[:, slot], tiles_of(x_in, s)).then_inc(x_in_sem.sem, 16)

            give_credits(sp, [x_stored])
            load_x(0, 0)
            sp.dma_start(ident[:, :], ident_dram).then_inc(consts_in, 16)
            sp.dma_start(triangles[:, :, :], triangles_dram.rearrange("k p t -> p k t")).then_inc(consts_in, 16)
            sp.dma_start(conv_w[:, :, :], conv_cols.rearrange("p (k c) -> p k c", c=CONV)).then_inc(consts_in, 16)
            sp.dma_start(conv_b[:, :], conv_b_col).then_inc(consts_in, 16)
            sp.dma_start(dt_w[:, :, :], dt_w_t.rearrange("(k p) h -> p k h", p=P)).then_inc(consts_in, 16)
            sp.dma_start(dt_bias[:, :], dt_b.partition_broadcast(P)).then_inc(consts_in, 16)
            sp.dma_start(a_logs[:, :], a_log.partition_broadcast(P)).then_inc(consts_in, 16)
            sp.dma_start(d_all[:, :], d_skip.partition_broadcast(P)).then_inc(consts_in, 16)
            sp.dma_start(ln_w[:, :, :], ln_cols.rearrange("p (k c) -> p k c", c=IB)).then_inc(consts_in, 16)
            for i, (src, dst, _) in enumerate(pieces):
                if i >= 2:
                    sp.wait_ge(stage_lo, i - 1)
                sp.dma_start(staged(i, dst), src).then_inc(stage_in[i % 2], 16)

            def step(s, slot, last):
                if not last:
                    load_x(s + 1, 1 - slot)
                wait_read(sp, ring, s, f"out{TT // 2 - 1}", last)
                sp.dma_start(tiles_of(x_out, s), x[:, slot]).then_inc(x_stored.sem, 16)

            over_sequences(sp, step)
            wait(sp, x_stored, SEQS, 0)

        @block.gpsimd
        def _(pool):
            pool.memset(minus_half[:, :], -0.5).then_inc(filled, 1)
            pool.memset(u_pad[:, :, 0:PAD], 0.0).then_inc(filled, 1)
            pool.wait_ge(filled, 2)
            pool.wait_ge(consts_in, 16 * CONSTS)

            def rsqrt(s, moments_sem, var, sum_, sum_sem, out, out_sem):
                wait_alone(pool, alone_pool, moments_sem.sem, moments_sem.at(s, TT))
                pool.tensor_scalar(sum_[:, :], var, LN_EPS, None, ALU.add).then_inc(sum_sem.sem, 1)
                wait(pool, sum_sem, s, 1)
                pool.tensor_tensor(out[:, :], sum_[:, :], minus_half[:, :], ALU.pow).then_inc(out_sem.sem, 1)

            def norm(s):
                rsqrt(s, moments_done, moments[:, :, 1], var_eps, eps_added, rstd, rstd_done)

            norm(0)

            def step(s, slot, last):
                if not last:
                    norm(s + 1)
                wait(pool, a_done, s, 1)
                for i in range(HALVES):
                    c, h = i // 2, i % 2 * HALF
                    wait(pool, log_decay_summed, s, i - 1)
                    pool.tensor_tensor(a_tri[:, i % 2], triangles[:, 0, :].unsqueeze(1).broadcast_to([P, HALF, P]),
                                       per_head(a[:, c, h:h + HALF], P), ALU.mult).then_inc(a_tri_done.sem, 1)
                    if h and c:
                        wait(pool, decays_done, s, 2)
                        wait(pool, state_summed, s, c - 1)
                        pool.tensor_tensor(heads(u_end[:, :]), heads(u_dt[:, c - 1, :]), per_head(decay_end[:, c - 1, :]),
                                           ALU.mult).then_inc(u_end_done.sem, 1)
                    if h:
                        wait(pool, u_dt_done, s, c + 1)
                        pool.tensor_tensor(heads(u_tok[:, c, :]), heads(u_tok[:, c, :]), per_head(d_all[:, :]),
                                           ALU.mult).then_inc(skip_done.sem, 1)
                rsqrt(s, y_moments_done, y_moments[:, :, 1], y_var_eps, y_eps_added, y_rstd, y_rstd_done)

            over_sequences(pool, step)

        @block.scalar
        def _(act):
            for i, (_, hi, _) in enumerate(pieces):
                act.wait_ge(stage_in[i % 2], 16 * (i // 2 + 1))
                act.activation(hi, staged(i, hi), ACT.Copy).then_inc(stage_hi, 1)
            act.wait_ge(consts_in, 16 * CONSTS)
            act.activation(a_exp[:, :], a_logs[:, :], ACT.Exp).then_inc(a_exp_done, 1)
            give_credits(act, [decay_done])

            def turn(s):
                for f in range(FB):
                    wait_filled(act, ring, s, f"turn{f}", False)
                    act.activation(xT_hi[:, f, :], ps[:, ring.bank(s, f"turn{f}", False), :],
                                   ACT.Copy).then_inc(turn_hi.sem, 1)

            def pad_in(s):
                for m in range(IB):
                    wait_filled(act, ring, s, f"u{m}", False)
                    if s is not None:
                        wait(act, conv_part, s, (m + 1) * CONV)
                    act.activation(u_pad[:, m, PAD:], ps[:, ring.bank(s, f"u{m}", False), :],
                                   ACT.Copy).then_inc(ring.free["act"], 1)

            def silu(s, m):
                wait(act, conv_part, 0 if s is None else s + 1, (m + 1) * CONV)
                act.activation(u_hi[:, m, :], u[:, m, :], ACT.Silu)
                act.activation(u[:, m, :], u[:, m, :], ACT.Silu).then_inc(u_done.sem, 1)

            turn(None)
            pad_in(None)
            for m in range(IB):
                silu(None, m)

            def step(s, slot, last):
                def take(use, out, func, **more):
                    wait_filled(act, ring, s, use, last)
                    act.activation(out, ps[:, ring.bank(s, use, last), :], func, **more).then_inc(ring.free["act"], 1)

                for m in range(IB):
                    take(f"z{m}", z[:, m, :], ACT.Silu)
                wait(act, dt_raw_done, s, 1)
                act.activation(dt_abs[:, :, :], dt_raw[:, :, :], ACT.Abs).then_inc(softplus_part.sem, 1)
                wait(act, softplus_part, s, 1)
                act.activation(dt_exp[:, :, :], dt_abs[:, :, :], ACT.Exp, scale=-1.0).then_inc(softplus_part.sem, 1)
                wait(act, softplus_part, s, 2)
                act.activation(dt_log[:, :, :], dt_exp[:, :, :], ACT.Ln, bias=1.0).then_inc(softplus_part.sem, 1)
                for m in range(IB):
                    take(f"b{m}", bT[:, m, :], ACT.Copy)
                wait(act, sums_done, s, 1)
                act.activation(decays[:, :, :, :], sums[:, :, :, :], ACT.Exp).then_inc(decays_done.sem, 1)
                wait(act, sums_done, s, 2)
                act.activation(decay_end[:, :, :], to_end[:, :, :], ACT.Exp).then_inc(decays_done.sem, 1)
                for c in range(TT):
                    take(f"u_tok{c}", u_tok[:, c, :], ACT.Copy)
                for c in range(TT):
                    take(f"b_tok{c}", b_tok[:, c, :], ACT.Copy)
                if not last:
                    turn(s)
                for i in range(HALVES):
                    wait(act, log_decay_summed, s, i + 1)
                    wait(act, scores_done, s, i - 1)
                    act.activation(decay[:, i % 2], ps_decay[:, i % 2], ACT.Exp).then_inc(decay_done.sem, 1)
                if not last:
                    pad_in(s)
                for f in range(IB):
                    if not last:
                        silu(s, f)
                    take(f"y{f}", bT[:, f, :], ACT.Identity, bias=ln_w[:, 1, f:f + 1], scale=ln_w[:, 0, f:f + 1])

            over_sequences(act, step)

        @block.vector
        def _(dve):
            for i, (_, hi, lo) in enumerate(pieces):
                dve.wait_ge(stage_hi, i + 1)
                dve.tensor_tensor(lo, staged(i, lo), hi, ALU.subtract).then_inc(stage_lo, 1)
            dve.wait_ge(consts_in, 16 * CONSTS)
            dve.wait_ge(a_exp_done, 1)
            dve.tensor_scalar(a_neg[:, :], a_exp[:, :], -1.0, None, ALU.mult).then_inc(consts_made, 1)
            dve.tensor_copy(ident16[:, :], ident[:, :]).then_inc(consts_made, 1)
            dve.tensor_copy(masked16[:, :, :],
                            triangles[:, 3, :].unsqueeze(1).broadcast_to([P, HALF, P])).then_inc(consts_made, 1)
            dve.wait_ge(consts_made, 3)
            dve.wait_ge(filled, 2)
            for r in range(2):
                dve.memset(cT[(1 - r) * HD:(2 - r) * HD, r], 0.0)
            give_credits(dve, [scores_done, state_done, y_read])

            def norm_stats(s, slot):
                wait(dve, x_in_sem, s, 1)
                for t in range(TT):
                    dve.bn_stats(stats[:, t, :], x[:, slot, t, :]).then_inc(stats_done.sem, 1)
                wait_alone(dve, alone, stats_done.sem, stats_done.at(s, TT))
                for t in range(TT):
                    dve.bn_aggr(moments[:, t, :], stats[:, t, :]).then_inc(moments_done.sem, 1)

            def norm_apply(s, slot):
                wait(dve, rstd_done, s, 1)
                for t in range(TT):
                    dve.tensor_scalar(xn[:, t, :], x[:, slot, t, :], moments[:, t, 0:1], rstd[:, t:t + 1],
                                      ALU.subtract, ALU.mult).then_inc(xn_done.sem, 1)

            def turn(s):
                for f in range(FB):
                    wait(dve, turn_hi, 0 if s is None else s + 1, f + 1)
                    dve.tensor_tensor(xT_lo[:, f, :], ps[:, ring.bank(s, f"turn{f}", False), :], xT_hi[:, f, :],
                                      ALU.subtract).then_inc(ring.free["dve"], 1)

            def conv(s, m):
                n = 0 if s is None else s + 1
                wait_read(dve, ring, s, f"u{m}", False)
                dve.tensor_scalar(u[:, m, :], u_pad[:, m, 0:SEQ], conv_w[:, m, 0:1], conv_b[:, m:m + 1],
                                  ALU.mult, ALU.add).then_inc(conv_part.sem, 1)
                for tap in range(1, CONV):
                    wait(dve, conv_part, n, m * CONV + tap)
                    dve.scalar_tensor_tensor(out=u[:, m, :], in0=u_pad[:, m, tap:tap + SEQ], scalar=conv_w[:, m, tap:tap + 1],
                                             in1=u[:, m, :], op0=ALU.mult, op1=ALU.add).then_inc(conv_part.sem, 1)

            def u_low(s, m):
                wait(dve, u_done, 0 if s is None else s + 1, m + 1)
                dve.tensor_tensor(u_lo[:, m, :], u[:, m, :], u_hi[:, m, :], ALU.subtract).then_inc(u_split.sem, 1)

            norm_stats(0, 0)
            norm_apply(0, 0)
            turn(None)
            for m in range(IB):
                conv(None, m)
            for m in range(IB):
                u_low(None, m)

            def step(s, slot, last):
                wait(dve, dt_summed, s, 1)
                dve.tensor_tensor(dt_raw[:, :, :], ps_dt, dt_bias[:, :].unsqueeze(1).broadcast_to([P, TT, H]),
                                  ALU.add).then_inc(dt_raw_done.sem, 1)
                if not last:
                    norm_stats(s + 1, 1 - slot)
                wait(dve, softplus_part, s, 3)
                dve.scalar_tensor_tensor(out=dt[:, :, :], in0=dt_raw[:, :, :], scalar=0.0, in1=dt_log[:, :, :],
                                         op0=ALU.max, op1=ALU.add).then_inc(dt_done.sem, 1)
                wait(dve, dt_done, s, 1)
                dve.tensor_tensor(a[:, :, :], dt[:, :, :], a_neg[:, :].unsqueeze(1).broadcast_to([P, TT, H]),
                                  ALU.mult).then_inc(a_done.sem, 1)
                if not last:
                    norm_apply(s + 1, 1 - slot)
                wait(dve, sums_summed, s, 1)
                dve.tensor_copy(sums[:, :, :, :], ps_sums).then_inc(sums_done.sem, 1)
                wait(dve, sums_done, s, 1)
                dve.tensor_tensor(to_end[:, :, :], sums[:, 1], sums[:, 0], ALU.subtract).then_inc(sums_done.sem, 1)
                for m in range(IB):
                    wait_filled(dve, ring, s, f"c{m}", last)
                    bank = ps[:, ring.bank(s, f"c{m}", last), :]
                    dve.tensor_copy(cT[0:HD, 0, m, :], bank[0:HD, :])
                    dve.tensor_copy(cT[HD:P, 1, m, :], bank[HD:P, :]).then_inc(ring.free["dve"], 1)
                wait(dve, decays_done, s, 1)
                for r in range(2):
                    part = slice(r * HD, (r + 1) * HD)
                    by_pair = decays[part, 1].rearrange("p t (q r) -> p t q r", r=2)
                    dve.tensor_copy(decay_state[part, :, :], by_pair[:, :, :, r]).then_inc(decay_state_done.sem, 1)
                for c in range(TT):
                    wait_read(dve, ring, s, f"u_tok{c}", last)
                    dve.tensor_tensor(heads(u_dt[:, c, :]), heads(u_tok[:, c, :]), per_head(dt[:, c, :]),
                                      ALU.mult).then_inc(u_dt_done.sem, 1)
                if not last:
                    turn(s)
                wait(dve, decay_state_done, s, 2)

                def scores_of(i):
                    wait(dve, scores_summed, s, i + 1)
                    wait(dve, decay_done, s, i + 1)
                    wait(dve, y_summed, s, i - 1)
                    dve.tensor_tensor(scores[:, i % 2], decay[:, i % 2], ps_scores[:, :, :],
                                      ALU.mult).then_inc(scores_done.sem, 1)

                def update_state(c):
                    if c:
                        dve.tensor_tensor(state_old[:, :, :], state[:, :, :], per_head(decay_state[:, c, :]),
                                          ALU.mult).then_inc(state_decayed.sem, 1)
                        wait(dve, state_decayed, s, c)
                    wait(dve, state_summed, s, c + 1)
                    if c:
                        dve.tensor_tensor(state[:, :, :], ps_state, state_old[:, :, :], ALU.add).then_inc(state_done.sem, 1)
                    else:
                        dve.tensor_copy(state[:, :, :], ps_state).then_inc(state_done.sem, 1)

                def combine(c):
                    wait(dve, y_summed, s, 2 * c + 2)
                    if c:
                        wait(dve, y_old_summed, s, c)
                        dve.tensor_tensor(heads(y_old[:, :]), heads(ps_y_old[:, :]), per_head(decays[:, 0, c, :]),
                                          ALU.mult).then_inc(y_part.sem, 1)
                        wait(dve, y_part, s, c)
                        dve.tensor_tensor(y_sum[:, :], ps_y[:, :], y_old[:, :], ALU.add).then_inc(y_read.sem, 1)
                    else:
                        dve.tensor_copy(y_sum[:, :], ps_y[:, :]).then_inc(y_read.sem, 1)
                    wait(dve, y_read, s, c + 1)
                    wait(dve, skip_done, s, c + 1)
                    dve.tensor_tensor(u_tok[:, c, :], y_sum[:, :], u_tok[:, c, :], ALU.add).then_inc(y_done.sem, 1)
                    wait(dve, y_done, s, c + 1)
                    dve.bn_stats(y_stats[:, c, :], u_tok[:, c, :]).then_inc(y_stats_done.sem, 1)

                for i in range(HALVES + 1):
                    if i < HALVES:
                        scores_of(i)
                    if i and i % 2 == 0:
                        c = i // 2 - 1
                        if c < TT - 1:
                            update_state(c)
                        combine(c)
                wait_alone(dve, alone, y_stats_done.sem, y_stats_done.at(s, TT))
                for c in range(TT):
                    dve.bn_aggr(y_moments[:, c, :], y_stats[:, c, :]).then_inc(y_moments_done.sem, 1)
                if not last:
                    conv(s, 0)
                wait(dve, y_rstd_done, s, 1)
                for c in range(TT):
                    dve.tensor_scalar(u_tok[:, c, :], u_tok[:, c, :], y_moments[:, c, 0:1], y_rstd[:, c:c + 1],
                                      ALU.subtract, ALU.mult).then_inc(yn_done.sem, 1)
                for f in range(IB):
                    if not last and f + 1 < IB:
                        conv(s, f + 1)
                    if not last:
                        u_low(s, f)
                    wait_read(dve, ring, s, f"y{f}", last)
                    dve.tensor_tensor(bT[:, f, :], bT[:, f, :], z[:, f, :], ALU.mult).then_inc(g_gated.sem, 1)
                    wait(dve, g_gated, s, f + 1)
                    dve.tensor_copy(g_hi[:, f, :], bT[:, f, :]).then_inc(g_hi_done.sem, 1)
                    wait(dve, g_hi_done, s, f + 1)
                    dve.tensor_tensor(g_lo[:, f, :], bT[:, f, :], g_hi[:, f, :], ALU.subtract).then_inc(g_split.sem, 1)
                for pair in range(TT // 2):
                    wait_filled(dve, ring, s, f"out{pair}", last)
                    part = x[:, slot, 2 * pair:2 * pair + 2, :].rearrange("p t d -> p (t d)")
                    dve.tensor_tensor(part, ps[:, ring.bank(s, f"out{pair}", last), :], part,
                                      ALU.add).then_inc(ring.free["dve"], 1)

            over_sequences(dve, step)

        @block.tensor
        def _(pe):
            pe.wait_ge(consts_in, 16 * CONSTS)
            give_credits(pe, [log_decay_summed, y_summed, state_summed])

            def turn(s):
                wait(pe, xn_done, 0 if s is None else s + 1, TT)
                for f in range(FB):
                    wait_free(pe, ring, s, f"turn{f}", False)
                    for t in range(TT):
                        last = pe.transpose(ps[:, ring.bank(s, f"turn{f}", False), t * P:(t + 1) * P],
                                            xn[:, t, f * P:(f + 1) * P], ident[:, :])
                    last.then_inc(ring.full, 1)

            def in_product(s, use, m, last):
                wait_free(pe, ring, s, use, last)
                for f in range(FB):
                    w = slice(m * P, (m + 1) * P)
                    mm = split_product(pe, ps[:, ring.bank(s, use, last), :], in_hi[:, f, w], in_lo[:, f, w],
                                       xT_hi[:, f, :], xT_lo[:, f, :], f == 0, f == FB - 1)
                mm.then_inc(ring.full, 1)

            def u_tiles(s):
                wait_read(pe, ring, s, f"turn{FB - 1}", False)
                for m in range(IB):
                    in_product(s, f"u{m}", m, False)

            turn(None)
            pe.wait_ge(stage_lo, len(pieces))
            pe.wait_ge(consts_made, 3)
            u_tiles(None)

            def step(s, slot, last):
                for m in range(IB):
                    in_product(s, f"z{m}", IB + m, last)

                wait(pe, u_done, s, IB)
                wait(pe, state_done, s, 0)
                for t in range(TT):
                    for k in range(IB):
                        mm = pe.matmul(ps_dt[:, t, :], u[:, k, t * P:(t + 1) * P], dt_w[:, k, :],
                                       start=(k == 0), stop=(k == IB - 1))
                mm.then_inc(dt_summed.sem, 1)

                wait(pe, u_split, s, IB)
                for name, hi, lo in (("b", bw_hi, bw_lo), ("c", cw_hi, cw_lo)):
                    for m in range(IB):
                        use = f"{name}{m}"
                        wait_free(pe, ring, s, use, last)
                        w = slice(m * P, (m + 1) * P)
                        for k in range(IB):
                            mm = split_product(pe, ps[:, ring.bank(s, use, last), :], hi[:, k, w], lo[:, k, w],
                                               u_hi[:, k, :], u_lo[:, k, :], k == 0, k == IB - 1)
                        mm.then_inc(ring.full, 1)
                    if name == "b":
                        wait(pe, a_done, s, 1)
                        for kind, w in enumerate((0, 2)):
                            mm = pe.matmul(ps_sums[:, kind].rearrange("p t h -> p (t h)"), triangles[:, w, :],
                                           a[:, :, :].rearrange("p t h -> p (t h)"), start=True, stop=True)
                        mm.then_inc(sums_summed.sem, 1)

                for name, source in (("u_tok", u), ("b_tok", bT)):
                    if name == "b_tok":
                        wait_read(pe, ring, s, f"b{IB - 1}", last)
                    for c in range(TT):
                        use = f"{name}{c}"
                        wait_free(pe, ring, s, use, last)
                        for k in range(IB):
                            mm = pe.transpose(ps[:, ring.bank(s, use, last), k * P:(k + 1) * P],
                                              source[:, k, c * P:(c + 1) * P], ident[:, :])
                        mm.then_inc(ring.full, 1)
                if not last:
                    turn(s)

                def log_decays(i):
                    wait(pe, a_tri_done, s, i + 1)
                    wait(pe, decay_done, s, i - 1)
                    pe.matmul(ps_decay[:, i % 2], triangles[:, 1, :], a_tri[:, i % 2], start=True, stop=False)
                    pe.matmul(ps_decay[:, i % 2], ident16[:, :], masked16[:, :, :], start=False,
                              stop=True).then_inc(log_decay_summed.sem, 1)

                def rows(head):
                    return slice(head % 2 * HD, head % 2 * HD + HD)

                def b_dot_c(i):
                    c, h = i // 2, i % 2 * HALF
                    wait(pe, scores_done, s, i)
                    for n in range(HALF):
                        r, q, tok = (h + n) % 2, (h + n) // 2, slice(c * P, (c + 1) * P)
                        mm = pe.matmul(ps_scores[:, n, :], bT[:, q, tok], cT[:, r, q, tok], start=True, stop=True)
                    mm.then_inc(scores_summed.sem, 1)

                def y_within(i):
                    c, h = i // 2, i % 2 * HALF
                    wait(pe, scores_done, s, i + 1)
                    if h == 0:
                        wait(pe, u_dt_done, s, c + 1)
                        wait(pe, y_read, s, c)
                    for n in range(HALF):
                        d = slice((h + n) * HD, (h + n + 1) * HD)
                        mm = pe.matmul(ps_y[:, d], scores[:, i % 2, n, :], u_dt[:, c, d], start=True, stop=True)
                    mm.then_inc(y_summed.sem, 1)

                def y_from_state(c):
                    wait(pe, state_done, s, c)
                    wait(pe, y_read, s, c)
                    for head in range(H):
                        mm = pe.matmul(ps_y_old[:, head * HD:(head + 1) * HD], cT[:, head % 2, head // 2, c * P:(c + 1) * P],
                                       state[:, head // 2, :], start=True, stop=True)
                    mm.then_inc(y_old_summed.sem, 1)

                def new_state(c):
                    wait(pe, u_end_done, s, c + 1)
                    wait(pe, state_done, s, c)
                    for head in range(H):
                        d = slice(head * HD, (head + 1) * HD)
                        mm = pe.matmul(ps_state[rows(head), head // 2, :], b_tok[:, c, d], u_end[:, d],
                                       start=True, stop=True)
                    mm.then_inc(state_summed.sem, 1)

                log_decays(0)
                log_decays(1)
                wait_read(pe, ring, s, f"c{IB - 1}", last)
                wait_read(pe, ring, s, f"b_tok{TT - 1}", last)
                for i in range(HALVES + 1):
                    if i < HALVES:
                        b_dot_c(i)
                    if i:
                        y_within(i - 1)
                    if i + 2 < HALVES:
                        log_decays(i + 2)
                    if i and i % 2 == 0:
                        c = i // 2 - 1
                        if c:
                            y_from_state(c)
                        if c < TT - 1:
                            new_state(c)
                if not last:
                    u_tiles(s)
                wait(pe, yn_done, s, TT)
                for f in range(IB):
                    wait_free(pe, ring, s, f"y{f}", last)
                    for c in range(TT):
                        mm = pe.transpose(ps[:, ring.bank(s, f"y{f}", last), c * P:(c + 1) * P],
                                          u_tok[:, c, f * P:(f + 1) * P], ident[:, :])
                    mm.then_inc(ring.full, 1)
                wait(pe, g_split, s, IB)
                for pair in range(TT // 2):
                    use = f"out{pair}"
                    wait_free(pe, ring, s, use, last)
                    for t in range(2):
                        tok = slice((2 * pair + t) * P, (2 * pair + t + 1) * P)
                        for k in range(IB):
                            mm = split_product(pe, ps[:, ring.bank(s, use, last), t * D:(t + 1) * D], g_hi[:, k, tok],
                                               g_lo[:, k, tok], ow_hi[:, k, :], ow_lo[:, k, :],
                                               k == 0, k == IB - 1)
                    mm.then_inc(ring.full, 1)

            over_sequences(pe, step)


def moe_phase(nc, ident_dram, x_in, gate_w, w1, b1_cols, w2, b2, sw1, sw2, sb2, x_out):
    HIDDEN = w1.shape[2]
    KT = HIDDEN // P
    BRANCHES = 3
    K = BRANCHES * KT
    GROUPS = BRANCHES * FB
    TURN_AT = [11 + 2 * g for g in range(GROUPS)]
    NORM_AT, NORM_PARTS = 4, TT + 5
    STAGE = 1024
    CONSTS = 7

    with ExitStack() as ctx:
        def sb(name, shape, dt=F32):
            return ctx.enter_context(nc.sbuf_tensor(name, shape, dt))

        def psum(name, shape):
            return ctx.enter_context(nc.psum_tensor(name, shape, F32))

        def signal(name, per_seq, credit=0, unit=1):
            return Signal(ctx, nc, name, per_seq, credit, unit)

        w1_hi, w1_lo = sb("moe_w1_hi", [P, BRANCHES, FB, HIDDEN], F32R), sb("moe_w1_lo", [P, BRANCHES, FB, HIDDEN], F32R)
        w2_hi, w2_lo = sb("moe_w2_hi", [P, BRANCHES, KT, D], F32R), sb("moe_w2_lo", [P, BRANCHES, KT, D], F32R)
        b1_col = sb("moe_b1_col", [P, BRANCHES, KT])
        b2_all = sb("moe_b2_all", [P, 3, D])
        b2_sum = sb("moe_b2_sum", [P, D])
        gates = sb("moe_gates", [P, 2, D])
        ident = sb("moe_ident", [P, P])
        stage = sb("moe_stage", [P, 2, STAGE])
        x = sb("moe_x", [P, 2, TT, D])
        stats = sb("moe_stats", [P, TT, 6])
        moments = sb("moe_moments", [P, TT, 2])
        var_eps = sb("moe_var_eps", [P, TT])
        minus_half = sb("moe_minus_half", [P, TT])
        rstd = sb("moe_rstd", [P, TT])
        score = sb("moe_score", [P, 2, TT])
        score_work = sb("moe_score_work", [P, D])
        mask = sb("moe_mask", [P, 2, TT])
        xn = sb("moe_xn", [P, BRANCHES, TT, D])
        xT_hi = sb("moe_xT_hi", [P, 2, BRANCHES, FB, SEQ], F32R)
        xT_lo = sb("moe_xT_lo", [P, 2, BRANCHES, FB, SEQ], F32R)
        hid = sb("moe_hid", [P, RING, SEQ])
        hid_hi = sb("moe_hid_hi", [P, RING, SEQ], F32R)
        hid_lo = sb("moe_hid_lo", [P, RING, SEQ], F32R)

        ps_hid = psum("moe_ps_hid", [P, RING, SEQ])
        ps_out = psum("moe_ps_out", [P, 2, TT, D])
        ps_turn = psum("moe_ps_turn", [P, SEQ])

        consts_in = nc.alloc_semaphore(name="moe_consts_in")
        stage_in = [nc.alloc_semaphore(name=f"moe_stage_in{i}") for i in range(2)]
        stage_hi = nc.alloc_semaphore(name="moe_stage_hi")
        stage_lo = nc.alloc_semaphore(name="moe_stage_lo")
        b2_part = nc.alloc_semaphore(name="moe_b2_part")
        b2_ready = nc.alloc_semaphore(name="moe_b2_ready")
        half_set = nc.alloc_semaphore(name="moe_half_set")
        x_in_sem = signal("moe_x_in", 1, unit=16)
        x_stored = signal("moe_x_stored", 1, credit=2, unit=16)
        alone, alone_pool = nc.alloc_semaphore(name="moe_waits_of_dve"), nc.alloc_semaphore(name="moe_waits_of_pool")
        stats_done = signal("moe_stats_done", TT)
        moments_done = signal("moe_moments_done", TT)
        eps_added = signal("moe_eps_added", 1)
        rstd_done = signal("moe_rstd_done", 1)
        xn_done = signal("moe_xn_done", TT)
        score_done = signal("moe_score_done", 2 * TT)
        mask_done = signal("moe_mask_done", 2)
        masked_done = signal("moe_masked_done", 2 * TT)
        bias_added = signal("moe_bias_added", 1)
        turned = signal("moe_turned", GROUPS)
        turn_hi = signal("moe_turn_hi", GROUPS)
        turn_lo = signal("moe_turn_lo", GROUPS, credit=1)
        hid_summed = signal("moe_hid_summed", K)
        hid_act = signal("moe_hid_act", K, credit=RING)
        hid_split = signal("moe_hid_split", K, credit=RING)
        hid_used = signal("moe_hid_used", K, credit=RING)
        out_done = signal("moe_out_done", TT // 2, credit=2 * TT // 2)

        pieces = []
        for b, w in enumerate((sw1, w1[0], w1[1])):
            for f in range(FB):
                pieces.append((w.rearrange("(f p) h -> f p h", p=P)[f], w1_hi[:, b, f, :], w1_lo[:, b, f, :]))
        for b, w in enumerate((sw2, w2[0], w2[1])):
            for c in range(KT * D // STAGE):
                n = STAGE // D
                src = w.rearrange("(k p) d -> p k d", p=P)[:, c * n:(c + 1) * n, :]
                pieces.append((src, w2_hi[:, b, c * n:(c + 1) * n, :], w2_lo[:, b, c * n:(c + 1) * n, :]))

        def staged(i, dst):
            v = stage[:, i % 2, :]
            return v if len(dst.shape) == 2 else v.rearrange("p (k d) -> p k d", d=D)

        block = ctx.enter_context(nc.Block())

        @block.sync
        def _(sp):
            def load_x(s, slot):
                wait(sp, x_stored, s, -1)
                sp.dma_start(x[:, slot], tiles_of(x_in, s)).then_inc(x_in_sem.sem, 16)

            give_credits(sp, [x_stored])
            load_x(0, 0)
            sp.dma_start(ident[:, :], ident_dram).then_inc(consts_in, 16)
            for e, g in enumerate((gate_w[0:1, :], gate_w[1:2, :])):
                sp.dma_start(gates[:, e, :], g[0].partition_broadcast(P)).then_inc(consts_in, 16)
            for e, b in enumerate((sb2, b2[0], b2[1])):
                sp.dma_start(b2_all[:, e, :], b.partition_broadcast(P)).then_inc(consts_in, 16)
            sp.dma_start(b1_col[:, :, :], b1_cols.rearrange("p (b k) -> p b k", k=KT)).then_inc(consts_in, 16)
            for i, (src, dst, _) in enumerate(pieces):
                if i >= 2:
                    sp.wait_ge(stage_lo, i - 1)
                sp.dma_start(staged(i, dst), src).then_inc(stage_in[i % 2], 16)

            def step(s, slot, last):
                if not last:
                    load_x(s + 1, 1 - slot)
                wait(sp, out_done, s, TT // 2)
                sp.dma_start(tiles_of(x_out, s), x[:, slot]).then_inc(x_stored.sem, 16)

            over_sequences(sp, step)
            wait(sp, x_stored, SEQS, 0)

        @block.gpsimd
        def _(pool):
            pool.memset(minus_half[:, :], -0.5).then_inc(half_set, 1)
            pool.wait_ge(half_set, 1)
            pool.wait_ge(consts_in, 16 * CONSTS)
            pool.tensor_tensor(b2_sum[:, :], b2_all[:, 0, :], b2_all[:, 1, :], ALU.add).then_inc(b2_part, 1)
            pool.wait_ge(b2_part, 1)
            pool.tensor_tensor(b2_sum[:, :], b2_sum[:, :], b2_all[:, 2, :], ALU.add).then_inc(b2_ready, 1)
            pool.wait_ge(b2_ready, 1)

            def norm(s, slot):
                wait_alone(pool, alone_pool, moments_done.sem, moments_done.at(s, TT))
                pool.tensor_scalar(var_eps[:, :], moments[:, :, 1], LN_EPS, None, ALU.add).then_inc(eps_added.sem, 1)
                wait(pool, eps_added, s, 1)
                pool.tensor_tensor(rstd[:, :], var_eps[:, :], minus_half[:, :], ALU.pow).then_inc(rstd_done.sem, 1)
                wait(pool, xn_done, s, TT)
                pool.tensor_tensor(x[:, slot], x[:, slot], b2_sum[:, :].unsqueeze(1).broadcast_to([P, TT, D]),
                                   ALU.add).then_inc(bias_added.sem, 1)

            norm(0, 0)

            def step(s, slot, last):
                if not last:
                    norm(s + 1, 1 - slot)

            over_sequences(pool, step)

        @block.scalar
        def _(act):
            for i, (_, hi, _) in enumerate(pieces):
                act.wait_ge(stage_in[i % 2], 16 * (i // 2 + 1))
                act.activation(hi, staged(i, hi), ACT.Copy).then_inc(stage_hi, 1)
            act.wait_ge(consts_in, 16 * CONSTS)
            give_credits(act, [hid_act])

            def turn(s, slot, g):
                wait(act, turned, s, g + 1)
                act.activation(xT_hi[:, slot, g // FB, g % FB, :], ps_turn[:, :], ACT.Copy).then_inc(turn_hi.sem, 1)

            for g in range(GROUPS):
                turn(0, 0, g)

            def step(s, slot, last):
                for k in range(K):
                    wait(act, hid_summed, s, k + 1)
                    wait(act, hid_split, s, k + 1 - RING)
                    act.activation(hid[:, k % RING, :], ps_hid[:, k % RING, :], ACT.Relu,
                                   bias=b1_col[:, k // KT, k % KT:k % KT + 1])
                    wait(act, hid_used, s, k + 1 - RING)
                    act.activation(hid_hi[:, k % RING, :], ps_hid[:, k % RING, :], ACT.Relu,
                                   bias=b1_col[:, k // KT, k % KT:k % KT + 1]).then_inc(hid_act.sem, 1)
                    if k - LOOKAHEAD in TURN_AT and not last:
                        turn(s + 1, 1 - slot, TURN_AT.index(k - LOOKAHEAD))

            over_sequences(act, step)

        @block.vector
        def _(dve):
            for i, (_, hi, lo) in enumerate(pieces):
                dve.wait_ge(stage_hi, i + 1)
                dve.tensor_tensor(lo, staged(i, lo), hi, ALU.subtract).then_inc(stage_lo, 1)
            dve.wait_ge(consts_in, 16 * CONSTS)
            give_credits(dve, [turn_lo, hid_split, out_done])

            def norm_stats(s, slot):
                wait(dve, x_in_sem, s, 1)
                for t in range(TT):
                    dve.bn_stats(stats[:, t, :], x[:, slot, t, :]).then_inc(stats_done.sem, 1)
                wait_alone(dve, alone, stats_done.sem, stats_done.at(s, TT))
                for t in range(TT):
                    dve.bn_aggr(moments[:, t, :], stats[:, t, :]).then_inc(moments_done.sem, 1)

            def norm_apply(s, slot):
                wait(dve, rstd_done, s, 1)
                for t in range(TT):
                    dve.tensor_scalar(xn[:, 0, t, :], x[:, slot, t, :], moments[:, t, 0:1], rstd[:, t:t + 1],
                                      ALU.subtract, ALU.mult).then_inc(xn_done.sem, 1)

            def scores(s, t):
                wait(dve, xn_done, s, TT)
                for e in range(2):
                    if 2 * t + e:
                        wait(dve, score_done, s, 2 * t + e)
                    dve.tensor_tensor_reduce(score_work[:, :], xn[:, 0, t, :], gates[:, e, :], 1.0, 0.0, ALU.mult,
                                             ALU.add, score[:, e, t:t + 1]).then_inc(score_done.sem, 1)

            def route(s):
                wait(dve, score_done, s, 2 * TT)
                dve.tensor_tensor(mask[:, 0, :], score[:, 0, :], score[:, 1, :], ALU.is_ge).then_inc(mask_done.sem, 1)
                dve.tensor_tensor(mask[:, 1, :], score[:, 0, :], score[:, 1, :], ALU.is_lt).then_inc(mask_done.sem, 1)

            def masked(s, e):
                wait(dve, mask_done, s, 2)
                for t in range(TT):
                    dve.tensor_scalar(xn[:, 1 + e, t, :], xn[:, 0, t, :], mask[:, e, t:t + 1], None,
                                      ALU.mult).then_inc(masked_done.sem, 1)

            def norm_part(s, slot, n):
                if n == 0:
                    norm_stats(s, slot)
                if n == 1:
                    norm_apply(s, slot)
                if 2 <= n < 2 + TT:
                    scores(s, n - 2)
                if n == 2 + TT:
                    route(s)
                if n in (3 + TT, 4 + TT):
                    masked(s, n - 3 - TT)

            def turn(s, slot, g):
                wait(dve, turn_hi, s, g + 1)
                dve.tensor_tensor(xT_lo[:, slot, g // FB, g % FB, :], ps_turn[:, :], xT_hi[:, slot, g // FB, g % FB, :],
                                  ALU.subtract).then_inc(turn_lo.sem, 1)

            for n in range(NORM_PARTS):
                norm_part(0, 0, n)
            for g in range(GROUPS):
                turn(0, 0, g)

            def step(s, slot, last):
                for k in range(K):
                    wait(dve, hid_act, s, k + 1)
                    dve.tensor_tensor(hid_lo[:, k % RING, :], hid[:, k % RING, :], hid_hi[:, k % RING, :],
                                      ALU.subtract).then_inc(hid_split.sem, 1)
                    if 0 <= k - NORM_AT < NORM_PARTS and not last:
                        norm_part(s + 1, 1 - slot, k - NORM_AT)
                    if k - LOOKAHEAD in TURN_AT and not last:
                        turn(s + 1, 1 - slot, TURN_AT.index(k - LOOKAHEAD))
                wait(dve, hid_used, s, K)
                wait(dve, bias_added, s, 1)
                for half in range(TT // 2):
                    part = slice(2 * half, 2 * half + 2)
                    dve.tensor_tensor(x[:, slot, part, :], ps_out[:, slot, part, :], x[:, slot, part, :],
                                      ALU.add).then_inc(out_done.sem, 1)

            over_sequences(dve, step)

        @block.tensor
        def _(pe):
            give_credits(pe, [hid_used])
            pe.wait_ge(consts_in, 16 * CONSTS)

            def turn(s, g):
                b, f = g // FB, g % FB
                if b:
                    wait(pe, masked_done, s, b * TT)
                else:
                    wait(pe, xn_done, s, TT)
                wait(pe, turn_lo, s, g)
                for t in range(TT):
                    last = pe.transpose(ps_turn[:, t * P:(t + 1) * P], xn[:, b, t, f * P:(f + 1) * P], ident[:, :])
                last.then_inc(turned.sem, 1)

            for g in range(GROUPS):
                turn(0, g)
            pe.wait_ge(stage_lo, len(pieces))

            def first(s, slot, k):
                b, h = k // KT, slice(k % KT * P, (k % KT + 1) * P)
                wait(pe, hid_act, s, k + 1 - RING)
                for f in range(FB):
                    mm = split_product(pe, ps_hid[:, k % RING, :], w1_hi[:, b, f, h], w1_lo[:, b, f, h],
                                       xT_hi[:, slot, b, f, :], xT_lo[:, slot, b, f, :], f == 0, f == FB - 1)
                mm.then_inc(hid_summed.sem, 1)

            def second(s, slot, k):
                wait(pe, hid_split, s, k + 1)
                if k == 0:
                    wait(pe, out_done, s, -TT // 2)
                for t in range(TT):
                    tok = slice(t * P, (t + 1) * P)
                    mm = split_product(pe, ps_out[:, slot, t, :], hid_hi[:, k % RING, tok], hid_lo[:, k % RING, tok],
                                       w2_hi[:, k // KT, k % KT, :], w2_lo[:, k // KT, k % KT, :],
                                       k == 0 and t % 2 == 0, k == K - 1, shared_bank=True)
                mm.then_inc(hid_used.sem, 1)

            def step(s, slot, last):
                for k in range(LOOKAHEAD):
                    if k == 0:
                        wait(pe, turn_lo, s, GROUPS)
                    first(s, slot, k)
                for k in range(K):
                    if k + LOOKAHEAD < K:
                        first(s, slot, k + LOOKAHEAD)
                    second(s, slot, k)
                    if k in TURN_AT and not last:
                        turn(s + 1, TURN_AT.index(k))

            over_sequences(pe, step)


def tower_kernel(nc, a, out):

    def stream(name):
        return nc.dram_tensor(name, (SEQS * SEQ, D), F32).ap()

    h0, attended, h1, h2, h3 = (stream(n) for n in ("h0", "attended", "h1", "h2", "h3"))
    with nc.cleanup_on_exit():
        attention_phase(nc, a["ident"], a["select"], a["mask"], a["rope_cos"], a["rope_sin"], a["tokens"], a["emb"],
                        a["ln1"], a["q_ut"], a["q_v"], a["q_b"], a["k_ut"], a["k_v"], a["k_b"], a["v_ut"], a["v_v"],
                        a["v_b"], a["out_ut"], a["out_v"], a["out_b"], h0, attended)
    with nc.cleanup_on_exit():
        mlp_phase(nc, a["ident"], attended, h0, a["ln2"], a["fc1_u"], a["fc1_v"], a["fc1_b"], a["fc2_u"], a["fc2_v"],
                  a["fc2_b"], h1)
    with nc.cleanup_on_exit():
        ffn_phase(nc, a["ident"], h1, a["w_up_t"], a["w_down_t"], h2)
    with nc.cleanup_on_exit():
        mamba_phase(nc, a["ident"], a["triangles"], h2, a["in_proj_t"], a["conv_w"], a["conv_b"], a["a_log"],
                    a["dt_w_t"], a["dt_b"], a["b_w_t"], a["c_w_t"], a["d_skip"], a["ln_y"], a["out_proj_t"], h3)
    with nc.cleanup_on_exit():
        moe_phase(nc, a["ident"], h3, a["gate_w"], a["w1"], a["b1"], a["w2"], a["b2"], a["sw1"], a["sw2"], a["sb2"], out)


def kernel(**inputs):
    import numpy as np
    import concourse.bacc as bacc
    from concourse.bass_utils import run_bass_kernel_spmd

    def given(name):
        return np.ascontiguousarray(inputs[name])

    def turned(name):
        return np.ascontiguousarray(given(name).T)

    def columns(v):
        return np.ascontiguousarray(v.reshape(-1, P).T)

    def side_by_side(*vs):
        return np.ascontiguousarray(np.concatenate([columns(v) for v in vs], axis=1))

    def ranks_first(name):
        return np.ascontiguousarray(given(name).transpose(1, 2, 0))

    i, j = np.mgrid[0:P, 0:P]
    later = np.where(i > j, np.float32(-1e5), np.float32(0))
    triangles = np.stack([(i <= j).astype(np.float32), (i > j).astype(np.float32), np.ones((P, P), np.float32), later])
    inverse = np.float32(1) / (10000.0 ** (np.arange(0, D, 2) / D)).astype(np.float32)
    angle = (np.arange(SEQ, dtype=np.float32)[:, None] * inverse[None, :]).astype(np.float64)
    hd = given("L0_attn_q_V").shape[2]
    pairs = P // hd // 2
    select = np.zeros((4, pairs, P, P), np.float32)
    for half, places in enumerate(((0, 1), (2,), (0, 2), (1,))):
        for pair in range(pairs):
            for r in range(2):
                for n in range(hd):
                    for place in places:
                        select[half, pair, (2 * pair + r) * hd + n, 64 * r + place * hd + n] = 1.0

    conv = given("L1_attn_conv_w")
    taps = conv.shape[-1]
    b1 = given("L1_ffn_b1")
    arrays = {
        "ident": np.eye(P, dtype=np.float32),
        "select": select,
        "mask": np.where(j > i, np.float32(-1e30), np.float32(0)),
        "triangles": triangles,
        "rope_cos": np.cos(angle).astype(np.float32),
        "rope_sin": np.sin(angle).astype(np.float32),
        "tokens": np.ascontiguousarray(given("x").reshape(SEQS * TT, P).T),
        "emb": given("L0_tok_emb_weight"),
        "ln1": side_by_side(given("L0_attn_ln1_g"), given("L0_attn_ln1_b")),
        "ln2": side_by_side(given("L0_attn_ln2_g"), given("L0_attn_ln2_b")),
        "out_ut": turned("L0_attn_out_U"), "out_v": given("L0_attn_out_V"), "out_b": given("L0_attn_out_b"),
        "v_b": given("L0_attn_v_b").reshape(-1),
        "fc1_u": given("L0_attn_fc1_U"), "fc1_v": given("L0_attn_fc1_V"), "fc1_b": columns(given("L0_attn_fc1_b")),
        "fc2_u": given("L0_attn_fc2_U"), "fc2_v": given("L0_attn_fc2_V"), "fc2_b": given("L0_attn_fc2_b"),
        "w_up_t": turned("L0_ffn_w_up"), "w_down_t": turned("L0_ffn_w_down"),
        "in_proj_t": turned("L1_attn_in_proj_w"),
        "conv_w": np.ascontiguousarray(conv.reshape(-1, P, taps).transpose(1, 0, 2)).reshape(P, -1),
        "conv_b": columns(given("L1_attn_conv_b")), "a_log": given("L1_attn_A_log"),
        "dt_w_t": turned("L1_attn_dt_w"), "dt_b": given("L1_attn_dt_b"),
        "b_w_t": turned("L1_attn_B_w"), "c_w_t": turned("L1_attn_C_w"), "d_skip": given("L1_attn_D"),
        "ln_y": side_by_side(given("L1_attn_ln_w"), given("L1_attn_ln_b")),
        "out_proj_t": turned("L1_attn_out_proj_w"),
        "gate_w": given("L1_ffn_gate_w"), "w1": given("L1_ffn_w1"), "w2": given("L1_ffn_w2"), "b2": given("L1_ffn_b2"),
        "b1": side_by_side(given("L1_ffn_sb1"), b1[0], b1[1]),
        "sw1": given("L1_ffn_sw1"), "sw2": given("L1_ffn_sw2"), "sb2": given("L1_ffn_sb2"),
    }
    for n in "qkv":
        arrays[f"{n}_ut"] = ranks_first(f"L0_attn_{n}_U")
        arrays[f"{n}_v"] = given(f"L0_attn_{n}_V")
    for n in "qk":
        arrays[f"{n}_b"] = columns(given(f"L0_attn_{n}_b"))

    nc = bacc.Bacc("TRN2", target_bir_lowering=False, num_devices=1)
    aps = {name: nc.dram_tensor("in_" + name, a.shape, mybir.dt.from_np(a.dtype), kind="ExternalInput").ap()
           for name, a in arrays.items()}
    out = nc.dram_tensor("out", (SEQS * SEQ, D), F32, kind="ExternalOutput").ap()
    tower_kernel(nc, aps, out)
    result = run_bass_kernel_spmd(nc, [{"in_" + name: a for name, a in arrays.items()}], core_ids=[0])
    return result.results[0]["out"].reshape(SEQS, SEQ, D)
```

```python
from contextlib import ExitStack

import concourse.bass as bass
from concourse import mybir

F32 = mybir.dt.float32
F32R = mybir.dt.float32r
I32 = mybir.dt.int32
ACT = mybir.ActivationFunctionType
ALU = mybir.AluOpType
AX_X = mybir.AxisListType.X

P = 128
SEQS = 16
SEQ = 512
TT = SEQ // P
D = 256
FB = D // P
LN_EPS = 1e-5
RMS_EPS = 1e-8
LOOKAHEAD = 2
RING = 3


class Signal:

    def __init__(self, ctx, nc, name, per_seq, credit=0, unit=1):
        self.sem = nc.alloc_semaphore(name=name)
        self.per_seq, self.credit, self.unit = per_seq, credit, unit

    def at(self, s, k):
        return s * (self.per_seq * self.unit) + (k + self.credit) * self.unit


class Loads:

    def __init__(self, ctx, nc, name):
        self.sems = [nc.alloc_semaphore(name=f"{name}{slot}") for slot in range(2)]

    def wait(self, eng, s, slot):
        eng.wait_ge(self.sems[slot], (s - slot) * 8 + 16)


def wait(eng, signal, s, k):
    eng.wait_ge(signal.sem, signal.at(s, k))


def wait_alone(eng, tally, sem, value):
    eng.wait_ge(sem, value)
    eng.sem_inc(tally, 1)


def give_credits(eng, signals):
    for signal in signals:
        if signal.credit:
            eng.sem_inc(signal.sem, signal.credit * signal.unit)


def over_sequences(eng, step):
    with eng.Fori(0, SEQS // 2 - 1) as pair:
        step(pair * 2, 0, False)
        step(pair * 2 + 1, 1, False)
    step(SEQS - 2, 0, False)
    step(SEQS - 1, 1, True)


def over_steps(eng, step, peeled=1):
    step(0, 0, True, False)
    with eng.Fori(0, (SEQS - 1 - peeled) // 2) as pair:
        step(pair * 2 + 1, 1, False, False)
        step(pair * 2 + 2, 0, False, False)
    for s in range(SEQS - peeled, SEQS):
        step(s, s % 2, False, s == SEQS - 1)


def split_product(pe, out, w_hi, w_lo, x_hi, x_lo, first, last, shared_bank=False):
    pe.matmul(out, w_hi, x_hi, start=first, stop=False, skip_group_check=shared_bank)
    pe.matmul(out, w_hi, x_lo, start=False, stop=False, skip_group_check=shared_bank)
    return pe.matmul(out, w_lo, x_hi, start=False, stop=last, skip_group_check=shared_bank)


def tiles_of(x, s):
    return x.rearrange("(s t p) d -> s p t d", t=TT, p=P)[s]


class Ring:

    def __init__(self, ctx, nc, name, banks, before, each, end, skipped=()):
        self.banks, self.before, self.each, self.end, self.skipped = banks, before, each, end, skipped
        self.full = nc.alloc_semaphore(name=f"{name}_filled")
        self.free = {r: nc.alloc_semaphore(name=f"{name}_freed_by_{r}") for r in sorted(set(dict(each).values()))}
        assert len(before) % banks == 0 and len(each) % banks == 0

    def _uses(self, s, last):
        return self.before if s is None else self.end if last else self.each

    def _place(self, s, use, last):
        return [u for u, _ in self._uses(s, last)].index(use)

    def bank(self, s, use, last):
        return self._place(s, use, last) % self.banks

    def filled(self, s, use, last):
        n = self._place(s, use, last) + 1
        return n if s is None else s * len(self.each) + (len(self.before) - len(self.skipped) + n)

    def read(self, s, use, last):
        uses = self._uses(s, last)
        at = self._place(s, use, last)
        reader = uses[at][1]
        n = sum(r == reader for _, r in uses[:at + 1])
        if s is not None:
            n += self._earlier(s, reader)
        return self.free[reader], n

    def _earlier(self, s, reader):
        n = sum(r == reader for _, r in self.before) - sum(r == reader for _, r in self.skipped)
        return s * sum(r == reader for _, r in self.each) + n

    def freed(self, s, use, last):
        at = self._place(s, use, last)
        uses = self._uses(s, last)
        if at >= self.banks:
            reader = uses[at - self.banks][1]
            needs = [(reader, sum(r == reader for _, r in uses[:at - self.banks + 1]))]
        elif s is None:
            return []
        else:
            needs = [(reader, 0) for reader in self.free]
        found = []
        for reader, n in needs:
            if s is not None:
                n += self._earlier(s, reader)
            found.append((self.free[reader], n))
        return found


def wait_free(pe, ring, s, use, last):
    for sem, value in ring.freed(s, use, last):
        pe.wait_ge(sem, value)


def wait_filled(eng, ring, s, use, last):
    eng.wait_ge(ring.full, ring.filled(s, use, last))


def wait_read(eng, ring, s, use, last):
    eng.wait_ge(*ring.read(s, use, last))


def attention_phase(nc, ident_dram, sel_dram, mask_dram, rope_cos, rope_sin, tokens, emb, ln_cols,
                    q_ut, q_v, q_b_col, k_ut, k_v, k_b_col, v_ut, v_v, v_b, out_ut, out_v, out_b, h0_out, x_out):
    H, R, HD = q_v.shape
    GROUPS = 2
    GH = H // GROUPS
    PAIRS = H // 2
    ROB = out_ut.shape[0] // 2
    SCALE = float(HD) ** -0.5
    BF16 = mybir.dt.bfloat16
    assert GH * HD == P and D == H * HD and TT == 4

    QUADS = H // 4
    VW = 2 * HD

    PIECES = ((3,), (2, 0), (1,))
    NP = len(PIECES)
    TURNED = (((0, 0), (0, 1), (0, 2), (0, 3)), ((1, 1), (1, 2), (1, 3), (3, 3)), ((2, 2), (2, 3)))
    TURNED_AT = (0, 4, 8)
    KEYS_AT = {0: 0, 1: 4, 2: 8, 3: 7}
    TURNED_BY = ("act", "dve", "act")
    AT = {3: 0, 2: 4, 0: 7, 1: 8}
    TILES = 10

    def columns(qt):
        start = AT[qt] * P
        return slice(start, start + (qt + 1) * P)

    WORK = {(0, 2): "norm3", (2, 1): "out0", (3, 0): "out1", (4, 2): "norm0", (8, 2): "norm1", (12, 2): "norm2"}
    FRONT = ["turn0", "turn1", "q0", "k0", "v0", "v1", "q1", "k1"]
    for j in range(PAIRS):
        FRONT += [f"ksel{j}", f"qsel{j}"]
    at = (3, 1)
    for name in FRONT:
        while at in WORK:
            at = (at[0] + at[1], 1 - at[1])
        WORK[at] = name
    TAIL = ["norm3", "out0", "out1"]
    READER = {"turn": "dve", "q": "act", "k": "act", "v": "dve", "ksel": "act", "qsel": "dve", "norm": "dve", "out": "dve"}
    WORK_ORDER = [WORK[h, i] for h in range(H) for i in range(3) if (h, i) in WORK]

    def kind(name):
        return name.rstrip("0123456789")

    def with_reader(names):
        return [(name, READER[kind(name)]) for name in names]

    NORM_AT = {0: "moments", 1: "x", 2: "moments2", 3: "xn"}

    with ExitStack() as ctx:
        def sb(name, shape, dt=F32):
            return ctx.enter_context(nc.sbuf_tensor("att_" + name, shape, dt))

        def psum(name, shape):
            return ctx.enter_context(nc.psum_tensor("att_" + name, shape, F32))

        def sem(name):
            return nc.alloc_semaphore(name="att_" + name)

        def signal(name, per_seq, credit=0, unit=1):
            return Signal(ctx, nc, "att_" + name, per_seq, credit, unit)

        w_hi, w_lo = sb("w_hi", [P, 3, FB, D], F32R), sb("w_lo", [P, 3, FB, D], F32R)
        wo_hi, wo_lo = sb("wo_hi", [P, QUADS, D], F32R), sb("wo_lo", [P, QUADS, D], F32R)
        ln = sb("ln", [P, 2, FB])
        ln_b_wide = sb("ln_b_wide", [P, FB, P])
        b_in, b_col = sb("b_in", [P, 2, GROUPS]), sb("b_col", [P, 2, GROUPS])
        vb_in, vb_all = sb("vb_in", [P, D]), sb("vb_all", [P, D])
        ob_all = sb("ob_all", [P, D])
        ident, ident16 = sb("ident", [P, P]), sb("ident16", [P, P], BF16)
        mask_in, mask16 = sb("mask_in", [P, P]), sb("mask16", [P, P], BF16)
        sel = sb("sel", [P, 4, GH // 2, P], F32R)
        cos, sin = sb("cos", [P, TT, D // 2]), sb("sin", [P, TT, D // 2])
        minus_half = sb("minus_half", [P, TT])
        factor_v = sb("factor_v", [P, 3, H, HD])
        factor_ou, factor_ov = sb("factor_ou", [P, 2, D]), sb("factor_ov", [P, 2, D])

        ids = sb("ids", [P, SEQS * TT], I32)
        ids_now = sb("ids_now", [P, TT], I32)
        e = sb("e", [P, TT, D])
        rope_work = sb("rope_work", [P, 2, TT, D // 2])
        h0 = sb("h0", [P, TT, D])
        stats, stats2 = sb("stats", [P, TT, 6]), sb("stats2", [P, TT, 6])
        moments, moments2 = sb("moments", [P, TT, 2]), sb("moments2", [P, TT, 2])
        var_eps, var_eps2 = sb("var_eps", [P, TT]), sb("var_eps2", [P, TT])
        rstd, rstd2 = sb("rstd", [P, TT]), sb("rstd2", [P, TT])
        x_xn = sb("x_xn", [P, 2, TT, D])
        x, xn = x_xn[:, 0], x_xn[:, 1]
        xb = sb("xb", [P, 2, TT, D])
        xT_hi, xT_lo = sb("xT_hi", [P, FB, SEQ], F32R), sb("xT_lo", [P, FB, SEQ], F32R)
        flats = sb("flats", [P, 5, SEQ])
        qk, o, spread, wide = flats[:, 0:2], flats[:, 2], flats[:, 3], flats[:, 4]
        denom, recip = sb("denom", [P, H, TT]), sb("recip", [P, H, TT])
        qk_hi, qk_lo = sb("qk_hi", [P, 2, GROUPS, SEQ], F32R), sb("qk_lo", [P, 2, GROUPS, SEQ], F32R)
        q_rows = sb("q_rows", [P, H, SEQ], F32R)
        k_rows = sb("k_rows", [P, PAIRS, SEQ], F32R)
        v_wide = sb("v_wide", [P, 2, TT, H, VW])
        neg_max = sb("neg_max", [P, 2, TT])
        exps = sb("exps", [P, 4, TILES * P])
        o_hi, o_lo = sb("o_hi", [P, QUADS, SEQ], F32R), sb("o_lo", [P, QUADS, SEQ], F32R)
        exps_flat = exps[:, :, :].rearrange("p a b -> p (a b)")
        factor_u0 = exps_flat[:, 0:H * D].rearrange("p (h d) -> p h d", h=H)
        factor_padded = exps_flat[:, H * D:H * D + 2 * H * VW].rearrange("p (b h w) -> p b h w", b=2, w=VW)
        factor_u1 = v_wide[:, :, :, :, :].rearrange("p a b c d -> p (a b c d)").rearrange("p (h d) -> p h d", h=H)
        flats_all = flats[:, :, :].rearrange("p a b -> p (a b)")
        w_raw = flats_all[:, 0:3 * FB * D].rearrange("p (i f d) -> p i f d", i=3, f=FB)
        w_scaled = x_xn[:, :, :, :].rearrange("p a b c -> p (a b c)")[:, 0:3 * FB * D].rearrange("p (i f d) -> p i f d", i=3, f=FB)
        wo_raw = flats_all[:, 3 * FB * D:3 * FB * D + QUADS * D].rearrange("p (q d) -> p q d", q=QUADS)

        ps_s = psum("ps_s", [P, 2, SEQ])
        ps_t = psum("ps_t", [P, 2, SEQ])
        ps_o = psum("ps_o", [P, 2, SEQ])
        ps_w = psum("ps_w", [P, 2, SEQ])

        ring = Ring(ctx, nc, "att_work", 2, with_reader(FRONT), with_reader(WORK_ORDER),
                    with_reader(TAIL + ["norm0", "norm1", "norm2"]) + [("last_" + n, "dve") for n in TAIL], skipped=with_reader(TAIL))
        consts_in, sel_in, filled = sem("consts_in"), sem("sel_in"), sem("filled")
        factors_in = [sem(f"factors_in{i}") for i in range(4)]
        fused, w_copied, w_split_hi, w_ready = sem("fused"), sem("w_copied"), sem("w_split_hi"), sem("w_ready")
        wide_made, bias_fused, consts16 = sem("wide_made"), sem("bias_fused"), sem("consts16")
        ids_in = sem("ids_in")
        ids_copied = signal("ids_copied", 1)
        gathered = signal("gathered", 1, unit=16 * TT)
        rope_part = signal("rope_part", 2)
        rope_done = signal("rope_done", 2)
        h0_stored = signal("h0_stored", 1, credit=1, unit=16)
        h0_read = signal("h0_read", 1, credit=1)
        x_stored = signal("x_stored", 1, credit=2, unit=16)
        alone, alone_pool, alone_sp = sem("waits_of_dve"), sem("waits_of_pool"), sem("waits_of_sp")
        stats_done, stats2_done = signal("stats_done", TT), signal("stats2_done", TT)
        moments_done, moments2_done = signal("moments_done", TT), signal("moments2_done", TT)
        eps_added, eps2_added = signal("eps_added", 1), signal("eps2_added", 1)
        rstd_done, rstd2_done = signal("rstd_done", 1), signal("rstd2_done", 1)
        x_done, xn_done = signal("x_done", TT), signal("xn_done", TT)
        biased = signal("biased", 1, credit=1)
        turn_hi = signal("turn_hi", FB)
        qk_copied = signal("qk_copied", 2 * GROUPS)
        qk_split = signal("qk_split", 2 * GROUPS, credit=2)
        summed = signal("summed", NP * H)
        max_done = signal("max_done", NP * H)
        exp_done = signal("exp_done", NP * H, credit=2)
        turned = signal("turned", NP * H)
        taken = {"act": signal("taken_by_act", 2 * H, credit=2), "dve": signal("taken_by_dve", H, credit=1)}
        o_summed = signal("o_summed", QUADS)
        recip_done = signal("recip_done", QUADS, credit=QUADS)
        widened = signal("widened", QUADS)
        o_done = signal("o_done", QUADS, credit=2)
        o_hi_done = signal("o_hi_done", QUADS, credit=1)
        o_split = signal("o_split", QUADS, credit=1)

        def taken_at(h, p):
            by = TURNED_BY[p]
            per = TURNED_BY.count(by)
            return taken[by], h * per + TURNED_BY[:p + 1].count(by)

        def last_bank(name):
            return ps_w[:, ring.bank(SEQS - 1, "last_" + name, True)]

        def do_work(work, s, slot, first, last, h, i):
            name = WORK.get((h, i))
            if name is None or (first and name in TAIL) or (last and name in FRONT):
                return
            work(name, s, slot, last)

        block = ctx.enter_context(nc.Block())
        CONSTS = 10

        @block.sync
        def _(sp):
            give_credits(sp, [h0_stored, x_stored])
            sp.dma_start(ids[:, :], tokens).then_inc(ids_in, 16)

            def factors(i, ut, vv, buffer):
                sp.dma_start(buffer[0:R, :, :], ut.rearrange("h r d -> r h d")).then_inc(factors_in[i], 16)
                sp.dma_start(factor_v[0:R, i, :, :], vv.rearrange("h r d -> r h d")).then_inc(factors_in[i], 16)

            factors(0, q_ut, q_v, factor_u0)
            sp.dma_start(cos[:, :, :], rope_cos.rearrange("(t p) d -> p t d", p=P)).then_inc(consts_in, 16)
            sp.dma_start(sin[:, :, :], rope_sin.rearrange("(t p) d -> p t d", p=P)).then_inc(consts_in, 16)
            factors(1, k_ut, k_v, factor_u1)
            sp.dma_start(ln[:, :, :], ln_cols.rearrange("p (k f) -> p k f", f=FB)).then_inc(consts_in, 16)
            sp.dma_start(ident[:, :], ident_dram).then_inc(consts_in, 16)
            sp.dma_start(mask_in[:, :], mask_dram).then_inc(consts_in, 16)
            sp.dma_start(b_in[:, 0, :], q_b_col).then_inc(consts_in, 16)
            sp.dma_start(b_in[:, 1, :], k_b_col).then_inc(consts_in, 16)
            sp.dma_start(vb_in[:, :], v_b.partition_broadcast(P)).then_inc(consts_in, 16)
            sp.dma_start(ob_all[:, :], out_b.partition_broadcast(P)).then_inc(consts_in, 16)
            sp.wait_ge(fused, 1)
            factors(2, v_ut, v_v, factor_u0)
            sp.dma_start(factor_ou[0:ROB, :, :], out_ut.rearrange("(b r) d -> r b d", b=2)).then_inc(factors_in[3], 16)
            sp.dma_start(factor_ov[0:ROB, :, :], out_v.rearrange("(b r) d -> r b d", b=2)).then_inc(factors_in[3], 16)
            sp.dma_start(xb[:, :, :, :].rearrange("p a b c -> p (a b c)").rearrange("p (k j m) -> p k j m", k=4, j=GH // 2),
                         sel_dram.rearrange("k j p m -> p k j m")).then_inc(sel_in, 16)
            sp.wait_ge(sel_in, 16)
            sp.sem_inc(consts_in, 16)

            def store_h0(s):
                wait_alone(sp, alone_sp, rope_done.sem, rope_done.at(s, 2))
                sp.dma_start(tiles_of(h0_out, s), h0[:, :, :]).then_inc(h0_stored.sem, 16)

            store_h0(0)
            store_h0(1)

            def step(s, slot, first, last):
                if not first:
                    wait_alone(sp, alone_sp, *ring.read(s, "out1", last))
                    wait_alone(sp, alone_sp, biased.sem, biased.at(s, 1))
                    sp.dma_start(tiles_of(x_out, s - 1), xb[:, 1 - slot]).then_inc(x_stored.sem, 16)
                if not (isinstance(s, int) and s + 2 >= SEQS):
                    store_h0(s + 2)

            over_steps(sp, step, 3)
            wait_read(sp, ring, SEQS - 1, "last_out1", True)
            sp.dma_start(tiles_of(x_out, SEQS - 1), xb[:, (SEQS - 1) % 2]).then_inc(x_stored.sem, 16)
            wait(sp, x_stored, SEQS, 0)
            wait(sp, h0_stored, SEQS, 0)

        @block.gpsimd
        def _(pool):
            give_credits(pool, [biased, qk_split, o_split])
            pool.memset(minus_half[:, :], -0.5).then_inc(filled, 1)
            pool.memset(q_rows[:, :, :].bitcast(F32), 0.0).then_inc(filled, 1)
            pool.wait_ge(filled, 2)
            pool.wait_ge(ids_in, 16)

            def gather(s):
                pool.tensor_copy(ids_now[:, :], ids[:, bass.ds(s * TT, TT)]).then_inc(ids_copied.sem, 1)
                wait_alone(pool, alone_pool, ids_copied.sem, ids_copied.at(s, 1))
                for t in range(TT):
                    pool.indirect_dma_start(e[:, t, :], None, emb, bass.IndirectOffsetOnAxis(ap=ids_now[:, t:t + 1], axis=0)
                                            ).then_inc(gathered.sem, 16)

            def rope(s):
                wait(pool, gathered, s, 1)
                even, odd = e[:, :, 0:D:2], e[:, :, 1:D:2]
                a, b = rope_work[:, 0], rope_work[:, 1]
                pool.tensor_tensor(a, even, cos[:, :, :], ALU.mult)
                pool.tensor_tensor(b, odd, sin[:, :, :], ALU.mult).then_inc(rope_part.sem, 1)
                wait(pool, rope_part, s, 1)
                wait(pool, h0_stored, s, 0)
                wait(pool, h0_read, s, 0)
                pool.tensor_tensor(h0[:, :, 0:D:2], a, b, ALU.subtract).then_inc(rope_done.sem, 1)
                wait(pool, rope_done, s, 1)
                pool.tensor_tensor(a, even, sin[:, :, :], ALU.mult)
                pool.tensor_tensor(b, odd, cos[:, :, :], ALU.mult).then_inc(rope_part.sem, 1)
                wait(pool, rope_part, s, 2)
                pool.tensor_tensor(h0[:, :, 1:D:2], a, b, ALU.add).then_inc(rope_done.sem, 1)

            def norm(s, done, mom, added, ve, ready, r):
                wait_alone(pool, alone_pool, done.sem, done.at(s, TT))
                pool.tensor_scalar(ve[:, :], mom[:, :, 1], LN_EPS, None, ALU.add).then_inc(added.sem, 1)
                wait(pool, added, s, 1)
                pool.tensor_tensor(r[:, :], ve[:, :], minus_half[:, :], ALU.pow).then_inc(ready.sem, 1)

            def norm1(s):
                norm(s, moments_done, moments, eps_added, var_eps, rstd_done, rstd)

            def norm2(s):
                norm(s, moments2_done, moments2, eps2_added, var_eps2, rstd2_done, rstd2)

            def bias(s, slot):
                wait(pool, x_done, s, TT)
                wait(pool, x_stored, s, -1)
                pool.tensor_tensor(xb[:, slot], x[:, :, :], ob_all[:, :].unsqueeze(1).broadcast_to([P, TT, D]),
                                   ALU.add).then_inc(biased.sem, 1)

            def split_qk(s, name, last):
                i, n = "qk".index(kind(name)), int(name[-1])
                pool.wait_ge(*ring.read(s, name, last))
                pool.tensor_tensor(qk_lo[:, i, n, :], qk[:, i, :], qk_hi[:, i, n, :], ALU.subtract).then_inc(qk_split.sem, 1)

            def split_o(s, quad):
                wait(pool, o_hi_done, s, quad + 1)
                pool.tensor_tensor(o_lo[:, quad, :], o, o_hi[:, quad, :], ALU.subtract).then_inc(o_split.sem, 1)

            gather(0)
            pool.wait_ge(consts_in, 16 * CONSTS)
            rope(0)
            pool.wait_ge(fused, 2)
            pool.memset(v_wide[:, :, :, :, HD:VW], 0.0).then_inc(filled, 1)
            pool.wait_ge(consts16, 3)
            norm1(0)
            norm2(0)
            bias(0, 0)
            gather(1)
            for name in ("q0", "k0", "q1", "k1"):
                split_qk(None, name, False)
            rope(1)

            def widen(s, quad):
                wait(pool, recip_done, s, quad + 1)
                wait_alone(pool, alone_pool, o_done.sem, o_done.at(s, quad))
                pool.tensor_copy(wide.rearrange("p (t h w) -> p t h w", t=TT, w=VW),
                                 recip[:, 4 * quad:4 * quad + 4, :].rearrange("p h t -> p t h").unsqueeze(3).broadcast_to(
                                     [P, TT, 4, VW])).then_inc(widened.sem, 1)

            def step(s, slot, first, last):
                ahead = not (isinstance(s, int) and s + 2 >= SEQS)
                if not first:
                    widen(s - 1, QUADS - 1)
                if not last:
                    norm1(s + 1)
                if not first:
                    split_o(s - 1, QUADS - 1)
                if not last:
                    norm2(s + 1)
                widen(s, 0)
                if not last:
                    split_qk(s, "q0", last)
                    split_qk(s, "k0", last)
                split_o(s, 0)
                if not last:
                    split_qk(s, "q1", last)
                    split_qk(s, "k1", last)
                widen(s, 1)
                if not last:
                    bias(s + 1, 1 - slot)
                if ahead:
                    gather(s + 2)
                split_o(s, 1)
                if ahead:
                    rope(s + 2)
                widen(s, 2)
                split_o(s, 2)

            over_steps(pool, step, 3)
            widen(SEQS - 1, QUADS - 1)
            split_o(SEQS - 1, QUADS - 1)

        def fused_bank(i):
            return (ps_s[:, i, :] if i < 2 else ps_w[:, 0, :]).rearrange("p (f d) -> p f d", f=FB)

        fused_out = ps_o[:, :, :].rearrange("p b (q d) -> p (b q) d", d=D)

        @block.scalar
        def _(act):
            give_credits(act, [exp_done, taken["act"], o_hi_done])
            act.wait_ge(consts_in, 16 * CONSTS)
            act.activation(sel[:, :, :, :].rearrange("p a b c -> p (a b c)"), xb[:, :, :, :].rearrange("p a b c -> p (a b c)"),
                           ACT.Copy).then_inc(consts16, 1)
            act.activation(ident16[:, :], ident[:, :], ACT.Copy).then_inc(consts16, 1)
            act.activation(mask16[:, :], mask_in[:, :], ACT.Copy).then_inc(consts16, 1)
            for i in range(3):
                act.wait_ge(w_copied, 2 * (i + 1))
                act.activation(w_hi[:, i], w_scaled[:, i], ACT.Copy).then_inc(w_split_hi, 1)
            act.wait_ge(w_copied, 7)
            act.activation(wo_hi[:, :, :], wo_raw[:, :, :], ACT.Copy).then_inc(w_split_hi, 1)

            def work(name, s, slot, last):
                k, n = kind(name), int(name[-1])
                bank = ps_w[:, ring.bank(s, name, last)]
                if k in ("v", "out", "qsel", "norm"):
                    return
                wait_filled(act, ring, s, name, last)
                of = 0 if s is None else s + 1
                if k == "turn":
                    act.activation(xT_hi[:, n, :], bank, ACT.Copy).then_inc(turn_hi.sem, 1)
                if k in ("q", "k"):
                    i = "qk".index(k)
                    wait(act, qk_split, of, 2 * n + i - 1)
                    bias = b_col[:, i, n:n + 1]
                    act.activation(qk[:, i, :], bank, ACT.Identity, bias=bias)
                    act.activation(qk_hi[:, i, n, :], bank, ACT.Identity, bias=bias
                                   ).then_inc(ring.free["act"], 1)
                if k == "ksel":
                    act.activation(k_rows[:, n, :], bank, ACT.Copy).then_inc(ring.free["act"], 1)

            def exp(s, h, p):
                wait(act, max_done, s, NP * h + p + 1)
                if p == 0 and h % 4 == 0:
                    wait(act, recip_done, s, h // 4 + 1 - QUADS)
                for qt in PIECES[p]:
                    first = AT[PIECES[p][0]]
                    src = ps_s[:, (NP * h + p) % 2, (AT[qt] - first) * P:(AT[qt] - first + qt + 1) * P]
                    done = act.activation(exps[:, h % 2, columns(qt)], src, ACT.Exp, bias=neg_max[:, h % 2, qt:qt + 1],
                                          accum_out=denom[:, h, qt:qt + 1])
                done.then_inc(exp_done.sem, 1)

            def take(s, h, p):
                wait(act, turned, s, NP * h + p + 1)
                n = len(TURNED[p]) * P
                piece = slice(TURNED_AT[p] * P, TURNED_AT[p] * P + n)
                act.activation(exps[:, 2 + h % 2, piece], ps_t[:, (NP * h + p) % 2, 0:n], ACT.Copy
                               ).then_inc(taken["act"].sem, 1)

            act.wait_ge(w_ready, 9)
            for name in FRONT:
                work(name, None, 0, False)
            for p in range(NP):
                exp(0, 0, p)

            def split_o(s, quad):
                wait(act, o_done, s, quad + 1)
                act.activation(o_hi[:, quad, :], o, ACT.Copy).then_inc(o_hi_done.sem, 1)

            def step(s, slot, first, last):
                for h in range(H):
                    more = h < H - 1 or not last
                    nxt = (s, h + 1) if h < H - 1 else (s + 1, 0)
                    if more:
                        exp(*nxt, 0)
                    take(s, h, 0)
                    if more:
                        exp(*nxt, 1)
                        exp(*nxt, 2)
                    take(s, h, 2)
                    do_work(work, s, slot, first, last, h, 0)
                    if h % 4 == 1 and not (first and h < 4):
                        split_o(*((s, h // 4 - 1) if h > 4 else (s - 1, QUADS - 1)))
                    do_work(work, s, slot, first, last, h, 1)

            over_steps(act, step, 1)
            split_o(SEQS - 1, QUADS - 1)

        @block.vector
        def _(dve):
            give_credits(dve, [taken["dve"], recip_done, o_done, h0_read])
            dve.wait_ge(consts_in, 16 * CONSTS)
            for f in range(FB):
                dve.tensor_copy(ln_b_wide[:, f, :], ln[:, 1, f:f + 1].broadcast_to([P, P])).then_inc(wide_made, 1)
            dve.memset(factor_padded[:, :, :, :], 0.0).then_inc(wide_made, 1)
            dve.wait_ge(wide_made, 3)
            dve.wait_ge(factors_in[3], 32)
            dve.tensor_copy(factor_padded[0:ROB, :, :, 0:HD],
                            factor_ou[0:ROB, :, :].rearrange("p b (h d) -> p b h d", h=H)).then_inc(wide_made, 1)
            for i in range(3):
                scale = SCALE if i == 0 else 1.0
                dve.wait_ge(fused, i + 1)
                dve.tensor_scalar(w_raw[:, i], fused_bank(i), scale, None, ALU.mult).then_inc(w_copied, 1)
                dve.wait_ge(w_copied, 2 * i + 1)
                for f in range(FB):
                    done = dve.tensor_scalar(w_scaled[:, i, f, :], w_raw[:, i, f, :], ln[:, 0, f:f + 1], None, ALU.mult)
                done.then_inc(w_copied, 1)
            dve.wait_ge(fused, 4)
            dve.tensor_copy(wo_raw[:, :, :], fused_out).then_inc(w_copied, 1)
            dve.wait_ge(w_copied, 7)
            for i in range(3):
                dve.wait_ge(w_split_hi, i + 1)
                dve.tensor_tensor(w_lo[:, i], w_scaled[:, i], w_hi[:, i], ALU.subtract).then_inc(w_ready, 1)
            dve.wait_ge(w_split_hi, 4)
            dve.tensor_tensor(wo_lo[:, :, :], wo_raw[:, :, :], wo_hi[:, :, :], ALU.subtract).then_inc(w_ready, 1)
            dve.wait_ge(bias_fused, 1)
            dve.scalar_tensor_tensor(b_col[:, 0, :], b_in[:, 0, :], SCALE, ps_t[:, 1, 0:GROUPS], ALU.mult,
                                     ALU.add).then_inc(w_ready, 1)
            dve.tensor_tensor(b_col[:, 1, :], b_in[:, 1, :], ps_t[:, 1, GROUPS:2 * GROUPS], ALU.add).then_inc(w_ready, 1)
            dve.tensor_tensor(vb_all[:, :], vb_in[:, :], ps_t[:, 1, D:2 * D], ALU.add).then_inc(w_ready, 1)
            dve.wait_ge(w_ready, 7)
            dve.wait_ge(filled, 3)
            dve.sem_inc(w_ready, 2)

            def norm_part(part, s, slot):
                if part == "moments":
                    wait(dve, rope_done, s, 2)
                    for t in range(TT):
                        dve.bn_stats(stats[:, t, :], h0[:, t, :]).then_inc(stats_done.sem, 1)
                    wait_alone(dve, alone, stats_done.sem, stats_done.at(s, TT))
                    for t in range(TT):
                        dve.bn_aggr(moments[:, t, :], stats[:, t, :]).then_inc(moments_done.sem, 1)
                if part == "x":
                    wait(dve, rstd_done, s, 1)
                    wait(dve, biased, s, 0)
                    for t in range(TT):
                        done = dve.tensor_scalar(x[:, t, :], h0[:, t, :], moments[:, t, 0:1], rstd[:, t:t + 1],
                                                 ALU.subtract, ALU.mult).then_inc(x_done.sem, 1)
                    dve.wait_ge(x_done.sem, x_done.at(s, TT))
                    dve.sem_inc(h0_read.sem, 1)
                if part == "moments2":
                    for t in range(TT):
                        dve.bn_stats(stats2[:, t, :], x[:, t, :]).then_inc(stats2_done.sem, 1)
                    wait_alone(dve, alone, stats2_done.sem, stats2_done.at(s, TT))
                    for t in range(TT):
                        dve.bn_aggr(moments2[:, t, :], stats2[:, t, :]).then_inc(moments2_done.sem, 1)
                if part == "xn":
                    wait(dve, rstd2_done, s, 1)
                    for t in range(TT):
                        dve.tensor_scalar(xn[:, t, :], x[:, t, :], moments2[:, t, 0:1], rstd2[:, t:t + 1],
                                          ALU.subtract, ALU.mult).then_inc(xn_done.sem, 1)

            def work(name, s, slot, last):
                k, n = kind(name), int(name[-1])
                bank = ps_w[:, ring.bank(s, name, last)]
                of, vslot = (0, 0) if s is None else (s + 1, 1 - slot)
                if k == "turn":
                    wait(dve, turn_hi, of, n + 1)
                    dve.tensor_tensor(xT_lo[:, n, :], bank, xT_hi[:, n, :], ALU.subtract).then_inc(ring.free["dve"], 1)
                if k == "v":
                    wait_filled(dve, ring, s, name, last)
                    dve.tensor_tensor(v_wide[:, vslot, 2 * n:2 * n + 2, :, 0:HD],
                                      bank.rearrange("p (t h d) -> p t h d", t=2, h=H),
                                      vb_all[:, :].rearrange("p (h d) -> p h d", h=H).unsqueeze(1).broadcast_to([P, 2, H, HD]),
                                      ALU.add
                                      ).then_inc(ring.free["dve"], 1)
                if k == "qsel":
                    wait_filled(dve, ring, s, name, last)
                    dve.tensor_copy(q_rows[0:P // 2, 2 * n, :], bank[0:P // 2, :])
                    dve.tensor_copy(q_rows[P // 2:P, 2 * n + 1, :], bank[P // 2:P, :]).then_inc(ring.free["dve"], 1)
                if k == "norm":
                    normalise(bank, s - 1 if n == QUADS - 1 else s, n, name, last, s)
                if k == "out":
                    wait_filled(dve, ring, s, name, last)
                    wait(dve, biased, s, 0)
                    dst = xb[:, 1 - slot, 2 * n:2 * n + 2, :]
                    dve.tensor_tensor(dst, dst, bank.rearrange("p (t d) -> p t d", t=2), ALU.add
                                      ).then_inc(ring.free["dve"], 1)

            def maximum(s, h, p):
                wait(dve, summed, s, NP * h + p + 1)
                for qt in PIECES[p]:
                    first = AT[PIECES[p][0]]
                    src = ps_s[:, (NP * h + p) % 2, (AT[qt] - first) * P:(AT[qt] - first + qt + 1) * P]
                    done = dve.tensor_reduce(neg_max[:, h % 2, qt:qt + 1], src, AX_X, ALU.max, negate=True)
                done.then_inc(max_done.sem, 1)

            def take(s, h, p):
                wait(dve, turned, s, NP * h + p + 1)
                n = len(TURNED[p]) * P
                piece = slice(TURNED_AT[p] * P, TURNED_AT[p] * P + n)
                dve.tensor_copy(exps[:, 2 + h % 2, piece], ps_t[:, (NP * h + p) % 2, 0:n]).then_inc(taken["dve"].sem, 1)

            def invert(s, quad):
                wait(dve, exp_done, s, NP * 4 * (quad + 1))
                heads = slice(4 * quad, 4 * quad + 4)
                dve.reciprocal(recip[:, heads, :], denom[:, heads, :]).then_inc(recip_done.sem, 1)

            def normalise(bank, s, quad, name, last, step):
                wait(dve, o_summed, s, quad + 1)
                wait(dve, o_split, s, quad)
                wait_filled(dve, ring, step, name, last)
                dve.tensor_copy(spread, bank).then_inc(ring.free["dve"], 1)
                wait_read(dve, ring, step, name, last)
                dve.tensor_tensor(o, ps_o[:, quad % 2, :], spread, ALU.mult).then_inc(o_done.sem, 1)

            norm_part("moments", 0, 0)
            norm_part("x", 0, 0)
            norm_part("moments2", 0, 0)
            norm_part("xn", 0, 0)
            for name in FRONT:
                work(name, None, 0, False)
            for p in range(NP):
                maximum(0, 0, p)

            def step(s, slot, first, last):
                for h in range(H):
                    more = h < H - 1 or not last
                    nxt = (s, h + 1) if h < H - 1 else (s + 1, 0)
                    if more:
                        maximum(*nxt, 0)
                    if h:
                        do_work(work, s, slot, first, last, h - 1, 1)
                        do_work(work, s, slot, first, last, h - 1, 2)
                    if more:
                        maximum(*nxt, 1)
                    take(s, h, 1)
                    if more:
                        maximum(*nxt, 2)
                    if h % 4 == 3:
                        invert(s, h // 4)
                    if h in NORM_AT and not last:
                        norm_part(NORM_AT[h], s + 1, 1 - slot)
                    do_work(work, s, slot, first, last, h, 0)
                do_work(work, s, slot, first, last, H - 1, 1)
                do_work(work, s, slot, first, last, H - 1, 2)

            over_steps(dve, step, 1)
            normalise(last_bank("norm3"), SEQS - 1, QUADS - 1, "last_norm3", True, SEQS - 1)
            wait(dve, biased, SEQS - 1, 1)
            for n in range(2):
                wait_filled(dve, ring, SEQS - 1, f"last_out{n}", True)
                dst = xb[:, (SEQS - 1) % 2, 2 * n:2 * n + 2, :]
                dve.tensor_tensor(dst, dst, last_bank(f"out{n}").rearrange("p (t d) -> p t d", t=2), ALU.add
                                  ).then_inc(ring.free["dve"], 1)

        @block.tensor
        def _(pe):
            for i in range(3):
                pe.wait_ge(factors_in[i], 32)
                buffer = factor_u1 if i == 1 else factor_u0
                for h in range(H):
                    for f in range(FB):
                        mm = pe.matmul(fused_bank(i)[:, f, h * HD:(h + 1) * HD], buffer[0:R, h, f * P:(f + 1) * P],
                                       factor_v[0:R, i, h, :], start=True, stop=True, skip_group_check=True)
                mm.then_inc(fused, 1)
            pe.wait_ge(wide_made, 4)
            for q in range(QUADS):
                for b in range(2):
                    mm = pe.matmul(fused_out[:, q, :], factor_padded[0:ROB, b, 4 * q:4 * q + 4, :].rearrange("p h w -> p (h w)"),
                                   factor_ov[0:ROB, b, :], start=(b == 0), stop=(b == 1), skip_group_check=True)
            mm.then_inc(fused, 1)
            pe.wait_ge(w_copied, 6)
            for i in range(2):
                for m in range(GROUPS):
                    for f in range(FB):
                        pe.matmul(ps_t[:, 1, 2 * i + m:2 * i + m + 1], w_raw[:, i, f, m * P:(m + 1) * P], ln[:, 1, f:f + 1],
                                  start=(f == 0), stop=(f == FB - 1), skip_group_check=True)
            for f in range(FB):
                mm = pe.matmul(ps_t[:, 1, D:2 * D], ln_b_wide[:, f, :], w_raw[:, 2, f, :], start=(f == 0), stop=(f == FB - 1),
                               skip_group_check=True)
            mm.then_inc(bias_fused, 1)
            pe.wait_ge(w_ready, 9)
            pe.wait_ge(consts16, 3)

            def work(name, s, slot, last):
                k, n = kind(name), int(name[-1])
                bank = ps_w[:, ring.bank(s, name, last)]
                of = 0 if s is None else s + 1
                wait_free(pe, ring, s, name, last)
                if k == "turn":
                    wait(pe, xn_done, of, TT)
                    for t in range(TT):
                        mm = pe.transpose(bank[:, t * P:(t + 1) * P], xn[:, t, n * P:(n + 1) * P], ident[:, :])
                if k in ("q", "k"):
                    i = "qk".index(k)
                    wait_read(pe, ring, s, "turn1", last)
                    for f in range(FB):
                        mm = split_product(pe, bank, w_hi[:, i, f, n * P:(n + 1) * P], w_lo[:, i, f, n * P:(n + 1) * P],
                                           xT_hi[:, f, :], xT_lo[:, f, :], f == 0, f == FB - 1)
                if k == "v":
                    for t in range(2):
                        tok = slice((2 * n + t) * P, (2 * n + t + 1) * P)
                        for f in range(FB):
                            mm = split_product(pe, bank[:, t * D:(t + 1) * D], xT_hi[:, f, tok], xT_lo[:, f, tok],
                                               w_hi[:, 2, f, :], w_lo[:, 2, f, :], f == 0, f == FB - 1, True)
                if k in ("qsel", "ksel"):
                    i = "qk".index(k[0])
                    g, j = n // (GH // 2), n % (GH // 2)
                    wait(pe, qk_split, of, 2 * g + i + 1)
                    pe.matmul(bank, sel[:, 2 * i, j, :], qk_hi[:, i, g, :], start=True, stop=False)
                    mm = pe.matmul(bank, sel[:, 2 * i + 1, j, :], qk_lo[:, i, g, :], start=False, stop=True)
                if k == "norm":
                    mm = spread_sums(bank, s - 1 if n == QUADS - 1 else s, n)
                if k == "out":
                    if n == 0:
                        wait(pe, o_split, s - 1, QUADS)
                    mm = out(bank, n)
                mm.then_inc(ring.full, 1)

            def spread_sums(bank, s, quad):
                wait(pe, widened, s, quad + 1)
                for qt in range(TT):
                    mm = pe.transpose(bank[:, qt * P:(qt + 1) * P], wide[:, qt * P:(qt + 1) * P], ident[:, :])
                return mm

            def out(bank, n):
                for t in range(2):
                    tok = slice((2 * n + t) * P, (2 * n + t + 1) * P)
                    for q in range(QUADS):
                        mm = split_product(pe, bank[:, t * D:(t + 1) * D], o_hi[:, q, tok], o_lo[:, q, tok],
                                           wo_hi[:, q, :], wo_lo[:, q, :], q == 0, q == QUADS - 1, True)
                return mm

            def scores(s, h, p, made_in):
                if h % 2 == 0 and p == 0:
                    wait_read(pe, ring, made_in, f"ksel{h // 2}", False)
                    wait_read(pe, ring, made_in, f"qsel{h // 2}", False)
                wait(pe, exp_done, s, NP * h + p - 1)
                for qt in PIECES[p]:
                    at = (AT[qt] - AT[PIECES[p][0]]) * P
                    pe.matmul(ps_s[:, (NP * h + p) % 2, at:at + (qt + 1) * P], q_rows[:, h, qt * P:(qt + 1) * P],
                              k_rows[:, h // 2, 0:(qt + 1) * P], start=True, stop=False, skip_group_check=True)
                    mm = pe.matmul(ps_s[:, (NP * h + p) % 2, at + qt * P:at + (qt + 1) * P], ident16[:, :], mask16[:, :],
                                   start=False, stop=True, skip_group_check=True)
                mm.then_inc(summed.sem, 1)

            def turn(s, h, p):
                if p == 0:
                    wait(pe, exp_done, s, NP * (h + 1))
                hb, pb = (h - 1, p + 1) if p < 2 else (h, 0)
                by, n = taken_at(hb, pb)
                wait(pe, by, s, n)
                for i, (kt, qt) in enumerate(TURNED[p]):
                    c = (AT[qt] + kt) * P
                    mm = pe.transpose(ps_t[:, (NP * h + p) % 2, i * P:(i + 1) * P], exps[:, h % 2, c:c + P], ident[:, :])
                mm.then_inc(turned.sem, 1)

            def weigh(s, slot, pair):
                if pair % 4 == 0:
                    wait(pe, o_done, s, pair // 4 - 1)
                for p in range(NP):
                    by, n = taken_at(pair + 1, p)
                    wait(pe, by, s, n)
                for kt in range(TT):
                    c = slice(KEYS_AT[kt] * P, (KEYS_AT[kt] + TT - kt) * P)
                    for h in (pair, pair + 1):
                        rows = slice(VW * (h % 4), VW * (h % 4) + VW)
                        mm = pe.matmul(ps_o[rows, h // 4 % 2, kt * P:SEQ], v_wide[:, slot, kt, h, :], exps[:, 2 + h % 2, c],
                                       start=(kt == 0), stop=(kt == TT - 1), skip_group_check=True)
                if pair % 4 == 2:
                    mm.then_inc(o_summed.sem, 1)

            for name in FRONT:
                work(name, None, 0, False)
            wait_read(pe, ring, None, f"ksel{PAIRS - 1}", False)
            wait_read(pe, ring, None, f"qsel{PAIRS - 1}", False)
            for p in range(NP):
                scores(0, 0, p, None)

            def step(s, slot, first, last):
                for h in range(H):
                    more = h < H - 1 or not last
                    nxt, made_in = ((s, h + 1), None if first else s - 1) if h < H - 1 else ((s + 1, 0), s)
                    if more:
                        scores(*nxt, 0, made_in)
                        scores(*nxt, 1, made_in)
                    if h and h % 2 == 0:
                        weigh(s, slot, h - 2)
                    turn(s, h, 0)
                    turn(s, h, 1)
                    if more:
                        scores(*nxt, 2, made_in)
                    do_work(work, s, slot, first, last, h, 0)
                    turn(s, h, 2)
                    do_work(work, s, slot, first, last, h, 1)
                    if h == H - 1:
                        weigh(s, slot, h - 1)
                    do_work(work, s, slot, first, last, h, 2)

            over_steps(pe, step, 1)
            wait_free(pe, ring, SEQS - 1, "last_norm3", True)
            spread_sums(last_bank("norm3"), SEQS - 1, QUADS - 1).then_inc(ring.full, 1)
            wait(pe, o_split, SEQS - 1, QUADS)
            for n in range(2):
                wait_free(pe, ring, SEQS - 1, f"last_out{n}", True)
                out(last_bank(f"out{n}"), n).then_inc(ring.full, 1)


def mlp_phase(nc, ident_dram, x_in, res_in, ln_cols, fc1_u, fc1_v, fc1_b_col, fc2_u, fc2_v, fc2_b, x_out):
    F = fc1_v.shape[1]
    R = fc1_u.shape[1]
    K = F // P
    RING, PS_RING = 4, 2
    FINISH_AT = 3
    NORM_WITH = [0, 2]
    TURN_AT = [3, 4]
    RANK_AT = 5
    TAKE_AT = [min(k + LOOKAHEAD, K - 1) for k in TURN_AT]
    assert R == P

    with ExitStack() as ctx:
        def sb(name, shape, dt=F32):
            return ctx.enter_context(nc.sbuf_tensor("mlp_" + name, shape, dt))

        def psum(name, shape):
            return ctx.enter_context(nc.psum_tensor("mlp_" + name, shape, F32))

        def sem(name):
            return nc.alloc_semaphore(name="mlp_" + name)

        def signal(name, per_seq, credit=0, unit=1):
            return Signal(ctx, nc, "mlp_" + name, per_seq, credit, unit)

        u1_raw, u1_scaled = sb("u1_raw", [P, FB, R]), sb("u1_scaled", [P, FB, R])
        v1_raw, u2_raw, v2_raw = sb("v1_raw", [P, F]), sb("u2_raw", [P, K, R]), sb("v2_raw", [P, D])
        u1_hi, u1_lo = sb("u1_hi", [P, FB, R], F32R), sb("u1_lo", [P, FB, R], F32R)
        v1_hi, v1_lo = sb("v1_hi", [P, F], F32R), sb("v1_lo", [P, F], F32R)
        u2_hi, u2_lo = sb("u2_hi", [P, K, R], F32R), sb("u2_lo", [P, K, R], F32R)
        v2_hi, v2_lo = sb("v2_hi", [P, D], F32R), sb("v2_lo", [P, D], F32R)
        ln = sb("ln", [P, 2, FB])
        rank_bias = sb("rank_bias", [P, 1])
        fc1_b = sb("fc1_b", [P, K])
        fc2_b_all = sb("fc2_b_all", [P, D])
        ident = sb("ident", [P, P])
        x = sb("x", [P, 2, TT, D])
        res = sb("res", [P, 2, TT, D])
        y = sb("y", [P, 2, TT, D])
        stats = sb("stats", [P, TT, 6])
        moments = sb("moments", [P, TT, 2])
        var_eps = sb("var_eps", [P, TT])
        minus_half = sb("minus_half", [P, TT])
        rstd = sb("rstd", [P, TT])
        xn = sb("xn", [P, TT, D])
        xT_hi, xT_lo = sb("xT_hi", [P, FB, SEQ], F32R), sb("xT_lo", [P, FB, SEQ], F32R)
        m1, m1_hi, m1_lo = sb("m1", [P, SEQ]), sb("m1_hi", [P, SEQ], F32R), sb("m1_lo", [P, SEQ], F32R)
        m2_hi, m2_lo = sb("m2_hi", [P, SEQ], F32R), sb("m2_lo", [P, SEQ], F32R)
        hid = sb("hid", [P, RING, SEQ])
        hid_hi, hid_lo = sb("hid_hi", [P, RING, SEQ], F32R), sb("hid_lo", [P, RING, SEQ], F32R)

        ps_hid = psum("ps_hid", [P, PS_RING, SEQ])
        ps_m1, ps_m2, ps_turn = psum("ps_m1", [P, SEQ]), psum("ps_m2", [P, SEQ]), psum("ps_turn", [P, SEQ])
        ps_out = psum("ps_out", [P, TT, D])

        consts_in, filled = sem("consts_in"), sem("filled")
        scaled, bias_summed, halves_hi, w_ready = sem("scaled"), sem("bias_summed"), sem("halves_hi"), sem("w_ready")
        x_loads = Loads(ctx, nc, "mlp_x_loads")
        res_loads = Loads(ctx, nc, "mlp_res_loads")
        y_stored = signal("y_stored", 1, credit=2, unit=16)
        alone_sp = sem("waits_of_sp")
        alone, alone_pool = sem("waits_of_dve"), sem("waits_of_pool")
        stats_done = signal("stats_done", TT)
        moments_done = signal("moments_done", TT)
        eps_added = signal("eps_added", 1)
        rstd_done = signal("rstd_done", 1)
        xn_done = signal("xn_done", TT)
        x_added = signal("x_added", 1)
        biased = signal("biased", 1)
        turned = signal("turned", FB)
        turn_hi = signal("turn_hi", FB)
        turn_lo = signal("turn_lo", FB, credit=1)
        m1_summed = signal("m1_summed", 1)
        m1_hi_done = signal("m1_hi_done", 1)
        m1_split = signal("m1_split", 1)
        hid_summed = signal("hid_summed", K)
        hid_act = signal("hid_act", K, credit=RING)
        hid_split = signal("hid_split", K, credit=RING)
        hid_used = signal("hid_used", K, credit=RING)
        m2_hi_done = signal("m2_hi_done", 1)
        m2_split = signal("m2_split", 1, credit=1)
        out_summed = signal("out_summed", TT // 2)
        out_done = signal("out_done", TT // 2, credit=TT // 2)

        def flat(w):
            return w[:, :] if len(w.shape) == 2 else w[:, :, :].rearrange("p a b -> p (a b)")

        block = ctx.enter_context(nc.Block())
        CONSTS = 8

        @block.sync
        def _(sp):
            def load_x(s, slot):
                sp.dma_start(x[:, slot], tiles_of(x_in, s)).then_inc(x_loads.sems[slot], 16)

            def load_res(s, slot):
                sp.dma_start(res[:, slot], tiles_of(res_in, s)).then_inc(res_loads.sems[slot], 16)

            give_credits(sp, [y_stored])
            load_x(0, 0)
            sp.dma_start(u1_raw[:, :, :], fc1_u.rearrange("(f p) r -> p f r", p=P)).then_inc(consts_in, 16)
            sp.dma_start(ln[:, :, :], ln_cols.rearrange("p (k f) -> p k f", f=FB)).then_inc(consts_in, 16)
            sp.dma_start(ident[:, :], ident_dram).then_inc(consts_in, 16)
            sp.dma_start(v1_raw[:, :], fc1_v).then_inc(consts_in, 16)
            sp.dma_start(u2_raw[:, :, :], fc2_u.rearrange("(k p) r -> p k r", p=P)).then_inc(consts_in, 16)
            sp.dma_start(v2_raw[:, :], fc2_v).then_inc(consts_in, 16)
            sp.dma_start(fc1_b[:, :], fc1_b_col).then_inc(consts_in, 16)
            sp.dma_start(fc2_b_all[:, :], fc2_b.partition_broadcast(P)).then_inc(consts_in, 16)
            load_res(0, 0)
            load_x(1, 1)
            load_res(1, 1)

            def store(s, slot):
                wait_alone(sp, alone_sp, out_done.sem, out_done.at(s, TT // 2))
                wait_alone(sp, alone_sp, y_stored.sem, y_stored.at(s, 0))
                sp.dma_start(tiles_of(x_out, s), y[:, slot]).then_inc(y_stored.sem, 16)

            def step(s, slot, first, last):
                if not first:
                    store(s - 1, 1 - slot)
                    if not (isinstance(s, int) and s + 1 >= SEQS):
                        load_res(s + 1, 1 - slot)
                if not (isinstance(s, int) and s + 2 >= SEQS):
                    wait_alone(sp, alone_sp, xn_done.sem, xn_done.at(s, TT))
                    wait_alone(sp, alone_sp, x_added.sem, x_added.at(s, 1))
                    load_x(s + 2, slot)

            over_steps(sp, step, 3)
            store(SEQS - 1, (SEQS - 1) % 2)
            wait(sp, y_stored, SEQS, 0)

        @block.gpsimd
        def _(pool):
            pool.memset(minus_half[:, :], -0.5).then_inc(filled, 1)
            pool.wait_ge(filled, 1)
            pool.wait_ge(consts_in, 16 * CONSTS)

            def norm(s):
                wait_alone(pool, alone_pool, moments_done.sem, moments_done.at(s, TT))
                pool.tensor_scalar(var_eps[:, :], moments[:, :, 1], LN_EPS, None, ALU.add).then_inc(eps_added.sem, 1)
                wait(pool, eps_added, s, 1)
                pool.tensor_tensor(rstd[:, :], var_eps[:, :], minus_half[:, :], ALU.pow).then_inc(rstd_done.sem, 1)

            norm(0)

            def step(s, slot, last):
                if not last:
                    norm(s + 1)
                res_loads.wait(pool, s, slot)
                x_loads.wait(pool, s, slot)
                pool.tensor_tensor(res[:, slot], res[:, slot], x[:, slot], ALU.add).then_inc(x_added.sem, 1)
                wait(pool, x_added, s, 1)
                pool.tensor_tensor(res[:, slot], res[:, slot], fc2_b_all[:, :].unsqueeze(1).broadcast_to([P, TT, D]),
                                   ALU.add).then_inc(biased.sem, 1)

            over_sequences(pool, step)

        @block.scalar
        def _(act):
            give_credits(act, [hid_act])
            act.wait_ge(scaled, FB)
            for src, hi in ((u1_scaled, u1_hi), (v1_raw, v1_hi), (u2_raw, u2_hi), (v2_raw, v2_hi)):
                act.activation(flat(hi), flat(src), ACT.Copy).then_inc(halves_hi, 1)

            def turn(s, f):
                wait(act, turned, s, f + 1)
                act.activation(xT_hi[:, f, :], ps_turn[:, :], ACT.Copy).then_inc(turn_hi.sem, 1)

            def take_m1(s):
                wait(act, m1_summed, s, 1)
                act.activation(m1[:, :], ps_m1[:, :], ACT.Identity, bias=rank_bias[:, 0:1])
                act.activation(m1_hi[:, :], ps_m1[:, :], ACT.Identity, bias=rank_bias[:, 0:1]).then_inc(m1_hi_done.sem, 1)

            for f in range(FB):
                turn(0, f)
            act.wait_ge(w_ready, 5)
            take_m1(0)

            def step(s, slot, last):
                for k in range(K):
                    wait(act, hid_summed, s, k + 1)
                    wait(act, hid_split, s, k + 1 - RING)
                    act.activation(hid[:, k % RING, :], ps_hid[:, k % PS_RING, :], ACT.Gelu_apprx_tanh,
                                   bias=fc1_b[:, k:k + 1])
                    wait(act, hid_used, s, k + 1 - RING)
                    act.activation(hid_hi[:, k % RING, :], ps_hid[:, k % PS_RING, :], ACT.Gelu_apprx_tanh,
                                   bias=fc1_b[:, k:k + 1]).then_inc(hid_act.sem, 1)
                    for f in range(FB):
                        if k == TAKE_AT[f] and not last:
                            turn(s + 1, f)
                    if k == K - 1 and not last:
                        take_m1(s + 1)
                wait(act, hid_used, s, K)
                act.activation(m2_hi[:, :], ps_m2[:, :], ACT.Copy).then_inc(m2_hi_done.sem, 1)

            over_sequences(act, step)

        @block.vector
        def _(dve):
            give_credits(dve, [turn_lo, hid_split, m2_split, out_done])
            dve.wait_ge(consts_in, 16 * CONSTS)
            for f in range(FB):
                dve.tensor_scalar(u1_scaled[:, f, :], u1_raw[:, f, :], ln[:, 0, f:f + 1], None,
                                  ALU.mult).then_inc(scaled, 1)
            dve.wait_ge(bias_summed, 1)
            dve.tensor_copy(rank_bias[:, :], ps_m1[:, 0:1]).then_inc(w_ready, 1)
            dve.wait_ge(scaled, FB)
            for i, (src, hi, lo) in enumerate(((u1_scaled, u1_hi, u1_lo), (v1_raw, v1_hi, v1_lo), (u2_raw, u2_hi, u2_lo),
                                               (v2_raw, v2_hi, v2_lo))):
                dve.wait_ge(halves_hi, i + 1)
                dve.tensor_tensor(flat(lo), flat(src), flat(hi), ALU.subtract).then_inc(w_ready, 1)

            def norm_part(s, slot, n):
                if n == 0:
                    x_loads.wait(dve, s, slot)
                    for t in range(TT):
                        dve.bn_stats(stats[:, t, :], x[:, slot, t, :]).then_inc(stats_done.sem, 1)
                    wait_alone(dve, alone, stats_done.sem, stats_done.at(s, TT))
                    for t in range(TT):
                        dve.bn_aggr(moments[:, t, :], stats[:, t, :]).then_inc(moments_done.sem, 1)
                if n == 1:
                    wait(dve, rstd_done, s, 1)
                    for t in range(TT):
                        dve.tensor_scalar(xn[:, t, :], x[:, slot, t, :], moments[:, t, 0:1], rstd[:, t:t + 1],
                                          ALU.subtract, ALU.mult).then_inc(xn_done.sem, 1)

            def turn(s, f):
                wait(dve, turn_hi, s, f + 1)
                dve.tensor_tensor(xT_lo[:, f, :], ps_turn[:, :], xT_hi[:, f, :], ALU.subtract).then_inc(turn_lo.sem, 1)

            def take_m1(s):
                wait(dve, m1_hi_done, s, 1)
                dve.tensor_tensor(m1_lo[:, :], m1[:, :], m1_hi[:, :], ALU.subtract).then_inc(m1_split.sem, 1)

            for n in range(2):
                norm_part(0, 0, n)
            for f in range(FB):
                turn(0, f)
            take_m1(0)

            def finish(s, slot):
                wait(dve, biased, s, 1)
                wait(dve, y_stored, s, -1)
                for h in range(TT // 2):
                    wait(dve, out_summed, s, h + 1)
                    part = slice(2 * h, 2 * h + 2)
                    dve.tensor_tensor(y[:, slot, part, :], ps_out[:, part, :], res[:, slot, part, :],
                                      ALU.add).then_inc(out_done.sem, 1)

            def step(s, slot, first, last):
                for k in range(K):
                    wait(dve, hid_act, s, k + 1)
                    dve.tensor_tensor(hid_lo[:, k % RING, :], hid[:, k % RING, :], hid_hi[:, k % RING, :],
                                      ALU.subtract).then_inc(hid_split.sem, 1)
                    if k == FINISH_AT and not first:
                        finish(s - 1, 1 - slot)
                    if k in NORM_WITH and not last:
                        norm_part(s + 1, 1 - slot, NORM_WITH.index(k))
                    for f in range(FB):
                        if k == TAKE_AT[f] and not last:
                            turn(s + 1, f)
                if not last:
                    take_m1(s + 1)
                wait(dve, m2_hi_done, s, 1)
                dve.tensor_tensor(m2_lo[:, :], ps_m2[:, :], m2_hi[:, :], ALU.subtract).then_inc(m2_split.sem, 1)

            over_steps(dve, step)
            finish(SEQS - 1, (SEQS - 1) % 2)

        @block.tensor
        def _(pe):
            give_credits(pe, [hid_used])
            pe.wait_ge(consts_in, 16 * CONSTS)
            for f in range(FB):
                mm = pe.matmul(ps_m1[:, 0:1], u1_raw[:, f, :], ln[:, 1, f:f + 1], start=(f == 0), stop=(f == FB - 1))
            mm.then_inc(bias_summed, 1)

            def turn(s, f):
                wait(pe, xn_done, s, TT)
                wait(pe, turn_lo, s, f)
                for t in range(TT):
                    last = pe.transpose(ps_turn[:, t * P:(t + 1) * P], xn[:, t, f * P:(f + 1) * P], ident[:, :])
                last.then_inc(turned.sem, 1)

            def rank_in(s):
                wait(pe, turn_lo, s, FB)
                wait(pe, m1_split, s, 0)
                for f in range(FB):
                    mm = split_product(pe, ps_m1[:, :], u1_hi[:, f, :], u1_lo[:, f, :], xT_hi[:, f, :], xT_lo[:, f, :],
                                       f == 0, f == FB - 1)
                mm.then_inc(m1_summed.sem, 1)

            for f in range(FB):
                turn(0, f)
            pe.wait_ge(w_ready, 5)
            wait(pe, turn_lo, 0, FB)
            for f in range(FB):
                mm = split_product(pe, ps_m1[:, :], u1_hi[:, f, :], u1_lo[:, f, :], xT_hi[:, f, :], xT_lo[:, f, :],
                                   f == 0, f == FB - 1)
            mm.then_inc(m1_summed.sem, 1)

            def up(s, k):
                if k == 0:
                    wait(pe, m1_split, s, 1)
                wait(pe, hid_act, s, k + 1 - PS_RING)
                h = slice(k * P, (k + 1) * P)
                split_product(pe, ps_hid[:, k % PS_RING, :], v1_hi[:, h], v1_lo[:, h], m1_hi[:, :], m1_lo[:, :],
                              True, True).then_inc(hid_summed.sem, 1)

            def down(s, k):
                wait(pe, hid_split, s, k + 1)
                if k == 0:
                    wait(pe, m2_split, s, 0)
                split_product(pe, ps_m2[:, :], u2_hi[:, k, :], u2_lo[:, k, :], hid_hi[:, k % RING, :],
                              hid_lo[:, k % RING, :], k == 0, k == K - 1).then_inc(hid_used.sem, 1)

            def rank_out(s):
                wait(pe, m2_split, s, 1)
                wait(pe, out_done, s, 0)
                for t in range(TT):
                    tok = slice(t * P, (t + 1) * P)
                    mm = split_product(pe, ps_out[:, t, :], m2_hi[:, tok], m2_lo[:, tok], v2_hi[:, :], v2_lo[:, :],
                                       True, True)
                    if t % 2:
                        mm.then_inc(out_summed.sem, 1)

            def step(s, slot, first, last):
                for k in range(LOOKAHEAD):
                    up(s, k)
                if not first:
                    rank_out(s - 1)
                for k in range(K):
                    if k + LOOKAHEAD < K:
                        up(s, k + LOOKAHEAD)
                    down(s, k)
                    if k in TURN_AT and not last:
                        turn(s + 1, TURN_AT.index(k))
                    if k == RANK_AT and not last:
                        rank_in(s + 1)

            over_steps(pe, step)
            rank_out(SEQS - 1)


def ffn_phase(nc, ident_dram, x_in, w_up_t, w_down_t, x_out):
    F = w_up_t.shape[1]
    K = F // P
    RING, PS_RING = 4, 2
    NORM_WITH = [0, 2, 5]
    TURN_AT = [5, 6]
    TAKE_AT = [min(k + LOOKAHEAD, K - 1) for k in TURN_AT]
    COPY_AT = 6
    FINISH_AT = 2

    with ExitStack() as ctx:
        def sb(name, shape, dt=F32):
            return ctx.enter_context(nc.sbuf_tensor(name, shape, dt))

        def psum(name, shape):
            return ctx.enter_context(nc.psum_tensor(name, shape, F32))

        def sem(name):
            return nc.alloc_semaphore(name=name)

        def signal(name, per_seq, credit=0, unit=1):
            return Signal(ctx, nc, name, per_seq, credit, unit)

        w_raw = sb("ffn_w_raw", [P, 2, FB * F])
        w_abs = sb("ffn_w_abs", [P, FB * F])
        w_sum = sb("ffn_w_sum", [P, 2])
        limit = sb("ffn_limit", [P, 2])
        minus_limit = sb("ffn_minus_limit", [P, 2])
        below = sb("ffn_below", [P, 2, FB * F])
        w_up = sb("ffn_w_up", [P, FB, F], F32R)
        w_down = sb("ffn_w_down", [P, K, D], F32R)
        ones = sb("ffn_ones", [P, P])
        ident = sb("ffn_ident", [P, P])
        x = sb("ffn_x", [P, 2, TT, D])
        y = sb("ffn_y", [P, 2, TT, D])
        stats = sb("ffn_stats", [P, TT, 6])
        moments = sb("ffn_moments", [P, TT, 2])
        var_eps = sb("ffn_var_eps", [P, TT])
        minus_half = sb("ffn_minus_half", [P, TT])
        half = sb("ffn_half", [P, TT])
        rstd = sb("ffn_rstd", [P, TT])
        square_work = sb("ffn_square_work", [P, D])
        x_sq = sb("ffn_x_sq", [P, TT])
        x_ms = sb("ffn_x_ms", [P, TT])
        x_rms = sb("ffn_x_rms", [P, TT])
        x_rms_eps = sb("ffn_x_rms_eps", [P, TT])
        x_scale = sb("ffn_x_scale", [P, TT])
        h_ms = sb("ffn_h_ms", [P, TT])
        h_rms = sb("ffn_h_rms", [P, TT])
        h_rms_eps = sb("ffn_h_rms_eps", [P, TT])
        h_scale = sb("ffn_h_scale", [P, TT])
        xn = sb("ffn_xn", [P, TT, D])
        xr = sb("ffn_xr", [P, TT, D])
        xT_hi = sb("ffn_xT_hi", [P, 2, FB, SEQ], F32R)
        xT_lo = sb("ffn_xT_lo", [P, 2, FB, SEQ], F32R)
        hid = sb("ffn_hid", [P, RING, SEQ])
        hid_sq = sb("ffn_hid_sq", [P, RING, SEQ])
        hid_hi = sb("ffn_hid_hi", [P, RING, SEQ], F32R)
        hid_lo = sb("ffn_hid_lo", [P, RING, SEQ], F32R)

        ps_hid = psum("ffn_ps_hid", [P, PS_RING, SEQ])
        ps_out = psum("ffn_ps_out", [P, 2, TT, D])
        ps_turn = psum("ffn_ps_turn", [P, SEQ])
        ps_sq = psum("ffn_ps_sq", [P, SEQ])

        consts_in, w_in = sem("ffn_consts_in"), sem("ffn_w_in")
        filled, abs_done, total_done, limit_done = sem("ffn_filled"), sem("ffn_abs_done"), sem("ffn_total_done"), sem("ffn_limit_done")
        below_done, w_ready = sem("ffn_below_done"), sem("ffn_w_ready")
        x_loads = Loads(ctx, nc, "ffn_x_loads")
        y_stored = signal("ffn_y_stored", 1, credit=2, unit=16)
        alone, alone_pool, alone_sp = (nc.alloc_semaphore(name="ffn_waits_of_" + e) for e in ("dve", "pool", "sp"))
        x_copied = signal("ffn_x_copied", 1)
        stats_done = signal("ffn_stats_done", TT)
        moments_done = signal("ffn_moments_done", TT)
        eps_added = signal("ffn_eps_added", 1)
        rstd_done = signal("ffn_rstd_done", 1)
        xn_done = signal("ffn_xn_done", TT)
        x_sq_done = signal("ffn_x_sq_done", TT)
        x_ms_done = signal("ffn_x_ms_done", 1)
        x_rms_done = signal("ffn_x_rms_done", 1)
        x_scale_part = signal("ffn_x_scale_part", 2)
        xr_done = signal("ffn_xr_done", TT)
        turned = signal("ffn_turned", FB)
        turn_hi = signal("ffn_turn_hi", FB)
        turn_lo = signal("ffn_turn_lo", FB, credit=1)
        hid_summed = signal("ffn_hid_summed", K)
        hid_act = signal("ffn_hid_act", K, credit=RING)
        sq_done = signal("ffn_sq_done", K, credit=RING)
        hid_split = signal("ffn_hid_split", K, credit=RING)
        hid_used = signal("ffn_hid_used", K, credit=RING)
        sq_summed = signal("ffn_sq_summed", K, credit=RING)
        h_ms_done = signal("ffn_h_ms_done", 1, credit=1)
        h_rms_done = signal("ffn_h_rms_done", 1)
        h_scale_part = signal("ffn_h_scale_part", 2)
        out_done = signal("ffn_out_done", TT, credit=2 * TT)

        block = ctx.enter_context(nc.Block())

        @block.sync
        def _(sp):
            def load_x(s, slot):
                sp.dma_start(x[:, slot], tiles_of(x_in, s)).then_inc(x_loads.sems[slot], 16)

            give_credits(sp, [y_stored])
            sp.dma_start(w_raw[:, 0, :].rearrange("p (f h) -> p f h", f=FB),
                         w_up_t.rearrange("(f p) h -> p f h", p=P)).then_inc(w_in, 16)
            load_x(0, 0)
            sp.dma_start(w_raw[:, 1, :].rearrange("p (k d) -> p k d", k=K),
                         w_down_t.rearrange("(k p) d -> p k d", p=P)).then_inc(w_in, 16)
            sp.dma_start(ident[:, :], ident_dram).then_inc(consts_in, 16)
            load_x(1, 1)

            def store(s, slot):
                wait_alone(sp, alone_sp, out_done.sem, out_done.at(s, TT))
                sp.dma_start(tiles_of(x_out, s), y[:, slot]).then_inc(y_stored.sem, 16)

            def step(s, slot, first, last):
                if not (isinstance(s, int) and s + 2 >= SEQS):
                    wait_alone(sp, alone_sp, xn_done.sem, xn_done.at(s, TT))
                    wait_alone(sp, alone_sp, x_copied.sem, x_copied.at(s, 1))
                    load_x(s + 2, slot)
                if not first:
                    wait_alone(sp, alone_sp, x_copied.sem, x_copied.at(s, 1))
                    store(s - 1, 1 - slot)

            over_steps(sp, step, 3)
            store(SEQS - 1, (SEQS - 1) % 2)
            wait(sp, y_stored, SEQS, 0)

        @block.gpsimd
        def _(pool):
            pool.memset(minus_half[:, :], -0.5).then_inc(filled, 1)
            pool.memset(half[:, :], 0.5).then_inc(filled, 1)
            pool.memset(ones[:, :], 1.0).then_inc(filled, 1)
            pool.wait_ge(filled, 3)
            give_credits(pool, [sq_done])

            def norm(s):
                wait_alone(pool, alone_pool, moments_done.sem, moments_done.at(s, TT))
                pool.tensor_scalar(var_eps[:, :], moments[:, :, 1], LN_EPS, None, ALU.add).then_inc(eps_added.sem, 1)
                wait(pool, eps_added, s, 1)
                pool.tensor_tensor(rstd[:, :], var_eps[:, :], minus_half[:, :], ALU.pow).then_inc(rstd_done.sem, 1)

            def rms(s):
                wait_alone(pool, alone_pool, x_sq_done.sem, x_sq_done.at(s, TT))
                pool.tensor_scalar(x_ms[:, :], x_sq[:, :], 1.0 / D, None, ALU.mult).then_inc(x_ms_done.sem, 1)
                wait(pool, x_ms_done, s, 1)
                pool.tensor_tensor(x_rms[:, :], x_ms[:, :], half[:, :], ALU.pow).then_inc(x_rms_done.sem, 1)

            norm(0)
            rms(0)

            def hidden_rms(s):
                wait(pool, h_ms_done, s, 1)
                pool.tensor_tensor(h_rms[:, :], h_ms[:, :], half[:, :], ALU.pow).then_inc(h_rms_done.sem, 1)

            def step(s, slot, first, last):
                for k in range(K):
                    wait(pool, hid_act, s, k + 1)
                    wait(pool, sq_summed, s, k + 1 - RING)
                    pool.tensor_tensor(hid_sq[:, k % RING, :], hid[:, k % RING, :], hid[:, k % RING, :],
                                       ALU.mult).then_inc(sq_done.sem, 1)
                    if k == 0 and not last:
                        norm(s + 1)
                    if k == 1 and not first:
                        hidden_rms(s - 1)
                    if k == 4 and not last:
                        rms(s + 1)

            over_steps(pool, step)
            hidden_rms(SEQS - 1)

        @block.scalar
        def _(act):
            give_credits(act, [hid_act])
            act.wait_ge(w_in, 32)
            for i in range(2):
                if i:
                    act.wait_ge(abs_done, i)
                act.activation(w_abs[:, :], w_raw[:, i, :], ACT.Abs, accum_out=w_sum[:, i:i + 1]).then_inc(abs_done, 1)

            def squares(s):
                for t in range(TT):
                    wait(act, xn_done, s, t + 1)
                    if t:
                        wait(act, x_sq_done, s, t)
                    act.activation(square_work[:, :], xn[:, t, :], ACT.Square,
                                   accum_out=x_sq[:, t:t + 1]).then_inc(x_sq_done.sem, 1)

            def copy_x(s, slot):
                x_loads.wait(act, s, slot)
                wait(act, y_stored, s, -1)
                act.activation(y[:, slot].rearrange("p t d -> p (t d)"), x[:, slot].rearrange("p t d -> p (t d)"),
                               ACT.Copy).then_inc(x_copied.sem, 1)

            squares(0)
            copy_x(0, 0)

            def turn(s, slot, f):
                wait(act, turned, s, f + 1)
                act.activation(xT_hi[:, slot, f, :], ps_turn[:, :], ACT.Copy).then_inc(turn_hi.sem, 1)

            for f in range(FB):
                turn(0, 0, f)

            def step(s, slot, first, last):
                for k in range(K):
                    wait(act, hid_summed, s, k + 1)
                    wait(act, hid_split, s, k + 1 - RING)
                    wait(act, sq_done, s, k + 1 - RING)
                    act.activation(hid[:, k % RING, :], ps_hid[:, k % PS_RING, :], ACT.Gelu)
                    wait(act, hid_used, s, k + 1 - RING)
                    act.activation(hid_hi[:, k % RING, :], ps_hid[:, k % PS_RING, :], ACT.Gelu).then_inc(hid_act.sem, 1)
                    if k == 3 and not last:
                        squares(s + 1)
                    for f in range(FB):
                        if k == TAKE_AT[f] and not last:
                            turn(s + 1, 1 - slot, f)
                    if k == COPY_AT and not last:
                        copy_x(s + 1, 1 - slot)

            over_steps(act, step)

        @block.vector
        def _(dve):
            give_credits(dve, [turn_lo, hid_split, out_done, h_ms_done])
            dve.wait_ge(total_done, 1)
            dve.tensor_scalar(limit[:, :], ps_sq[:, 0:2], 0.5 / (F * D), None, ALU.mult).then_inc(limit_done, 1)
            dve.tensor_scalar(minus_limit[:, :], ps_sq[:, 0:2], -0.5 / (F * D), None, ALU.mult).then_inc(limit_done, 1)
            dve.wait_ge(limit_done, 2)
            for i, w in enumerate((w_up, w_down)):
                dve.tensor_scalar(below[:, i, :], w_raw[:, i, :], minus_limit[:, i:i + 1], None,
                                  ALU.is_lt).then_inc(below_done, 1)
                dve.wait_ge(below_done, i + 1)
                dve.scalar_tensor_tensor(out=w[:, :, :].rearrange("p a b -> p (a b)"), in0=w_raw[:, i, :],
                                         scalar=limit[:, i:i + 1], in1=below[:, i, :], op0=ALU.is_gt,
                                         op1=ALU.subtract).then_inc(w_ready, 1)

            def norm_part(s, slot, n):
                if n == 0:
                    x_loads.wait(dve, s, slot)
                    for t in range(TT):
                        dve.bn_stats(stats[:, t, :], x[:, slot, t, :]).then_inc(stats_done.sem, 1)
                    wait_alone(dve, alone, stats_done.sem, stats_done.at(s, TT))
                    for t in range(TT):
                        dve.bn_aggr(moments[:, t, :], stats[:, t, :]).then_inc(moments_done.sem, 1)
                if n == 1:
                    wait(dve, rstd_done, s, 1)
                    for t in range(TT):
                        dve.tensor_scalar(xn[:, t, :], x[:, slot, t, :], moments[:, t, 0:1], rstd[:, t:t + 1],
                                          ALU.subtract, ALU.mult).then_inc(xn_done.sem, 1)
                if n == 2:
                    wait(dve, x_rms_done, s, 1)
                    dve.tensor_scalar(x_rms_eps[:, :], x_rms[:, :], RMS_EPS, None, ALU.add).then_inc(x_scale_part.sem, 1)
                    wait(dve, x_scale_part, s, 1)
                    dve.reciprocal(x_scale[:, :], x_rms_eps[:, :]).then_inc(x_scale_part.sem, 1)
                    wait(dve, x_scale_part, s, 2)
                    for t in range(TT):
                        dve.tensor_scalar(xr[:, t, :], xn[:, t, :], x_scale[:, t:t + 1], None,
                                          ALU.mult).then_inc(xr_done.sem, 1)

            def turn(s, slot, f):
                wait(dve, turn_hi, s, f + 1)
                dve.tensor_tensor(xT_lo[:, slot, f, :], ps_turn[:, :], xT_hi[:, slot, f, :],
                                  ALU.subtract).then_inc(turn_lo.sem, 1)

            for n in range(len(NORM_WITH)):
                norm_part(0, 0, n)
            for f in range(FB):
                turn(0, 0, f)

            def mean_squares(s):
                wait(dve, sq_summed, s, K)
                dve.tensor_scalar(h_ms[:, :], ps_sq[:, 0:TT], 1.0 / F, None, ALU.mult).then_inc(h_ms_done.sem, 1)

            def finish(s, slot):
                wait(dve, h_rms_done, s, 1)
                dve.tensor_scalar(h_rms_eps[:, :], h_rms[:, :], RMS_EPS, None, ALU.add).then_inc(h_scale_part.sem, 1)
                wait(dve, h_scale_part, s, 1)
                dve.reciprocal(h_scale[:, :], h_rms_eps[:, :]).then_inc(h_scale_part.sem, 1)
                wait(dve, h_scale_part, s, 2)
                wait(dve, hid_used, s, K)
                wait(dve, x_copied, s, 1)
                for t in range(TT):
                    dve.scalar_tensor_tensor(out=y[:, slot, t, :], in0=ps_out[:, slot, t, :], scalar=h_scale[:, t:t + 1],
                                             in1=y[:, slot, t, :], op0=ALU.mult, op1=ALU.add).then_inc(out_done.sem, 1)

            def step(s, slot, first, last):
                for k in range(K):
                    wait(dve, hid_act, s, k + 1)
                    dve.tensor_tensor(hid_lo[:, k % RING, :], hid[:, k % RING, :], hid_hi[:, k % RING, :],
                                      ALU.subtract).then_inc(hid_split.sem, 1)
                    if k in NORM_WITH and not last:
                        norm_part(s + 1, 1 - slot, NORM_WITH.index(k))
                    if k == 0 and not first:
                        mean_squares(s - 1)
                    if k == FINISH_AT and not first:
                        finish(s - 1, 1 - slot)
                    for f in range(FB):
                        if k == TAKE_AT[f] and not last:
                            turn(s + 1, 1 - slot, f)

            over_steps(dve, step)
            mean_squares(SEQS - 1)
            finish(SEQS - 1, (SEQS - 1) % 2)

        @block.tensor
        def _(pe):
            give_credits(pe, [hid_used, sq_summed])
            pe.wait_ge(consts_in, 16)
            pe.wait_ge(filled, 3)
            pe.wait_ge(abs_done, 2)
            pe.matmul(ps_sq[:, 0:2], ones[:, :], w_sum[:, :], start=True, stop=True).then_inc(total_done, 1)

            def turn(s, f):
                wait(pe, xr_done, s, TT)
                wait(pe, turn_lo, s, f)
                for t in range(TT):
                    last = pe.transpose(ps_turn[:, t * P:(t + 1) * P], xr[:, t, f * P:(f + 1) * P], ident[:, :])
                last.then_inc(turned.sem, 1)

            for f in range(FB):
                turn(0, f)
            pe.wait_ge(w_ready, 2)

            def up(s, slot, k):
                wait(pe, hid_act, s, k + 1 - PS_RING)
                for f in range(FB):
                    w = w_up[:, f, k * P:(k + 1) * P]
                    pe.matmul(ps_hid[:, k % PS_RING, :], w, xT_hi[:, slot, f, :], start=(f == 0), stop=False)
                    mm = pe.matmul(ps_hid[:, k % PS_RING, :], w, xT_lo[:, slot, f, :], start=False, stop=(f == FB - 1))
                mm.then_inc(hid_summed.sem, 1)

            def down(s, slot, k):
                wait(pe, hid_split, s, k + 1)
                if k == 0:
                    wait(pe, out_done, s, -TT)
                for t in range(TT):
                    tok = slice(t * P, (t + 1) * P)
                    pe.matmul(ps_out[:, slot, t, :], hid_hi[:, k % RING, tok], w_down[:, k, :],
                              start=(k == 0 and t % 2 == 0), stop=False, skip_group_check=True)
                    mm = pe.matmul(ps_out[:, slot, t, :], hid_lo[:, k % RING, tok], w_down[:, k, :],
                                   start=False, stop=(k == K - 1), skip_group_check=True)
                mm.then_inc(hid_used.sem, 1)

            def squares(s, k):
                wait(pe, sq_done, s, k + 1)
                if k == 0:
                    wait(pe, h_ms_done, s, 0)
                for t in range(TT):
                    mm = pe.matmul(ps_sq[:, t:t + 1], hid_sq[:, k % RING, t * P:(t + 1) * P], ones[:, 0:1],
                                   start=(k == 0 and t == 0), stop=(k == K - 1), skip_group_check=True)
                mm.then_inc(sq_summed.sem, 1)

            def step(s, slot, first, last):
                wait(pe, turn_lo, s, FB)
                for k in range(LOOKAHEAD):
                    up(s, slot, k)
                for k in range(K):
                    if k + LOOKAHEAD < K:
                        up(s, slot, k + LOOKAHEAD)
                    if k:
                        squares(s, k - 1)
                    down(s, slot, k)
                    if k in TURN_AT and not last:
                        turn(s + 1, TURN_AT.index(k))
                squares(s, K - 1)

            over_steps(pe, step)


def mamba_phase(nc, ident_dram, triangles_dram, x_in, in_proj_t, conv_cols, conv_b_col, a_log, dt_w_t, dt_b,
                b_w_t, c_w_t, d_skip, ln_cols, out_proj_t, x_out):
    DI = b_w_t.shape[0]
    H = a_log.shape[0]
    HD = DI // H
    IB = DI // P
    CONV = conv_cols.shape[1] // IB
    PAD = CONV - 1
    HALF = H // 2
    HALVES = 2 * TT
    PIECE = 1024
    assert HD * 2 == P and HALF * P == SEQ

    with ExitStack() as ctx:
        def sb(name, shape, dt=F32):
            return ctx.enter_context(nc.sbuf_tensor("ssm_" + name, shape, dt))

        def psum(name, shape):
            return ctx.enter_context(nc.psum_tensor("ssm_" + name, shape, F32))

        def sem(name):
            return nc.alloc_semaphore(name="ssm_" + name)

        def signal(name, per_seq, credit=0, unit=1):
            return Signal(ctx, nc, "ssm_" + name, per_seq, credit, unit)

        in_hi, in_lo = sb("in_hi", [P, FB, 2 * DI], F32R), sb("in_lo", [P, FB, 2 * DI], F32R)
        bw_hi, bw_lo = sb("bw_hi", [P, IB, DI], F32R), sb("bw_lo", [P, IB, DI], F32R)
        cw_hi, cw_lo = sb("cw_hi", [P, IB, DI], F32R), sb("cw_lo", [P, IB, DI], F32R)
        ow_hi, ow_lo = sb("ow_hi", [P, IB, D], F32R), sb("ow_lo", [P, IB, D], F32R)
        ident = sb("ident", [P, P])
        triangles = sb("triangles", [P, 4, P])
        ident16 = sb("ident16", [P, P], mybir.dt.bfloat16)
        masked16 = sb("masked16", [P, HALF, P], mybir.dt.bfloat16)
        conv_w = sb("conv_w", [P, IB, CONV])
        conv_b = sb("conv_b", [P, IB])
        dt_w = sb("dt_w", [P, IB, H])
        dt_bias = sb("dt_bias", [P, H])
        a_logs = sb("a_logs", [P, H])
        a_exp = sb("a_exp", [P, H])
        a_neg = sb("a_neg", [P, H])
        d_all = sb("d_all", [P, H])
        ln_w = sb("ln_w", [P, 2, IB])

        x = sb("x", [P, 2, TT, D])
        stats = sb("stats", [P, TT, 6])
        moments = sb("moments", [P, TT, 2])
        var_eps = sb("var_eps", [P, TT])
        minus_half = sb("minus_half", [P, TT])
        rstd = sb("rstd", [P, TT])
        xn = sb("xn", [P, TT, D])
        xT_hi, xT_lo = sb("xT_hi", [P, FB, SEQ], F32R), sb("xT_lo", [P, FB, SEQ], F32R)
        u_pad = sb("u_pad", [P, IB, PAD + SEQ])
        u = sb("u", [P, IB, SEQ])
        u_hi, u_lo = sb("u_hi", [P, IB, SEQ], F32R), sb("u_lo", [P, IB, SEQ], F32R)
        z = sb("z", [P, 2, IB, SEQ])
        bT = sb("bT", [P, IB, SEQ])
        cT = sb("cT", [P, 2, IB, SEQ])
        b_tok, u_tok, u_dt = sb("b_tok", [P, TT, DI]), sb("u_tok", [P, TT, DI]), sb("u_dt", [P, TT, DI])
        stage = b_tok[:, :, :].rearrange("p (i t) d -> p i (t d)", i=2)
        dt_raw = sb("dt_raw", [P, TT, H])
        dt_abs = sb("dt_abs", [P, TT, H])
        dt_exp = sb("dt_exp", [P, TT, H])
        dt_log = sb("dt_log", [P, TT, H])
        dt = sb("dt", [P, TT, H])
        a = sb("a", [P, TT, H])
        sums = sb("sums", [P, 2, TT, H])
        to_end = sb("to_end", [P, TT, H])
        decays = sb("decays", [P, 2, TT, H])
        decay_end = sb("decay_end", [P, TT, H])
        decay_state = sb("decay_state", [P, TT, H // 2])
        a_tri = sb("a_tri", [P, 2, HALF, P])
        decay = sb("decay", [P, 2, HALF, P])
        u_end = sb("u_end", [P, DI])
        state = sb("state", [P, H // 2, HD])
        state_old = sb("state_old", [P, H // 2, HD])
        y_old, y_sum = xn[:, 0:2, :].rearrange("p t d -> p (t d)"), xn[:, 2:4, :].rearrange("p t d -> p (t d)")
        y_stats = sb("y_stats", [P, TT, 6])
        y_moments = sb("y_moments", [P, TT, 2])
        y_var_eps = sb("y_var_eps", [P, TT])
        y_rstd = sb("y_rstd", [P, TT])
        g_hi, g_lo = sb("g_hi", [P, IB, SEQ], F32R), sb("g_lo", [P, IB, SEQ], F32R)

        ps = psum("ps", [P, 2, SEQ])
        ps_decay = psum("ps_decay", [P, 2, HALF, P])
        ps_scores = psum("ps_scores", [P, HALF, P])
        ps_y = psum("ps_y", [P, DI])
        ps_y_old = psum("ps_y_old", [P, DI])
        ps_small = psum("ps_small", [P, 512])
        ps_state = ps_small[:, 0:H // 2 * HD].rearrange("p (q d) -> p q d", d=HD)
        ps_dt = ps_small[:, 256:256 + TT * H].rearrange("p (t h) -> p t h", h=H)
        ps_sums = ps_small[:, 320:320 + 2 * TT * H].rearrange("p (k t h) -> p k t h", k=2, h=H)

        def uses(name, n, reader):
            return [(f"{name}{i}", reader) for i in range(n)]

        ahead = uses("turn", FB, "dve")
        own = (uses("b", IB, "act") + uses("c", IB, "dve") + uses("u_tok", TT, "act")
               + uses("b_tok", TT, "act"))
        tail = uses("y", IB, "act") + uses("out", TT // 2, "dve")
        ahead += uses("u", IB, "act") + uses("z", IB, "act")
        ring = Ring(ctx, nc, "ssm_ps", 2, ahead, own + ahead + tail, own + tail)

        consts_in, filled = sem("consts_in"), sem("filled")
        stage_in = [sem(f"stage_in{i}") for i in range(2)]
        stage_hi, stage_lo = sem("stage_hi"), sem("stage_lo")
        a_exp_done, consts_made = sem("a_exp_done"), sem("consts_made")
        x_in_sem = signal("x_in", 1, unit=16)
        x_stored = signal("x_stored", 1, credit=2, unit=16)
        alone, alone_pool = sem("waits_of_dve"), sem("waits_of_pool")
        stats_done = signal("stats_done", TT)
        moments_done = signal("moments_done", TT)
        eps_added = signal("eps_added", 1)
        rstd_done = signal("rstd_done", 1)
        xn_done = signal("xn_done", TT)
        turn_hi = signal("turn_hi", FB)
        conv_part = signal("conv_part", IB * CONV)
        u_done = signal("u_done", IB)
        u_split = signal("u_split", IB)
        dt_summed = signal("dt_summed", 1)
        dt_raw_done = signal("dt_raw_done", 1)
        softplus_part = signal("softplus_part", 3)
        dt_done = signal("dt_done", 1)
        a_done = signal("a_done", 1)
        sums_summed = signal("sums_summed", 1)
        sums_done = signal("sums_done", 2)
        decays_done = signal("decays_done", 2)
        decay_state_done = signal("decay_state_done", 2)
        u_dt_done = signal("u_dt_done", TT)
        skip_done = signal("skip_done", TT)
        a_tri_done = signal("a_tri_done", HALVES)
        u_end_done = signal("u_end_done", TT - 1)
        log_decay_summed = signal("log_decay_summed", HALVES, credit=2)
        decay_done = signal("decay_done", HALVES, credit=2)
        scores_summed = signal("scores_summed", HALVES)
        scores_done = signal("scores_done", HALVES, credit=2)
        y_summed = signal("y_summed", HALVES, credit=2)
        y_old_summed = signal("y_old_summed", TT - 1)
        state_summed = signal("state_summed", TT - 1, credit=1)
        state_decayed = signal("state_decayed", TT - 2)
        state_done = signal("state_done", TT - 1, credit=1)
        y_read = signal("y_read", TT, credit=1)
        y_part = signal("y_part", TT - 1)
        y_done = signal("y_done", TT)
        y_stats_done = signal("y_stats_done", TT)
        y_moments_done = signal("y_moments_done", TT)
        y_eps_added = signal("y_eps_added", 1)
        y_rstd_done = signal("y_rstd_done", 1)
        yn_done = signal("yn_done", TT)
        g_gated = signal("g_gated", IB)
        g_hi_done = signal("g_hi_done", IB)
        g_split = signal("g_split", IB)

        pieces = []
        for f in range(FB):
            pieces.append((in_proj_t.rearrange("(f p) h -> f p h", p=P)[f], in_hi[:, f, :], in_lo[:, f, :]))
        for w, hi, lo, width in ((b_w_t, bw_hi, bw_lo, DI), (c_w_t, cw_hi, cw_lo, DI), (out_proj_t, ow_hi, ow_lo, D)):
            n = PIECE // width
            for c in range(0, IB, n):
                pieces.append((w.rearrange("(k p) d -> p k d", p=P)[:, c:c + n, :], hi[:, c:c + n, :], lo[:, c:c + n, :]))

        def staged(i, dst):
            v = stage[:, i % 2, :]
            return v if len(dst.shape) == 2 else v.rearrange("p (k d) -> p k d", k=dst.shape[1])

        def heads(v):
            return v.rearrange("p (h d) -> p h d", d=HD)

        def per_head(v, n=HD):
            return v.unsqueeze(2).broadcast_to([v.shape[0], v.shape[1], n])

        CONSTS = 9
        block = ctx.enter_context(nc.Block())

        @block.sync
        def _(sp):
            def load_x(s, slot):
                wait(sp, x_stored, s, -1)
                sp.dma_start(x[:, slot], tiles_of(x_in, s)).then_inc(x_in_sem.sem, 16)

            give_credits(sp, [x_stored])
            load_x(0, 0)
            sp.dma_start(ident[:, :], ident_dram).then_inc(consts_in, 16)
            sp.dma_start(triangles[:, :, :], triangles_dram.rearrange("k p t -> p k t")).then_inc(consts_in, 16)
            sp.dma_start(conv_w[:, :, :], conv_cols.rearrange("p (k c) -> p k c", c=CONV)).then_inc(consts_in, 16)
            sp.dma_start(conv_b[:, :], conv_b_col).then_inc(consts_in, 16)
            sp.dma_start(dt_w[:, :, :], dt_w_t.rearrange("(k p) h -> p k h", p=P)).then_inc(consts_in, 16)
            sp.dma_start(dt_bias[:, :], dt_b.partition_broadcast(P)).then_inc(consts_in, 16)
            sp.dma_start(a_logs[:, :], a_log.partition_broadcast(P)).then_inc(consts_in, 16)
            sp.dma_start(d_all[:, :], d_skip.partition_broadcast(P)).then_inc(consts_in, 16)
            sp.dma_start(ln_w[:, :, :], ln_cols.rearrange("p (k c) -> p k c", c=IB)).then_inc(consts_in, 16)
            for i, (src, dst, _) in enumerate(pieces):
                if i >= 2:
                    sp.wait_ge(stage_lo, i - 1)
                sp.dma_start(staged(i, dst), src).then_inc(stage_in[i % 2], 16)

            def step(s, slot, last):
                if not last:
                    load_x(s + 1, 1 - slot)
                wait_read(sp, ring, s, f"out{TT // 2 - 1}", last)
                sp.dma_start(tiles_of(x_out, s), x[:, slot]).then_inc(x_stored.sem, 16)

            over_sequences(sp, step)
            wait(sp, x_stored, SEQS, 0)

        @block.gpsimd
        def _(pool):
            pool.memset(minus_half[:, :], -0.5).then_inc(filled, 1)
            pool.memset(u_pad[:, :, 0:PAD], 0.0).then_inc(filled, 1)
            pool.wait_ge(filled, 2)
            pool.wait_ge(consts_in, 16 * CONSTS)

            def rsqrt(s, moments_sem, var, sum_, sum_sem, out, out_sem):
                wait_alone(pool, alone_pool, moments_sem.sem, moments_sem.at(s, TT))
                pool.tensor_scalar(sum_[:, :], var, LN_EPS, None, ALU.add).then_inc(sum_sem.sem, 1)
                wait(pool, sum_sem, s, 1)
                pool.tensor_tensor(out[:, :], sum_[:, :], minus_half[:, :], ALU.pow).then_inc(out_sem.sem, 1)

            def norm(s):
                rsqrt(s, moments_done, moments[:, :, 1], var_eps, eps_added, rstd, rstd_done)

            norm(0)

            def step(s, slot, last):
                if not last:
                    norm(s + 1)
                wait(pool, a_done, s, 1)
                for i in range(HALVES):
                    c, h = i // 2, i % 2 * HALF
                    wait(pool, log_decay_summed, s, i - 1)
                    pool.tensor_tensor(a_tri[:, i % 2], triangles[:, 0, :].unsqueeze(1).broadcast_to([P, HALF, P]),
                                       per_head(a[:, c, h:h + HALF], P), ALU.mult).then_inc(a_tri_done.sem, 1)
                    if h and c:
                        wait(pool, decays_done, s, 2)
                        wait(pool, state_summed, s, c - 1)
                        pool.tensor_tensor(heads(u_end[:, :]), heads(u_dt[:, c - 1, :]), per_head(decay_end[:, c - 1, :]),
                                           ALU.mult).then_inc(u_end_done.sem, 1)
                    if h:
                        wait(pool, u_dt_done, s, c + 1)
                        pool.tensor_tensor(heads(u_tok[:, c, :]), heads(u_tok[:, c, :]), per_head(d_all[:, :]),
                                           ALU.mult).then_inc(skip_done.sem, 1)
                rsqrt(s, y_moments_done, y_moments[:, :, 1], y_var_eps, y_eps_added, y_rstd, y_rstd_done)

            over_sequences(pool, step)

        @block.scalar
        def _(act):
            def split(i):
                hi = pieces[i][1]
                act.wait_ge(stage_in[i % 2], 16 * (i // 2 + 1))
                act.activation(hi, staged(i, hi), ACT.Copy).then_inc(stage_hi, 1)

            for i in range(FB):
                split(i)
            act.wait_ge(consts_in, 16 * CONSTS)
            act.activation(a_exp[:, :], a_logs[:, :], ACT.Exp).then_inc(a_exp_done, 1)
            give_credits(act, [decay_done])

            def turn(s):
                for f in range(FB):
                    wait_filled(act, ring, s, f"turn{f}", False)
                    act.activation(xT_hi[:, f, :], ps[:, ring.bank(s, f"turn{f}", False), :],
                                   ACT.Copy).then_inc(turn_hi.sem, 1)

            def pad_in(s):
                for m in range(IB):
                    wait_filled(act, ring, s, f"u{m}", False)
                    if s is not None:
                        wait(act, conv_part, s, (m + 1) * CONV)
                    act.activation(u_pad[:, m, PAD:], ps[:, ring.bank(s, f"u{m}", False), :],
                                   ACT.Copy).then_inc(ring.free["act"], 1)

            def silu(s, m):
                wait(act, conv_part, 0 if s is None else s + 1, (m + 1) * CONV)
                act.activation(u_hi[:, m, :], u[:, m, :], ACT.Silu)
                act.activation(u[:, m, :], u[:, m, :], ACT.Silu).then_inc(u_done.sem, 1)

            def gates(s, slot):
                for m in range(IB):
                    wait_filled(act, ring, s, f"z{m}", False)
                    act.activation(z[:, slot, m, :], ps[:, ring.bank(s, f"z{m}", False), :],
                                   ACT.Silu).then_inc(ring.free["act"], 1)

            turn(None)
            for i in range(FB, len(pieces)):
                split(i)
            pad_in(None)
            gates(None, 0)
            for m in range(IB):
                silu(None, m)

            def step(s, slot, last):
                def take(use, out, func, **more):
                    wait_filled(act, ring, s, use, last)
                    act.activation(out, ps[:, ring.bank(s, use, last), :], func, **more).then_inc(ring.free["act"], 1)

                wait(act, dt_raw_done, s, 1)
                act.activation(dt_abs[:, :, :], dt_raw[:, :, :], ACT.Abs).then_inc(softplus_part.sem, 1)
                wait(act, softplus_part, s, 1)
                act.activation(dt_exp[:, :, :], dt_abs[:, :, :], ACT.Exp, scale=-1.0).then_inc(softplus_part.sem, 1)
                wait(act, softplus_part, s, 2)
                act.activation(dt_log[:, :, :], dt_exp[:, :, :], ACT.Ln, bias=1.0).then_inc(softplus_part.sem, 1)
                for m in range(IB):
                    take(f"b{m}", bT[:, m, :], ACT.Copy)
                wait(act, sums_done, s, 1)
                act.activation(decays[:, :, :, :], sums[:, :, :, :], ACT.Exp).then_inc(decays_done.sem, 1)
                wait(act, sums_done, s, 2)
                act.activation(decay_end[:, :, :], to_end[:, :, :], ACT.Exp).then_inc(decays_done.sem, 1)
                for c in range(TT):
                    take(f"u_tok{c}", u_tok[:, c, :], ACT.Copy)
                for c in range(TT):
                    take(f"b_tok{c}", b_tok[:, c, :], ACT.Copy)
                if not last:
                    turn(s)
                    pad_in(s)
                for i in range(HALVES):
                    wait(act, log_decay_summed, s, i + 1)
                    wait(act, y_summed, s, i - 1)
                    act.activation(decay[:, i % 2], ps_decay[:, i % 2], ACT.Exp).then_inc(decay_done.sem, 1)
                if not last:
                    for m in range(IB - 1):
                        silu(s, m)
                    gates(s, 1 - slot)
                    silu(s, IB - 1)
                for f in range(IB):
                    take(f"y{f}", bT[:, f, :], ACT.Identity, bias=ln_w[:, 1, f:f + 1], scale=ln_w[:, 0, f:f + 1])

            over_sequences(act, step)

        @block.vector
        def _(dve):
            give_credits(dve, [scores_done, state_done, y_read])

            def split(i):
                _, hi, lo = pieces[i]
                dve.wait_ge(stage_hi, i + 1)
                dve.tensor_tensor(lo, staged(i, lo), hi, ALU.subtract).then_inc(stage_lo, 1)

            for i in range(FB):
                split(i)
            dve.wait_ge(consts_in, 16 * CONSTS)

            def norm_stats(s, slot):
                wait(dve, x_in_sem, s, 1)
                for t in range(TT):
                    dve.bn_stats(stats[:, t, :], x[:, slot, t, :]).then_inc(stats_done.sem, 1)
                wait_alone(dve, alone, stats_done.sem, stats_done.at(s, TT))
                for t in range(TT):
                    dve.bn_aggr(moments[:, t, :], stats[:, t, :]).then_inc(moments_done.sem, 1)

            def norm_apply(s, slot):
                wait(dve, rstd_done, s, 1)
                for t in range(TT):
                    dve.tensor_scalar(xn[:, t, :], x[:, slot, t, :], moments[:, t, 0:1], rstd[:, t:t + 1],
                                      ALU.subtract, ALU.mult).then_inc(xn_done.sem, 1)

            def turn(s):
                for f in range(FB):
                    wait(dve, turn_hi, 0 if s is None else s + 1, f + 1)
                    dve.tensor_tensor(xT_lo[:, f, :], ps[:, ring.bank(s, f"turn{f}", False), :], xT_hi[:, f, :],
                                      ALU.subtract).then_inc(ring.free["dve"], 1)

            def conv(s, m):
                n = 0 if s is None else s + 1
                wait_read(dve, ring, s, f"u{m}", False)
                dve.tensor_scalar(u[:, m, :], u_pad[:, m, 0:SEQ], conv_w[:, m, 0:1], conv_b[:, m:m + 1],
                                  ALU.mult, ALU.add).then_inc(conv_part.sem, 1)
                for tap in range(1, CONV):
                    wait(dve, conv_part, n, m * CONV + tap)
                    dve.scalar_tensor_tensor(out=u[:, m, :], in0=u_pad[:, m, tap:tap + SEQ], scalar=conv_w[:, m, tap:tap + 1],
                                             in1=u[:, m, :], op0=ALU.mult, op1=ALU.add).then_inc(conv_part.sem, 1)

            def u_low(s, m):
                wait(dve, u_done, 0 if s is None else s + 1, m + 1)
                dve.tensor_tensor(u_lo[:, m, :], u[:, m, :], u_hi[:, m, :], ALU.subtract).then_inc(u_split.sem, 1)

            norm_stats(0, 0)
            norm_apply(0, 0)
            turn(None)
            for i in range(FB, len(pieces)):
                split(i)
            dve.wait_ge(a_exp_done, 1)
            dve.tensor_scalar(a_neg[:, :], a_exp[:, :], -1.0, None, ALU.mult).then_inc(consts_made, 1)
            dve.tensor_copy(ident16[:, :], ident[:, :]).then_inc(consts_made, 1)
            dve.tensor_copy(masked16[:, :, :],
                            triangles[:, 3, :].unsqueeze(1).broadcast_to([P, HALF, P])).then_inc(consts_made, 1)
            dve.wait_ge(consts_made, 3)
            dve.wait_ge(filled, 2)
            for r in range(2):
                dve.memset(cT[(1 - r) * HD:(2 - r) * HD, r], 0.0)
            for m in range(IB):
                conv(None, m)
            for m in range(IB):
                u_low(None, m)

            def step(s, slot, last):
                wait(dve, dt_summed, s, 1)
                dve.tensor_tensor(dt_raw[:, :, :], ps_dt, dt_bias[:, :].unsqueeze(1).broadcast_to([P, TT, H]),
                                  ALU.add).then_inc(dt_raw_done.sem, 1)
                if not last:
                    norm_stats(s + 1, 1 - slot)
                wait(dve, softplus_part, s, 3)
                dve.scalar_tensor_tensor(out=dt[:, :, :], in0=dt_raw[:, :, :], scalar=0.0, in1=dt_log[:, :, :],
                                         op0=ALU.max, op1=ALU.add).then_inc(dt_done.sem, 1)
                wait(dve, dt_done, s, 1)
                dve.tensor_tensor(a[:, :, :], dt[:, :, :], a_neg[:, :].unsqueeze(1).broadcast_to([P, TT, H]),
                                  ALU.mult).then_inc(a_done.sem, 1)
                if not last:
                    norm_apply(s + 1, 1 - slot)
                wait(dve, sums_summed, s, 1)
                dve.tensor_copy(sums[:, :, :, :], ps_sums).then_inc(sums_done.sem, 1)
                wait(dve, sums_done, s, 1)
                dve.tensor_tensor(to_end[:, :, :], sums[:, 1], sums[:, 0], ALU.subtract).then_inc(sums_done.sem, 1)
                for m in range(IB):
                    wait_filled(dve, ring, s, f"c{m}", last)
                    bank = ps[:, ring.bank(s, f"c{m}", last), :]
                    dve.tensor_copy(cT[0:HD, 0, m, :], bank[0:HD, :])
                    dve.tensor_copy(cT[HD:P, 1, m, :], bank[HD:P, :]).then_inc(ring.free["dve"], 1)
                wait(dve, decays_done, s, 1)
                for r in range(2):
                    part = slice(r * HD, (r + 1) * HD)
                    by_pair = decays[part, 1].rearrange("p t (q r) -> p t q r", r=2)
                    dve.tensor_copy(decay_state[part, :, :], by_pair[:, :, :, r]).then_inc(decay_state_done.sem, 1)
                for c in range(TT):
                    wait_read(dve, ring, s, f"u_tok{c}", last)
                    dve.tensor_tensor(heads(u_dt[:, c, :]), heads(u_tok[:, c, :]), per_head(dt[:, c, :]),
                                      ALU.mult).then_inc(u_dt_done.sem, 1)
                if not last:
                    turn(s)
                wait(dve, decay_state_done, s, 2)

                def scores_of(i):
                    wait(dve, scores_summed, s, i + 1)
                    wait(dve, decay_done, s, i + 1)
                    dve.tensor_tensor(decay[:, i % 2], decay[:, i % 2], ps_scores[:, :, :],
                                      ALU.mult).then_inc(scores_done.sem, 1)

                def update_state(c):
                    if c:
                        dve.tensor_tensor(state_old[:, :, :], state[:, :, :], per_head(decay_state[:, c, :]),
                                          ALU.mult).then_inc(state_decayed.sem, 1)
                        wait(dve, state_decayed, s, c)
                    wait(dve, state_summed, s, c + 1)
                    if c:
                        dve.tensor_tensor(state[:, :, :], ps_state, state_old[:, :, :], ALU.add).then_inc(state_done.sem, 1)
                    else:
                        dve.tensor_copy(state[:, :, :], ps_state).then_inc(state_done.sem, 1)

                def combine(c):
                    wait(dve, y_summed, s, 2 * c + 2)
                    if c:
                        wait(dve, y_old_summed, s, c)
                        dve.tensor_tensor(heads(y_old), heads(ps_y_old), per_head(decays[:, 0, c, :]),
                                          ALU.mult).then_inc(y_part.sem, 1)
                        wait(dve, y_part, s, c)
                        dve.tensor_tensor(y_sum, ps_y[:, :], y_old, ALU.add).then_inc(y_read.sem, 1)
                    else:
                        dve.tensor_copy(y_sum, ps_y[:, :]).then_inc(y_read.sem, 1)
                    wait(dve, y_read, s, c + 1)
                    wait(dve, skip_done, s, c + 1)
                    dve.tensor_tensor(u_tok[:, c, :], y_sum, u_tok[:, c, :], ALU.add).then_inc(y_done.sem, 1)
                    wait(dve, y_done, s, c + 1)
                    dve.bn_stats(y_stats[:, c, :], u_tok[:, c, :]).then_inc(y_stats_done.sem, 1)

                for i in range(HALVES + 1):
                    if i < HALVES:
                        scores_of(i)
                    if i % 2 and not last:
                        conv(s, i // 2)
                    if i and i % 2 == 0:
                        c = i // 2 - 1
                        if c < TT - 1:
                            update_state(c)
                        combine(c)
                wait_alone(dve, alone, y_stats_done.sem, y_stats_done.at(s, TT))
                for c in range(TT):
                    dve.bn_aggr(y_moments[:, c, :], y_stats[:, c, :]).then_inc(y_moments_done.sem, 1)
                wait(dve, y_rstd_done, s, 1)
                for c in range(TT):
                    dve.tensor_scalar(u_tok[:, c, :], u_tok[:, c, :], y_moments[:, c, 0:1], y_rstd[:, c:c + 1],
                                      ALU.subtract, ALU.mult).then_inc(yn_done.sem, 1)
                if not last:
                    for m in range(IB):
                        u_low(s, m)
                for f in range(IB):
                    wait_read(dve, ring, s, f"y{f}", last)
                    dve.tensor_tensor(bT[:, f, :], bT[:, f, :], z[:, slot, f, :], ALU.mult).then_inc(g_gated.sem, 1)
                    wait(dve, g_gated, s, f + 1)
                    dve.tensor_copy(g_hi[:, f, :], bT[:, f, :]).then_inc(g_hi_done.sem, 1)
                    wait(dve, g_hi_done, s, f + 1)
                    dve.tensor_tensor(g_lo[:, f, :], bT[:, f, :], g_hi[:, f, :], ALU.subtract).then_inc(g_split.sem, 1)
                for pair in range(TT // 2):
                    wait_filled(dve, ring, s, f"out{pair}", last)
                    part = x[:, slot, 2 * pair:2 * pair + 2, :].rearrange("p t d -> p (t d)")
                    dve.tensor_tensor(part, ps[:, ring.bank(s, f"out{pair}", last), :], part,
                                      ALU.add).then_inc(ring.free["dve"], 1)

            over_sequences(dve, step)

        @block.tensor
        def _(pe):
            pe.wait_ge(consts_in, 16 * CONSTS)
            give_credits(pe, [log_decay_summed, y_summed, state_summed])

            def turn(s):
                wait(pe, xn_done, 0 if s is None else s + 1, TT)
                for f in range(FB):
                    wait_free(pe, ring, s, f"turn{f}", False)
                    for t in range(TT):
                        last = pe.transpose(ps[:, ring.bank(s, f"turn{f}", False), t * P:(t + 1) * P],
                                            xn[:, t, f * P:(f + 1) * P], ident[:, :])
                    last.then_inc(ring.full, 1)

            def in_product(s, use, m, last):
                wait_free(pe, ring, s, use, last)
                for f in range(FB):
                    w = slice(m * P, (m + 1) * P)
                    mm = split_product(pe, ps[:, ring.bank(s, use, last), :], in_hi[:, f, w], in_lo[:, f, w],
                                       xT_hi[:, f, :], xT_lo[:, f, :], f == 0, f == FB - 1)
                mm.then_inc(ring.full, 1)

            def u_tiles(s):
                wait_read(pe, ring, s, f"turn{FB - 1}", False)
                for m in range(IB):
                    in_product(s, f"u{m}", m, False)

            def z_tiles(s):
                for m in range(IB):
                    in_product(s, f"z{m}", IB + m, False)

            def dt_product(s):
                wait(pe, u_done, s, IB)
                wait(pe, state_done, s, 0)
                for t in range(TT):
                    for k in range(IB):
                        mm = pe.matmul(ps_dt[:, t, :], u[:, k, t * P:(t + 1) * P], dt_w[:, k, :],
                                       start=(k == 0), stop=(k == IB - 1))
                mm.then_inc(dt_summed.sem, 1)

            turn(None)
            pe.wait_ge(stage_lo, FB)
            u_tiles(None)
            z_tiles(None)
            dt_product(0)
            pe.wait_ge(stage_lo, len(pieces))
            pe.wait_ge(consts_made, 3)

            def step(s, slot, last):
                wait(pe, u_split, s, IB)
                for name, hi, lo in (("b", bw_hi, bw_lo), ("c", cw_hi, cw_lo)):
                    for m in range(IB):
                        use = f"{name}{m}"
                        wait_free(pe, ring, s, use, last)
                        w = slice(m * P, (m + 1) * P)
                        for k in range(IB):
                            mm = split_product(pe, ps[:, ring.bank(s, use, last), :], hi[:, k, w], lo[:, k, w],
                                               u_hi[:, k, :], u_lo[:, k, :], k == 0, k == IB - 1)
                        mm.then_inc(ring.full, 1)
                    if name == "b":
                        wait(pe, a_done, s, 1)
                        for kind, w in enumerate((0, 2)):
                            mm = pe.matmul(ps_sums[:, kind].rearrange("p t h -> p (t h)"), triangles[:, w, :],
                                           a[:, :, :].rearrange("p t h -> p (t h)"), start=True, stop=True)
                        mm.then_inc(sums_summed.sem, 1)

                for name, source in (("u_tok", u), ("b_tok", bT)):
                    if name == "b_tok":
                        wait_read(pe, ring, s, f"b{IB - 1}", last)
                    for c in range(TT):
                        use = f"{name}{c}"
                        wait_free(pe, ring, s, use, last)
                        for k in range(IB):
                            mm = pe.transpose(ps[:, ring.bank(s, use, last), k * P:(k + 1) * P],
                                              source[:, k, c * P:(c + 1) * P], ident[:, :])
                        mm.then_inc(ring.full, 1)
                if not last:
                    turn(s)

                def log_decays(i):
                    wait(pe, a_tri_done, s, i + 1)
                    wait(pe, decay_done, s, i - 1)
                    pe.matmul(ps_decay[:, i % 2], triangles[:, 1, :], a_tri[:, i % 2], start=True, stop=False)
                    pe.matmul(ps_decay[:, i % 2], ident16[:, :], masked16[:, :, :], start=False,
                              stop=True).then_inc(log_decay_summed.sem, 1)

                def rows(head):
                    return slice(head % 2 * HD, head % 2 * HD + HD)

                def b_dot_c(i):
                    c, h = i // 2, i % 2 * HALF
                    wait(pe, scores_done, s, i)
                    for n in range(HALF):
                        r, q, tok = (h + n) % 2, (h + n) // 2, slice(c * P, (c + 1) * P)
                        mm = pe.matmul(ps_scores[:, n, :], bT[:, q, tok], cT[:, r, q, tok], start=True, stop=True)
                    mm.then_inc(scores_summed.sem, 1)

                def y_within(i):
                    c, h = i // 2, i % 2 * HALF
                    wait(pe, scores_done, s, i + 1)
                    if h == 0:
                        wait(pe, u_dt_done, s, c + 1)
                        wait(pe, y_read, s, c)
                    for n in range(HALF):
                        d = slice((h + n) * HD, (h + n + 1) * HD)
                        mm = pe.matmul(ps_y[:, d], decay[:, i % 2, n, :], u_dt[:, c, d], start=True, stop=True)
                    mm.then_inc(y_summed.sem, 1)

                def y_from_state(c):
                    wait(pe, state_done, s, c)
                    wait(pe, y_read, s, c)
                    for head in range(H):
                        mm = pe.matmul(ps_y_old[:, head * HD:(head + 1) * HD], cT[:, head % 2, head // 2, c * P:(c + 1) * P],
                                       state[:, head // 2, :], start=True, stop=True)
                    mm.then_inc(y_old_summed.sem, 1)

                def new_state(c):
                    wait(pe, u_end_done, s, c + 1)
                    wait(pe, state_done, s, c)
                    for head in range(H):
                        d = slice(head * HD, (head + 1) * HD)
                        mm = pe.matmul(ps_state[rows(head), head // 2, :], b_tok[:, c, d], u_end[:, d],
                                       start=True, stop=True)
                    mm.then_inc(state_summed.sem, 1)

                log_decays(0)
                log_decays(1)
                if not last:
                    u_tiles(s)
                wait_read(pe, ring, s, f"c{IB - 1}", last)
                wait_read(pe, ring, s, f"b_tok{TT - 1}", last)
                for i in range(HALVES + 1):
                    if i < HALVES:
                        b_dot_c(i)
                    if i:
                        y_within(i - 1)
                    if i + 2 < HALVES:
                        log_decays(i + 2)
                    if i and i % 2 == 0:
                        c = i // 2 - 1
                        if c:
                            y_from_state(c)
                        if c < TT - 1:
                            new_state(c)
                if not last:
                    z_tiles(s)
                wait(pe, yn_done, s, TT)
                for f in range(IB):
                    wait_free(pe, ring, s, f"y{f}", last)
                    for c in range(TT):
                        mm = pe.transpose(ps[:, ring.bank(s, f"y{f}", last), c * P:(c + 1) * P],
                                          u_tok[:, c, f * P:(f + 1) * P], ident[:, :])
                    mm.then_inc(ring.full, 1)
                if not last:
                    dt_product(s + 1)
                wait(pe, g_split, s, IB)
                for pair in range(TT // 2):
                    use = f"out{pair}"
                    wait_free(pe, ring, s, use, last)
                    for t in range(2):
                        tok = slice((2 * pair + t) * P, (2 * pair + t + 1) * P)
                        for k in range(IB):
                            mm = split_product(pe, ps[:, ring.bank(s, use, last), t * D:(t + 1) * D], g_hi[:, k, tok],
                                               g_lo[:, k, tok], ow_hi[:, k, :], ow_lo[:, k, :],
                                               k == 0, k == IB - 1)
                    mm.then_inc(ring.full, 1)

            over_sequences(pe, step)


def moe_phase(nc, ident_dram, x_in, gate_w, w1, b1_cols, w2, b2, sw1, sw2, sb2, x_out):
    HIDDEN = w1.shape[2]
    KT = HIDDEN // P
    BRANCHES = 3
    K = BRANCHES * KT
    GROUPS = BRANCHES * FB
    TURN_AT = [11 + 2 * g for g in range(GROUPS)]
    NORM_AT, NORM_PARTS = 4, TT + 5
    STAGE = 1024
    CONSTS = 7

    with ExitStack() as ctx:
        def sb(name, shape, dt=F32):
            return ctx.enter_context(nc.sbuf_tensor(name, shape, dt))

        def psum(name, shape):
            return ctx.enter_context(nc.psum_tensor(name, shape, F32))

        def signal(name, per_seq, credit=0, unit=1):
            return Signal(ctx, nc, name, per_seq, credit, unit)

        w1_hi, w1_lo = sb("moe_w1_hi", [P, BRANCHES, FB, HIDDEN], F32R), sb("moe_w1_lo", [P, BRANCHES, FB, HIDDEN], F32R)
        w2_hi, w2_lo = sb("moe_w2_hi", [P, BRANCHES, KT, D], F32R), sb("moe_w2_lo", [P, BRANCHES, KT, D], F32R)
        b1_col = sb("moe_b1_col", [P, BRANCHES, KT])
        b2_all = sb("moe_b2_all", [P, 3, D])
        b2_sum = sb("moe_b2_sum", [P, D])
        gates = sb("moe_gates", [P, 2, D])
        ident = sb("moe_ident", [P, P])
        stage = sb("moe_stage", [P, 2, STAGE])
        x = sb("moe_x", [P, 2, TT, D])
        stats = sb("moe_stats", [P, TT, 6])
        moments = sb("moe_moments", [P, TT, 2])
        var_eps = sb("moe_var_eps", [P, TT])
        minus_half = sb("moe_minus_half", [P, TT])
        rstd = sb("moe_rstd", [P, TT])
        score = sb("moe_score", [P, 2, TT])
        score_work = sb("moe_score_work", [P, D])
        mask = sb("moe_mask", [P, 2, TT])
        xn = sb("moe_xn", [P, BRANCHES, TT, D])
        xT_hi = sb("moe_xT_hi", [P, 2, BRANCHES, FB, SEQ], F32R)
        xT_lo = sb("moe_xT_lo", [P, 2, BRANCHES, FB, SEQ], F32R)
        hid = sb("moe_hid", [P, RING, SEQ])
        hid_hi = sb("moe_hid_hi", [P, RING, SEQ], F32R)
        hid_lo = sb("moe_hid_lo", [P, RING, SEQ], F32R)

        ps_hid = psum("moe_ps_hid", [P, RING, SEQ])
        ps_out = psum("moe_ps_out", [P, 2, TT, D])
        ps_turn = psum("moe_ps_turn", [P, SEQ])

        consts_in = nc.alloc_semaphore(name="moe_consts_in")
        stage_in = [nc.alloc_semaphore(name=f"moe_stage_in{i}") for i in range(2)]
        stage_hi = nc.alloc_semaphore(name="moe_stage_hi")
        stage_lo = nc.alloc_semaphore(name="moe_stage_lo")
        b2_part = nc.alloc_semaphore(name="moe_b2_part")
        b2_ready = nc.alloc_semaphore(name="moe_b2_ready")
        half_set = nc.alloc_semaphore(name="moe_half_set")
        x_loads = Loads(ctx, nc, "moe_x_loads")
        x_stored = signal("moe_x_stored", 1, credit=2, unit=16)
        alone_sp = nc.alloc_semaphore(name="moe_waits_of_sp")
        alone, alone_pool = nc.alloc_semaphore(name="moe_waits_of_dve"), nc.alloc_semaphore(name="moe_waits_of_pool")
        stats_done = signal("moe_stats_done", TT)
        moments_done = signal("moe_moments_done", TT)
        eps_added = signal("moe_eps_added", 1)
        rstd_done = signal("moe_rstd_done", 1)
        xn_done = signal("moe_xn_done", TT)
        score_done = signal("moe_score_done", 2 * TT)
        mask_done = signal("moe_mask_done", 2)
        masked_done = signal("moe_masked_done", 2 * TT)
        bias_added = signal("moe_bias_added", 1)
        turned = signal("moe_turned", GROUPS)
        turn_hi = signal("moe_turn_hi", GROUPS)
        turn_lo = signal("moe_turn_lo", GROUPS, credit=1)
        hid_summed = signal("moe_hid_summed", K)
        hid_act = signal("moe_hid_act", K, credit=RING)
        hid_split = signal("moe_hid_split", K, credit=RING)
        hid_used = signal("moe_hid_used", K, credit=RING)
        out_done = signal("moe_out_done", TT // 2, credit=2 * TT // 2)

        pieces = []
        for b, (wa, wb) in enumerate(((sw1, sw2), (w1[0], w2[0]), (w1[1], w2[1]))):
            for f in range(FB):
                pieces.append((wa.rearrange("(f p) h -> f p h", p=P)[f], w1_hi[:, b, f, :], w1_lo[:, b, f, :]))
            for c in range(KT * D // STAGE):
                n = STAGE // D
                src = wb.rearrange("(k p) d -> p k d", p=P)[:, c * n:(c + 1) * n, :]
                pieces.append((src, w2_hi[:, b, c * n:(c + 1) * n, :], w2_lo[:, b, c * n:(c + 1) * n, :]))
        PER_FFN = FB + KT * D // STAGE
        LATE = {2 * n: PER_FFN + n for n in range(2 * PER_FFN)}
        assert max(LATE) < 2 * KT and 2 * (FB - 1) < KT - LOOKAHEAD

        def staged(i, dst):
            v = stage[:, i % 2, :]
            return v if len(dst.shape) == 2 else v.rearrange("p (k d) -> p k d", d=D)

        block = ctx.enter_context(nc.Block())

        @block.sync
        def _(sp):
            def load_x(s, slot):
                wait_alone(sp, alone_sp, x_stored.sem, x_stored.at(s, -1))
                sp.dma_start(x[:, slot], tiles_of(x_in, s)).then_inc(x_loads.sems[slot], 16)

            give_credits(sp, [x_stored])
            load_x(0, 0)
            load_x(1, 1)
            sp.dma_start(ident[:, :], ident_dram).then_inc(consts_in, 16)
            for e, g in enumerate((gate_w[0:1, :], gate_w[1:2, :])):
                sp.dma_start(gates[:, e, :], g[0].partition_broadcast(P)).then_inc(consts_in, 16)
            for e, b in enumerate((sb2, b2[0], b2[1])):
                sp.dma_start(b2_all[:, e, :], b.partition_broadcast(P)).then_inc(consts_in, 16)
            sp.dma_start(b1_col[:, :, :], b1_cols.rearrange("p (b k) -> p b k", k=KT)).then_inc(consts_in, 16)
            for i, (src, dst, _) in enumerate(pieces):
                if i >= 2:
                    sp.wait_ge(stage_lo, i - 1)
                sp.dma_start(staged(i, dst), src).then_inc(stage_in[i % 2], 16)

            def step(s, slot, last):
                wait(sp, out_done, s, TT // 2)
                sp.dma_start(tiles_of(x_out, s), x[:, slot]).then_inc(x_stored.sem, 16)
                if not (isinstance(s, int) and s + 2 >= SEQS):
                    load_x(s + 2, slot)

            over_sequences(sp, step)
            wait(sp, x_stored, SEQS, 0)

        @block.gpsimd
        def _(pool):
            pool.memset(minus_half[:, :], -0.5).then_inc(half_set, 1)
            pool.wait_ge(half_set, 1)
            pool.wait_ge(consts_in, 16 * CONSTS)
            pool.tensor_tensor(b2_sum[:, :], b2_all[:, 0, :], b2_all[:, 1, :], ALU.add).then_inc(b2_part, 1)
            pool.wait_ge(b2_part, 1)
            pool.tensor_tensor(b2_sum[:, :], b2_sum[:, :], b2_all[:, 2, :], ALU.add).then_inc(b2_ready, 1)
            pool.wait_ge(b2_ready, 1)

            def norm(s, slot):
                wait_alone(pool, alone_pool, moments_done.sem, moments_done.at(s, TT))
                pool.tensor_scalar(var_eps[:, :], moments[:, :, 1], LN_EPS, None, ALU.add).then_inc(eps_added.sem, 1)
                wait(pool, eps_added, s, 1)
                pool.tensor_tensor(rstd[:, :], var_eps[:, :], minus_half[:, :], ALU.pow).then_inc(rstd_done.sem, 1)
                wait(pool, xn_done, s, TT)
                pool.tensor_tensor(x[:, slot], x[:, slot], b2_sum[:, :].unsqueeze(1).broadcast_to([P, TT, D]),
                                   ALU.add).then_inc(bias_added.sem, 1)

            norm(0, 0)

            def step(s, slot, last):
                if not last:
                    norm(s + 1, 1 - slot)

            over_sequences(pool, step)

        @block.scalar
        def _(act):
            def split(i):
                hi = pieces[i][1]
                act.wait_ge(stage_in[i % 2], 16 * (i // 2 + 1))
                act.activation(hi, staged(i, hi), ACT.Copy).then_inc(stage_hi, 1)

            for i in range(PER_FFN):
                split(i)
            act.wait_ge(consts_in, 16 * CONSTS)
            give_credits(act, [hid_act])

            def turn(s, slot, g):
                wait(act, turned, s, g + 1)
                act.activation(xT_hi[:, slot, g // FB, g % FB, :], ps_turn[:, :], ACT.Copy).then_inc(turn_hi.sem, 1)

            for g in range(GROUPS):
                turn(0, 0, g)

            def step(s, slot, first, last):
                for k in range(K):
                    wait(act, hid_summed, s, k + 1)
                    wait(act, hid_split, s, k + 1 - RING)
                    act.activation(hid[:, k % RING, :], ps_hid[:, k % RING, :], ACT.Relu,
                                   bias=b1_col[:, k // KT, k % KT:k % KT + 1])
                    wait(act, hid_used, s, k + 1 - RING)
                    act.activation(hid_hi[:, k % RING, :], ps_hid[:, k % RING, :], ACT.Relu,
                                   bias=b1_col[:, k // KT, k % KT:k % KT + 1]).then_inc(hid_act.sem, 1)
                    if k - LOOKAHEAD in TURN_AT and not last:
                        turn(s + 1, 1 - slot, TURN_AT.index(k - LOOKAHEAD))
                    if first and k in LATE:
                        split(LATE[k])

            over_steps(act, step)

        @block.vector
        def _(dve):
            def split(i):
                _, hi, lo = pieces[i]
                dve.wait_ge(stage_hi, i + 1)
                dve.tensor_tensor(lo, staged(i, lo), hi, ALU.subtract).then_inc(stage_lo, 1)

            dve.wait_ge(consts_in, 16 * CONSTS)
            give_credits(dve, [turn_lo, hid_split, out_done])

            def norm_stats(s, slot):
                x_loads.wait(dve, s, slot)
                for t in range(TT):
                    dve.bn_stats(stats[:, t, :], x[:, slot, t, :]).then_inc(stats_done.sem, 1)
                wait_alone(dve, alone, stats_done.sem, stats_done.at(s, TT))
                for t in range(TT):
                    dve.bn_aggr(moments[:, t, :], stats[:, t, :]).then_inc(moments_done.sem, 1)

            def norm_apply(s, slot):
                wait(dve, rstd_done, s, 1)
                for t in range(TT):
                    dve.tensor_scalar(xn[:, 0, t, :], x[:, slot, t, :], moments[:, t, 0:1], rstd[:, t:t + 1],
                                      ALU.subtract, ALU.mult).then_inc(xn_done.sem, 1)

            def scores(s, t):
                wait(dve, xn_done, s, TT)
                for e in range(2):
                    if 2 * t + e:
                        wait(dve, score_done, s, 2 * t + e)
                    dve.tensor_tensor_reduce(score_work[:, :], xn[:, 0, t, :], gates[:, e, :], 1.0, 0.0, ALU.mult,
                                             ALU.add, score[:, e, t:t + 1]).then_inc(score_done.sem, 1)

            def route(s):
                wait(dve, score_done, s, 2 * TT)
                dve.tensor_tensor(mask[:, 0, :], score[:, 0, :], score[:, 1, :], ALU.is_ge).then_inc(mask_done.sem, 1)
                dve.tensor_tensor(mask[:, 1, :], score[:, 0, :], score[:, 1, :], ALU.is_lt).then_inc(mask_done.sem, 1)

            def masked(s, e):
                wait(dve, mask_done, s, 2)
                for t in range(TT):
                    dve.tensor_scalar(xn[:, 1 + e, t, :], xn[:, 0, t, :], mask[:, e, t:t + 1], None,
                                      ALU.mult).then_inc(masked_done.sem, 1)

            def norm_part(s, slot, n):
                if n == 0:
                    norm_stats(s, slot)
                if n == 1:
                    norm_apply(s, slot)
                if 2 <= n < 2 + TT:
                    scores(s, n - 2)
                if n == 2 + TT:
                    route(s)
                if n in (3 + TT, 4 + TT):
                    masked(s, n - 3 - TT)

            def turn(s, slot, g):
                wait(dve, turn_hi, s, g + 1)
                dve.tensor_tensor(xT_lo[:, slot, g // FB, g % FB, :], ps_turn[:, :], xT_hi[:, slot, g // FB, g % FB, :],
                                  ALU.subtract).then_inc(turn_lo.sem, 1)

            for n in range(NORM_PARTS):
                norm_part(0, 0, n)
                if n % 2 == 1 and n // 2 < PER_FFN:
                    split(n // 2)
            for g in range(GROUPS):
                turn(0, 0, g)

            def step(s, slot, first, last):
                for k in range(K):
                    wait(dve, hid_act, s, k + 1)
                    dve.tensor_tensor(hid_lo[:, k % RING, :], hid[:, k % RING, :], hid_hi[:, k % RING, :],
                                      ALU.subtract).then_inc(hid_split.sem, 1)
                    if 0 <= k - NORM_AT < NORM_PARTS and not last:
                        norm_part(s + 1, 1 - slot, k - NORM_AT)
                    if k - LOOKAHEAD in TURN_AT and not last:
                        turn(s + 1, 1 - slot, TURN_AT.index(k - LOOKAHEAD))
                    if first and k in LATE:
                        split(LATE[k])
                wait(dve, hid_used, s, K)
                wait(dve, bias_added, s, 1)
                for half in range(TT // 2):
                    part = slice(2 * half, 2 * half + 2)
                    dve.tensor_tensor(x[:, slot, part, :], ps_out[:, slot, part, :], x[:, slot, part, :],
                                      ALU.add).then_inc(out_done.sem, 1)

            over_steps(dve, step)

        @block.tensor
        def _(pe):
            give_credits(pe, [hid_used])
            pe.wait_ge(consts_in, 16 * CONSTS)

            def turn(s, g):
                b, f = g // FB, g % FB
                if b:
                    wait(pe, masked_done, s, b * TT)
                else:
                    wait(pe, xn_done, s, TT)
                wait(pe, turn_lo, s, g)
                for t in range(TT):
                    last = pe.transpose(ps_turn[:, t * P:(t + 1) * P], xn[:, b, t, f * P:(f + 1) * P], ident[:, :])
                last.then_inc(turned.sem, 1)

            for g in range(GROUPS):
                turn(0, g)
            pe.wait_ge(stage_lo, PER_FFN)

            def first(s, slot, k):
                b, h = k // KT, slice(k % KT * P, (k % KT + 1) * P)
                wait(pe, hid_act, s, k + 1 - RING)
                for f in range(FB):
                    mm = split_product(pe, ps_hid[:, k % RING, :], w1_hi[:, b, f, h], w1_lo[:, b, f, h],
                                       xT_hi[:, slot, b, f, :], xT_lo[:, slot, b, f, :], f == 0, f == FB - 1)
                mm.then_inc(hid_summed.sem, 1)

            def second(s, slot, k):
                wait(pe, hid_split, s, k + 1)
                if k == 0:
                    wait(pe, out_done, s, -TT // 2)
                for t in range(TT):
                    tok = slice(t * P, (t + 1) * P)
                    mm = split_product(pe, ps_out[:, slot, t, :], hid_hi[:, k % RING, tok], hid_lo[:, k % RING, tok],
                                       w2_hi[:, k // KT, k % KT, :], w2_lo[:, k // KT, k % KT, :],
                                       k == 0 and t % 2 == 0, k == K - 1, shared_bank=True)
                mm.then_inc(hid_used.sem, 1)

            def step(s, slot, first_one, last):
                for k in range(LOOKAHEAD):
                    if k == 0:
                        wait(pe, turn_lo, s, GROUPS)
                    first(s, slot, k)
                for k in range(K):
                    if first_one and k + LOOKAHEAD in (KT, 2 * KT):
                        pe.wait_ge(stage_lo, (k + LOOKAHEAD) // KT * PER_FFN + FB)
                    if k + LOOKAHEAD < K:
                        first(s, slot, k + LOOKAHEAD)
                    if first_one and k in (KT, 2 * KT):
                        pe.wait_ge(stage_lo, (k // KT + 1) * PER_FFN)
                    second(s, slot, k)
                    if k in TURN_AT and not last:
                        turn(s + 1, TURN_AT.index(k))

            over_steps(pe, step)


def tower_kernel(nc, a, out):

    def stream(name):
        return nc.dram_tensor(name, (SEQS * SEQ, D), F32).ap()

    h0, attended, h1, h2, h3 = (stream(n) for n in ("h0", "attended", "h1", "h2", "h3"))
    with nc.cleanup_on_exit():
        attention_phase(nc, a["ident"], a["select"], a["mask"], a["rope_cos"], a["rope_sin"], a["tokens"], a["emb"],
                        a["ln1"], a["q_ut"], a["q_v"], a["q_b"], a["k_ut"], a["k_v"], a["k_b"], a["v_ut"], a["v_v"],
                        a["v_b"], a["out_ut"], a["out_v"], a["out_b"], h0, attended)
    with nc.cleanup_on_exit():
        mlp_phase(nc, a["ident"], attended, h0, a["ln2"], a["fc1_u"], a["fc1_v"], a["fc1_b"], a["fc2_u"], a["fc2_v"],
                  a["fc2_b"], h1)
    with nc.cleanup_on_exit():
        ffn_phase(nc, a["ident"], h1, a["w_up_t"], a["w_down_t"], h2)
    with nc.cleanup_on_exit():
        mamba_phase(nc, a["ident"], a["triangles"], h2, a["in_proj_t"], a["conv_w"], a["conv_b"], a["a_log"],
                    a["dt_w_t"], a["dt_b"], a["b_w_t"], a["c_w_t"], a["d_skip"], a["ln_y"], a["out_proj_t"], h3)
    with nc.cleanup_on_exit():
        moe_phase(nc, a["ident"], h3, a["gate_w"], a["w1"], a["b1"], a["w2"], a["b2"], a["sw1"], a["sw2"], a["sb2"], out)


def kernel(**inputs):
    import numpy as np
    import concourse.bacc as bacc
    from concourse.bass_utils import run_bass_kernel_spmd

    def given(name):
        return np.ascontiguousarray(inputs[name])

    def turned(name):
        return np.ascontiguousarray(given(name).T)

    def columns(v):
        return np.ascontiguousarray(v.reshape(-1, P).T)

    def side_by_side(*vs):
        return np.ascontiguousarray(np.concatenate([columns(v) for v in vs], axis=1))

    def ranks_first(name):
        return np.ascontiguousarray(given(name).transpose(1, 2, 0))

    i, j = np.mgrid[0:P, 0:P]
    later = np.where(i > j, np.float32(-1e5), np.float32(0))
    triangles = np.stack([(i <= j).astype(np.float32), (i > j).astype(np.float32), np.ones((P, P), np.float32), later])
    inverse = np.float32(1) / (10000.0 ** (np.arange(0, D, 2) / D)).astype(np.float32)
    angle = (np.arange(SEQ, dtype=np.float32)[:, None] * inverse[None, :]).astype(np.float64)
    hd = given("L0_attn_q_V").shape[2]
    pairs = P // hd // 2
    select = np.zeros((4, pairs, P, P), np.float32)
    for half, places in enumerate(((0, 1), (2,), (0, 2), (1,))):
        for pair in range(pairs):
            for r in range(2):
                for n in range(hd):
                    for place in places:
                        select[half, pair, (2 * pair + r) * hd + n, 64 * r + place * hd + n] = 1.0

    conv = given("L1_attn_conv_w")
    taps = conv.shape[-1]
    b1 = given("L1_ffn_b1")
    arrays = {
        "ident": np.eye(P, dtype=np.float32),
        "select": select,
        "mask": np.where(j > i, np.float32(-1e30), np.float32(0)),
        "triangles": triangles,
        "rope_cos": np.cos(angle).astype(np.float32),
        "rope_sin": np.sin(angle).astype(np.float32),
        "tokens": np.ascontiguousarray(given("x").reshape(SEQS * TT, P).T),
        "emb": given("L0_tok_emb_weight"),
        "ln1": side_by_side(given("L0_attn_ln1_g"), given("L0_attn_ln1_b")),
        "ln2": side_by_side(given("L0_attn_ln2_g"), given("L0_attn_ln2_b")),
        "out_ut": turned("L0_attn_out_U"), "out_v": given("L0_attn_out_V"), "out_b": given("L0_attn_out_b"),
        "v_b": given("L0_attn_v_b").reshape(-1),
        "fc1_u": given("L0_attn_fc1_U"), "fc1_v": given("L0_attn_fc1_V"), "fc1_b": columns(given("L0_attn_fc1_b")),
        "fc2_u": given("L0_attn_fc2_U"), "fc2_v": given("L0_attn_fc2_V"), "fc2_b": given("L0_attn_fc2_b"),
        "w_up_t": turned("L0_ffn_w_up"), "w_down_t": turned("L0_ffn_w_down"),
        "in_proj_t": turned("L1_attn_in_proj_w"),
        "conv_w": np.ascontiguousarray(conv.reshape(-1, P, taps).transpose(1, 0, 2)).reshape(P, -1),
        "conv_b": columns(given("L1_attn_conv_b")), "a_log": given("L1_attn_A_log"),
        "dt_w_t": turned("L1_attn_dt_w"), "dt_b": given("L1_attn_dt_b"),
        "b_w_t": turned("L1_attn_B_w"), "c_w_t": turned("L1_attn_C_w"), "d_skip": given("L1_attn_D"),
        "ln_y": side_by_side(given("L1_attn_ln_w"), given("L1_attn_ln_b")),
        "out_proj_t": turned("L1_attn_out_proj_w"),
        "gate_w": given("L1_ffn_gate_w"), "w1": given("L1_ffn_w1"), "w2": given("L1_ffn_w2"), "b2": given("L1_ffn_b2"),
        "b1": side_by_side(given("L1_ffn_sb1"), b1[0], b1[1]),
        "sw1": given("L1_ffn_sw1"), "sw2": given("L1_ffn_sw2"), "sb2": given("L1_ffn_sb2"),
    }
    for n in "qkv":
        arrays[f"{n}_ut"] = ranks_first(f"L0_attn_{n}_U")
        arrays[f"{n}_v"] = given(f"L0_attn_{n}_V")
    for n in "qk":
        arrays[f"{n}_b"] = columns(given(f"L0_attn_{n}_b"))

    nc = bacc.Bacc("TRN2", target_bir_lowering=False, num_devices=1)
    aps = {name: nc.dram_tensor("in_" + name, a.shape, mybir.dt.from_np(a.dtype), kind="ExternalInput").ap()
           for name, a in arrays.items()}
    out = nc.dram_tensor("out", (SEQS * SEQ, D), F32, kind="ExternalOutput").ap()
    tower_kernel(nc, aps, out)
    result = run_bass_kernel_spmd(nc, [{"in_" + name: a for name, a in arrays.items()}], core_ids=[0])
    return result.results[0]["out"].reshape(SEQS, SEQ, D)
```
